# Optimizing a Trainium2 kernel written in Bass

```python
import numpy as np
import jax
import jax.numpy as jnp

def _softmax(x, axis=-1):
    return jax.nn.softmax(x, axis=axis)
def _gelu(x):
    return jax.nn.gelu(x, approximate=True)
def _silu(x):
    return jax.nn.silu(x)
def _sigmoid(x):
    return jax.nn.sigmoid(x)
def _layernorm(x, axis=-1, eps=1e-5):
    m = jnp.mean(x, axis=axis, keepdims=True)
    v = jnp.var(x, axis=axis, keepdims=True)
    return (x - m) / jnp.sqrt(v + eps)
def _scatter_add(tgt, idx, src, axis=0):
    return tgt.at[idx].add(src)
def _segment_sum(src, seg, n):
    return jax.ops.segment_sum(src, seg, n)

kernel_name = 'mk_metaformer_d1_conv_nhwc256_d28c69'

def setup_inputs(seed: int = 0):
    np.random.seed(seed)
    _w = jnp.asarray
    def _rec_inputs():
        import jax
        import jax.numpy as jnp
        _gk = jax.random.key(seed)
        x = -0.0005207 + 1.001 * jax.random.normal(jax.random.fold_in(_gk, 1), (8, 32, 32, 256), jnp.float32)
        return x
    x = _rec_inputs()
    def _L0_conv_setup():
        import jax, jax.numpy as jnp
        import numpy as np
        B, N1, N2, E = (8, 32, 32, 256)
        H = 8
        KD = E // H
        HD = E // H
        L = N1 * N2
        SCALING = KD ** (-0.5)
        LN_EPS = 1e-05

        def _rel_pos_2d():
            half = 1.0 / 10000.0 ** jnp.linspace(0.0, 1.0, KD // 2)
            angle = jnp.repeat(half, 2)
            decay = jnp.log(1.0 - 2.0 ** (-2.0 - 5.0 * jnp.arange(H, dtype=jnp.float32) / H))
            i1 = jnp.arange(N1, dtype=jnp.float32)
            i2 = jnp.arange(N2, dtype=jnp.float32)
            index_k = (i1[:, None] + i2[None, :]).reshape(L)
            sin_k = jnp.sin(index_k[:, None] * angle[None, :])
            cos_k = jnp.cos(index_k[:, None] * angle[None, :])
            sin_q = sin_k[None, None]
            cos_q = cos_k[None, None]
            d = (jnp.abs(i1[:, None, None, None] - i1[None, None, :, None]) + jnp.abs(i2[None, :, None, None] - i2[None, None, None, :])).reshape(L, L)
            mask = jnp.exp(d[None, :, :] * decay[:, None, None])
            mask = jnp.nan_to_num(mask)
            mask = mask / jnp.sqrt(mask.sum(-1, keepdims=True))
            return (sin_q, cos_q, sin_k, cos_k, mask)

        def rotate_every_two(x):
            x1 = x[..., ::2]
            x2 = x[..., 1::2]
            return jnp.stack((-x2, x1), axis=-1).reshape(x.shape)

        def theta_shift(x, sin, cos):
            return x * cos + rotate_every_two(x) * sin
        key = jax.random.key(seed)
        ks = jax.random.split(key, 5)
        gain_qkv = 2.0 ** (-2.5) * (6.0 / (E + E)) ** 0.5
        gain_o = 2.0 ** (-1) * (6.0 / (E + E)) ** 0.5
        x = jax.random.normal(ks[0], (B, N1, N2, E), dtype=jnp.float32)
        Wq = jax.random.uniform(ks[1], (E, E), jnp.float32, -gain_qkv, gain_qkv)
        Wk = jax.random.uniform(ks[2], (E, E), jnp.float32, -gain_qkv, gain_qkv)
        Wv = jax.random.uniform(ks[3], (E, E), jnp.float32, -gain_qkv, gain_qkv)
        Wo = jax.random.uniform(ks[4], (E, E), jnp.float32, -gain_o, gain_o)
        ln_g = jnp.ones((HD,), jnp.float32)
        ln_b = jnp.zeros((HD,), jnp.float32)
        return {'x': x, 'Wq': Wq, 'Wk': Wk, 'Wv': Wv, 'Wo': Wo, 'ln_g': ln_g, 'ln_b': ln_b}
    _L0_conv_all = _L0_conv_setup()
    _L0_conv_in = {k: v for k, v in _L0_conv_all.items() if k in ('Wq', 'Wk', 'Wv', 'Wo', 'ln_g', 'ln_b', )}
    del _L0_conv_all

    def _L0_ffn_setup():
        import jax, jax.numpy as jnp
        import numpy as np
        B, T, D, H, E = (16, 4096, 256, 512, 8)
        key = jax.random.key(seed)
        ks = jax.random.split(key, 5)
        x = jax.random.normal(ks[0], (B, T, D), dtype=jnp.float32)
        gate_w = jax.random.normal(ks[1], (D, E), dtype=jnp.float32) * 0.02
        gate_b = jnp.zeros((E,), dtype=jnp.float32)
        W1 = jax.random.normal(ks[2], (E, D, H), dtype=jnp.float32) * 0.02
        b1 = jnp.zeros((E, H), dtype=jnp.float32)
        W2 = jax.random.normal(ks[3], (E, H, D), dtype=jnp.float32) * 0.02
        b2 = jnp.zeros((E, D), dtype=jnp.float32)
        return {'x': x, 'gate_w': gate_w, 'gate_b': gate_b, 'W1': W1, 'b1': b1, 'W2': W2, 'b2': b2}
    _L0_ffn_all = _L0_ffn_setup()
    _L0_ffn_in = {k: v for k, v in _L0_ffn_all.items() if k in ('gate_w', 'gate_b', 'W1', 'b1', 'W2', 'b2', )}
    del _L0_ffn_all

    return {
        "x": x,
        "L0_conv_Wq": _L0_conv_in["Wq"],
        "L0_conv_Wk": _L0_conv_in["Wk"],
        "L0_conv_Wv": _L0_conv_in["Wv"],
        "L0_conv_Wo": _L0_conv_in["Wo"],
        "L0_conv_ln_g": _L0_conv_in["ln_g"],
        "L0_conv_ln_b": _L0_conv_in["ln_b"],
        "L0_ffn_gate_w": _L0_ffn_in["gate_w"],
        "L0_ffn_gate_b": _L0_ffn_in["gate_b"],
        "L0_ffn_W1": _L0_ffn_in["W1"],
        "L0_ffn_b1": _L0_ffn_in["b1"],
        "L0_ffn_W2": _L0_ffn_in["W2"],
        "L0_ffn_b2": _L0_ffn_in["b2"],
    }

def reference(x, L0_conv_Wq, L0_conv_Wk, L0_conv_Wv, L0_conv_Wo, L0_conv_ln_g, L0_conv_ln_b, L0_ffn_gate_w, L0_ffn_gate_b, L0_ffn_W1, L0_ffn_b1, L0_ffn_W2, L0_ffn_b2):
    import jax
    import jax.numpy as jnp
    def _L0_conv_ref(x, Wq, Wk, Wv, Wo, ln_g, ln_b):
        import jax, jax.numpy as jnp
        import numpy as np
        B, N1, N2, E = (8, 32, 32, 256)
        H = 8
        KD = E // H
        HD = E // H
        L = N1 * N2
        SCALING = KD ** (-0.5)
        LN_EPS = 1e-05

        def _rel_pos_2d():
            half = 1.0 / 10000.0 ** jnp.linspace(0.0, 1.0, KD // 2)
            angle = jnp.repeat(half, 2)
            decay = jnp.log(1.0 - 2.0 ** (-2.0 - 5.0 * jnp.arange(H, dtype=jnp.float32) / H))
            i1 = jnp.arange(N1, dtype=jnp.float32)
            i2 = jnp.arange(N2, dtype=jnp.float32)
            index_k = (i1[:, None] + i2[None, :]).reshape(L)
            sin_k = jnp.sin(index_k[:, None] * angle[None, :])
            cos_k = jnp.cos(index_k[:, None] * angle[None, :])
            sin_q = sin_k[None, None]
            cos_q = cos_k[None, None]
            d = (jnp.abs(i1[:, None, None, None] - i1[None, None, :, None]) + jnp.abs(i2[None, :, None, None] - i2[None, None, None, :])).reshape(L, L)
            mask = jnp.exp(d[None, :, :] * decay[:, None, None])
            mask = jnp.nan_to_num(mask)
            mask = mask / jnp.sqrt(mask.sum(-1, keepdims=True))
            return (sin_q, cos_q, sin_k, cos_k, mask)

        def rotate_every_two(x):
            x1 = x[..., ::2]
            x2 = x[..., 1::2]
            return jnp.stack((-x2, x1), axis=-1).reshape(x.shape)

        def theta_shift(x, sin, cos):
            return x * cos + rotate_every_two(x) * sin
        sin_q, cos_q, sin_k, cos_k, mask = _rel_pos_2d()
        xf = x.reshape(B, L, E)
        q = (xf @ Wq.T).reshape(B, L, H, KD).transpose(0, 2, 1, 3)
        k = (xf @ Wk.T * SCALING).reshape(B, L, H, KD).transpose(0, 2, 1, 3)
        vr = (xf @ Wv.T).reshape(B, L, H, HD).transpose(0, 2, 1, 3)
        qr = theta_shift(q, sin_q, cos_q)
        kr = theta_shift(k, sin_k[None, None], cos_k[None, None])
        qk = jnp.einsum('bhqd,bhkd->bhqk', qr, kr) * mask[None]
        den = jnp.clip(jax.lax.stop_gradient(jnp.abs(qk)).sum(-1, keepdims=True), 1.0, 50000.0)
        qk = qk / den
        out = jnp.einsum('bhqk,bhkd->bhqd', qk, vr).transpose(0, 2, 1, 3)
        mu = out.mean(-1, keepdims=True)
        var = out.var(-1, keepdims=True)
        out = (out - mu) / jnp.sqrt(var + LN_EPS) * ln_g + ln_b
        out = jax.nn.gelu(out.reshape(B, L, H * HD), approximate=False)
        out = out @ Wo.T
        return out.reshape(B, N1, N2, E)

    def _L0_ffn_ref(x, gate_w, gate_b, W1, b1, W2, b2):
        import jax, jax.numpy as jnp
        import numpy as np
        B, T, D, H, E = (16, 4096, 256, 512, 8)
        Bb, Tt, Dd = x.shape
        Ee = gate_w.shape[1]
        xf = x.reshape(-1, Dd)
        N = xf.shape[0]
        logits = xf @ gate_w + gate_b
        probs = jax.nn.softmax(logits, axis=-1)
        top2_vals, top2_idx = jax.lax.top_k(probs, 2)
        cw = jnp.zeros((N, Ee), dtype=xf.dtype).at[jnp.arange(N)[:, None], top2_idx].add(top2_vals)

        def step(acc, params):
            w1, bb1, w2, bb2, we = params
            h = jax.nn.gelu(xf @ w1 + bb1, approximate=False)
            y = h @ w2 + bb2
            return (acc + we[:, None] * y, None)
        out, _ = jax.lax.scan(step, jnp.zeros_like(xf), (W1, b1, W2, b2, cw.T))
        return out.reshape(Bb, Tt, Dd)

    def _gn(v, G=32, eps=1e-5):
        B_, H_, W_, C_ = v.shape
        g = v.reshape(B_, H_, W_, G, C_ // G)
        m = jnp.mean(g, axis=(1, 2, 4), keepdims=True)
        s = jnp.var(g, axis=(1, 2, 4), keepdims=True)
        return ((g - m) / jnp.sqrt(s + eps)).reshape(v.shape)

    def _ln_c(v, eps=1e-6):
        m = jnp.mean(v, axis=-1, keepdims=True)
        s = jnp.var(v, axis=-1, keepdims=True)
        return (v - m) / jnp.sqrt(s + eps)

    def _ln_t(v, eps=1e-5):
        m = jnp.mean(v, axis=-1, keepdims=True)
        s = jnp.var(v, axis=-1, keepdims=True)
        return (v - m) / jnp.sqrt(s + eps)

    def _to_tokens(v):
        B_, H_, W_, C_ = v.shape
        return v.reshape(B_, H_ * W_, C_)
    def _from_tokens(t, like):
        return t.reshape(like.shape)

    x = x + _L0_conv_ref(_ln_c(x), L0_conv_Wq, L0_conv_Wk, L0_conv_Wv, L0_conv_Wo, L0_conv_ln_g, L0_conv_ln_b)
    t = _to_tokens(x)
    t = t + _L0_ffn_ref(_ln_t(t), L0_ffn_gate_w, L0_ffn_gate_b, L0_ffn_W1, L0_ffn_b1, L0_ffn_W2, L0_ffn_b2)
    x = _from_tokens(t, x)
    return x


_drawn_inputs = setup_inputs


def setup_inputs(seed=0):
    import zlib

    import numpy as np

    out = dict(_drawn_inputs(seed))
    spreads = {'L0_conv_ln_g': (1.0, 0.2),
     'L0_conv_ln_b': (0.0, 0.1),
     'L0_ffn_gate_b': (0.0, 0.454),
     'L0_ffn_b1': (0.0, 0.8),
     'L0_ffn_b2': (0.0, 0.328)}
    factors = {'L0_ffn_W1': 2.998, 'L0_ffn_W2': 2.809}
    for name, (base, spread) in spreads.items():
        noise = np.random.default_rng([zlib.crc32(name.encode()), seed]).standard_normal(out[name].shape)
        drawn = base * np.exp(spread * noise) if base else spread * noise
        out[name] = jnp.asarray(drawn.astype(out[name].dtype))
    for name, factor in factors.items():
        out[name] = (out[name] * factor).astype(out[name].dtype)
    return out
```

```python
from contextlib import ExitStack

import numpy as np

import concourse.bass as bass
from concourse import mybir
from concourse.alu_op_type import AluOpType as ALU

F32 = mybir.dt.float32
F32R = mybir.dt.float32r
ACT = mybir.ActivationFunctionType
AX = mybir.AxisListType

B, N1, N2, C = 8, 32, 32, 256
L = N1 * N2
H, D = 8, C // 8
T = B * L
P = 128
HALF = 512
CC = C // P
HG = P // D
TT = HALF // P
ROWS = P // N2
KT = L // P
SPAN = N1 + (KT - 1) * ROWS
EXPERTS, HID = 8, 512


def after(engine, semaphore, value):
    if not (isinstance(value, int) and value <= 0):
        engine.wait_ge(semaphore, value)


def over_batches(engine, body):
    body(0, True, False)
    with engine.Fori(1, B - 1) as b:
        body(b, False, False)
    body(B - 1, False, True)


class Names:

    def __init__(self, nc, ctx, phase):
        self.nc, self.ctx, self.phase = nc, ctx, phase

    def sbuf(self, name, shape, dtype=F32):
        return self.ctx.enter_context(self.nc.sbuf_tensor(f"{self.phase}_{name}", shape, dtype))

    def psum(self, name, shape):
        return self.ctx.enter_context(self.nc.psum_tensor(f"{self.phase}_{name}", shape, F32))

    def sem(self, name):
        return self.ctx.enter_context(self.nc.semaphore(f"{self.phase}_{name}"))


def project(nc, x, wq, wk, wv, cos, sin, ident, q_hi, q_lo, k_hi, k_lo, v_out):
    with ExitStack() as ctx:
        a = Names(nc, ctx, "proj")
        wf = a.sbuf("w_float", [P, 3, CC, C])
        w_hi = a.sbuf("w_hi", [P, 3, CC, C], F32R)
        w_lo = a.sbuf("w_lo", [P, 3, CC, C], F32R)
        ws_hi = a.sbuf("w_swap_hi", [P, 2, CC, C], F32R)
        ws_lo = a.sbuf("w_swap_lo", [P, 2, CC, C], F32R)
        cos_t = a.sbuf("cos", [P, L])
        sin_t = a.sbuf("sin", [P, L])
        idt = a.sbuf("ident", [P, P])
        power = a.sbuf("power", [P, TT])
        eps = a.sbuf("eps", [P, TT])
        x_in = a.sbuf("x_in", [P, 2, TT, C])
        stats = a.sbuf("stats", [P, TT, 6])
        mean_var = a.sbuf("mean_var", [P, TT, 2])
        rstd_in = a.sbuf("rstd_in", [P, TT])
        rstd = a.sbuf("rstd", [P, TT])
        xn = a.sbuf("xn", [P, TT, C])
        x_hi = a.sbuf("x_hi", [P, 2, CC, HALF], F32R)
        x_lo = a.sbuf("x_lo", [P, 2, CC, HALF], F32R)
        by_cos = a.sbuf("by_cos", [P, 2, HALF])
        by_sin = a.sbuf("by_sin", [P, 2, HALF])
        turned = a.sbuf("turned", [P, 2, HALF])
        t_hi = a.sbuf("turned_hi", [P, 2, HALF], F32R)
        t_lo = a.sbuf("turned_lo", [P, 2, HALF], F32R)
        v_sb = a.sbuf("v", [P, 2, TT, C])
        pt = a.psum("x_turned", [P, CC, HALF])
        pa = a.psum("plain", [P, 2, HALF])
        pb = a.psum("swapped", [P, 2, HALF])
        pv = a.psum("v_acc", [P, CC, HALF])

        consts = a.sem("consts_loaded")
        power_set = a.sem("power_set")
        passed = a.sem("waits_passed")
        w_hi_ready, w_ready = a.sem("w_hi_ready"), a.sem("w_ready")
        x_loaded = [a.sem(f"x_loaded{i}") for i in range(2)]
        stats_done, moments_done = a.sem("stats_done"), a.sem("moments_done")
        eps_added, rstd_ready = a.sem("eps_added"), a.sem("rstd_ready")
        xn_ready, xt_ready = a.sem("xn_ready"), a.sem("xt_ready")
        x_hi_ready, x_lo_ready = a.sem("x_hi_ready"), a.sem("x_lo_ready")
        products = a.sem("products_ready")
        cos_done, sin_done = a.sem("cos_done"), a.sem("sin_done")
        turned_ready = a.sem("turned_ready")
        hi_ready, lo_ready = a.sem("hi_ready"), a.sem("lo_ready")
        stored = [a.sem(f"parts_stored{i}") for i in range(2)]
        v_acc_ready, v_ready = a.sem("v_acc_ready"), a.sem("v_ready")
        v_stored = [a.sem(f"v_stored{i}") for i in range(2)]

        xv = x.rearrange("(n t p) c -> n p t c", p=P, t=TT)
        vv = v_out.rearrange("(n t p) c -> n p t c", p=P, t=TT)
        parts = [(hi.rearrange("b (c p) l -> b c p l", p=P), lo.rearrange("b (c p) l -> b c p l", p=P))
                 for hi, lo in ((q_hi, q_lo), (k_hi, k_lo))]
        PIECES = 2 * CC

        def one(i, n):
            return i if isinstance(i, int) else bass.ds(i, n)

        def block_of(ap, j):
            return ap[j] if isinstance(j, int) else ap[bass.ds(j, 1)].rearrange("o p t c -> (o p) t c")

        block = ctx.enter_context(nc.Block())

        @block.sync
        def _(sp):
            for n, w in enumerate((wq, wk, wv)):
                sp.dma_start(wf[:, n], w.rearrange("(k p) c -> p k c", p=P)).then_inc(consts, 16)
            for dst, src in ((cos_t, cos), (sin_t, sin), (idt, ident)):
                sp.dma_start(dst[:], src).then_inc(consts, 16)
            sp.dma_start(x_in[:, 0], block_of(xv, 0)).then_inc(x_loaded[0], 16)

            def body(b, first, last):
                for h in range(2):
                    j = 2 * b + h
                    if not (last and h == 1):
                        after(sp, xn_ready, j)
                        sp.dma_start(x_in[:, 1 - h], block_of(xv, j + 1)).then_inc(x_loaded[1 - h], 16)
                    for m in range(PIECES):
                        n = PIECES * j + m
                        for part, src, ready in ((0, t_hi, hi_ready), (1, t_lo, lo_ready)):
                            sp.wait_ge(ready, n + 1)
                            dst = parts[m // CC][part]
                            dst = dst[b, m % CC] if isinstance(b, int) else \
                                dst[bass.ds(b, 1), m % CC].rearrange("o p l -> (o p) l")
                            sp.dma_start(dst[:, h * HALF:(h + 1) * HALF], src[:, m % 2].bitcast(F32))\
                                .then_inc(stored[m % 2], 16)
                    sp.wait_ge(v_ready, 2 * (j + 1))
                    sp.dma_start(block_of(vv, j), v_sb[:, h]).then_inc(v_stored[h], 16)

            over_batches(sp, body)
            for i in range(2):
                sp.wait_ge(stored[i], 2 * B * PIECES // 2 * 32)
                sp.wait_ge(v_stored[i], B * 16)

        @block.gpsimd
        def _(pool):
            nc.gpsimd.memset(power[:], -0.5).then_inc(power_set, 1)
            nc.gpsimd.memset(eps[:], 1e-6).then_inc(power_set, 1)
            pool.wait_ge(power_set, 2)

            def scale_of(j):
                pool.wait_ge(moments_done, j + 1)
                after(pool, xn_ready, j)
                nc.gpsimd.tensor_tensor(rstd_in[:], mean_var[:, :, 1], eps[:], ALU.add)\
                    .then_inc(eps_added, 1)
                pool.wait_ge(eps_added, j + 1)
                nc.gpsimd.tensor_tensor(rstd[:], rstd_in[:], power[:], ALU.pow).then_inc(rstd_ready, 1)

            scale_of(0)

            def body(b, first, last):
                for h in range(2):
                    j = 2 * b + h
                    for m in range(PIECES):
                        n, i = PIECES * j + m, m % 2
                        pool.wait_ge(sin_done, n + 1)
                        after(pool, lo_ready, n - 1)
                        nc.gpsimd.tensor_tensor(turned[:, i], by_cos[:, i], by_sin[:, i], ALU.add)\
                            .then_inc(turned_ready, 1)
                        pool.wait_ge(hi_ready, n + 1)
                        if not (first and h == 0 and m < 2):
                            pool.wait_ge(stored[i], 32 * ((PIECES // 2) * j + m // 2))
                        nc.gpsimd.tensor_tensor(t_lo[:, i], turned[:, i], t_hi[:, i].bitcast(F32), ALU.subtract)\
                            .then_inc(lo_ready, 1)
                        if m == 0 and not (last and h == 1):
                            scale_of(j + 1)

            over_batches(pool, body)

        @block.vector
        def _(dve):
            dve.wait_ge(consts, 6 * 16)
            nc.vector.tensor_copy(w_hi[:], wf[:]).then_inc(w_hi_ready, 1)
            pairs = lambda t: t.rearrange("p n k (c two) -> p n k c two", two=2)
            dve.wait_ge(w_hi_ready, 1)
            nc.vector.tensor_tensor(w_lo[:], wf[:], w_hi[:].bitcast(F32), ALU.subtract).then_inc(w_ready, 1)
            dve.wait_ge(w_ready, 1)
            count = 1
            for n in range(2):
                for dst, src in ((ws_hi, w_hi), (ws_lo, w_lo)):
                    for two in range(2):
                        nc.vector.tensor_copy(pairs(dst[:])[:, n, :, :, two],
                                              pairs(src[:].bitcast(F32))[:, n, :, :, 1 - two]).then_inc(w_ready, 1)

            def moments(j, h):
                dve.wait_ge(x_loaded[h], 16 * (j // 2 + 1) if isinstance(j, int) else 8 * j + (16 if h == 0 else 8))
                after(dve, moments_done, j)
                for t in range(TT):
                    last = nc.vector.bn_stats(stats[:, t], x_in[:, h, t])
                last.then_inc(stats_done, 1)
                dve.wait_ge(stats_done, j + 1)
                after(dve, xn_ready, j)
                after(dve, rstd_ready, j)
                dve.sem_inc(passed, 1)
                for t in range(TT):
                    last = nc.vector.bn_aggr(mean_var[:, t], stats[:, t])
                last.then_inc(moments_done, 1)

            def norm(j, h):
                dve.wait_ge(rstd_ready, j + 1)
                after(dve, xt_ready, 2 * j)
                for t in range(TT):
                    last = nc.vector.tensor_scalar(xn[:, t], x_in[:, h, t], mean_var[:, t, 0:1], rstd[:, t:t + 1],
                                                   ALU.subtract, ALU.mult)
                last.then_inc(xn_ready, 1)

            def low_part(j, h):
                for c in range(CC):
                    dve.wait_ge(x_hi_ready, CC * j + c + 1)
                    nc.vector.tensor_tensor(x_lo[:, h, c], pt[:, c], x_hi[:, h, c].bitcast(F32), ALU.subtract)\
                        .then_inc(x_lo_ready, 1)

            moments(0, 0)
            norm(0, 0)
            low_part(0, 0)

            def body(b, first, last):
                for h in range(2):
                    j = 2 * b + h
                    ahead = not (last and h == 1)
                    for m in range(PIECES):
                        n, i = PIECES * j + m, m % 2
                        dve.wait_ge(products, n + 1)
                        after(dve, turned_ready, n - 1)
                        at = slice(h * HALF, (h + 1) * HALF)
                        nc.vector.tensor_tensor(by_cos[:, i], pa[:, i], cos_t[:, at], ALU.mult).then_inc(cos_done, 1)
                        nc.vector.tensor_tensor(by_sin[:, i], pb[:, i], sin_t[:, at], ALU.mult).then_inc(sin_done, 1)
                        if ahead:
                            if m == 0:
                                moments(j + 1, 1 - h)
                            if m == 1:
                                norm(j + 1, 1 - h)
                            if m == 2:
                                low_part(j + 1, 1 - h)

            over_batches(dve, body)

        @block.scalar
        def _(act):
            def high_part(j, h):
                for c in range(CC):
                    act.wait_ge(xt_ready, CC * j + c + 1)
                    nc.scalar.activation(x_hi[:, h, c], pt[:, c], ACT.Copy).then_inc(x_hi_ready, 1)

            high_part(0, 0)

            def body(b, first, last):
                for h in range(2):
                    j = 2 * b + h
                    for m in range(PIECES):
                        n, i = PIECES * j + m, m % 2
                        act.wait_ge(turned_ready, n + 1)
                        if not (first and h == 0 and m < 2):
                            act.wait_ge(stored[i], 32 * ((PIECES // 2) * j + m // 2))
                        nc.scalar.activation(t_hi[:, i], turned[:, i], ACT.Copy).then_inc(hi_ready, 1)
                        if m == 2 and not (last and h == 1):
                            high_part(j + 1, 1 - h)
                    if not first:
                        act.wait_ge(v_stored[h], 16 * b)
                    for c in range(CC):
                        act.wait_ge(v_acc_ready, CC * j + c + 1)
                        nc.scalar.activation(v_sb[:, h, 2 * c:2 * c + 2, :],
                                             pv[:, c].rearrange("p (t c) -> p t c", t=2), ACT.Copy)\
                            .then_inc(v_ready, 1)

            over_batches(act, body)

        @block.tensor
        def _(pe):
            def turn(j, h):
                pe.wait_ge(xn_ready, j + 1)
                after(pe, x_lo_ready, CC * j)
                for c in range(CC):
                    for t in range(TT):
                        last = nc.tensor.transpose(pt[:, c, t * P:(t + 1) * P], xn[:, t, c * P:(c + 1) * P], idt[:])
                    last.then_inc(xt_ready, 1)

            def three(out, pairs):
                for n, (l, r) in enumerate(pairs):
                    last = nc.tensor.matmul(out, l, r, start=n == 0, stop=n == len(pairs) - 1)
                return last

            pe.wait_ge(consts, 6 * 16)
            turn(0, 0)
            pe.wait_ge(w_ready, 9)

            def body(b, first, last):
                for h in range(2):
                    j = 2 * b + h
                    pe.wait_ge(x_lo_ready, CC * (j + 1))
                    for m in range(PIECES):
                        n, i = PIECES * j + m, m % 2
                        kind, c = m // CC, m % CC
                        cols = slice(c * P, (c + 1) * P)
                        after(pe, sin_done, n - 1)
                        for out, hi, lo in ((pa[:, i], w_hi, w_lo), (pb[:, i], ws_hi, ws_lo)):
                            done = three(out, [(w[:, kind, k, cols], y[:, h, k])
                                               for k in range(CC) for w, y in ((hi, x_hi), (hi, x_lo), (lo, x_hi))])
                        done.then_inc(products, 1)
                        if m == 1 and not (last and h == 1):
                            turn(j + 1, 1 - h)
                    for t in range(TT):
                        c = t // 2
                        if t % 2 == 0:
                            after(pe, v_ready, CC * (j - 1) + c + 1) if not (first and h == 0) else None
                        rows = slice(t * P, (t + 1) * P)
                        done = three(pv[:, c, (t % 2) * C:(t % 2 + 1) * C],
                                     [(y[:, h, k, rows], w[:, 2, k])
                                      for k in range(CC) for w, y in ((w_hi, x_hi), (w_hi, x_lo), (w_lo, x_hi))])
                        if t % 2:
                            done.then_inc(v_acc_ready, 1)

            over_batches(pe, body)


def retain(nc, x, wo, ln_g, ln_b, decay, factor, ident, q_hi, q_lo, k_hi, k_lo, v_in, x1):
    HALVES, GROUPS, PAIRS = L // HALF, H // HG, HG // 2
    UNITS = GROUPS * HALVES
    STEPS = KT * PAIRS
    P_RING, A_RING = 4, 2
    with ExitStack() as ctx:
        a = Names(nc, ctx, "ret")
        decay_t = a.sbuf("decay", [P, H, SPAN * N2])
        factor_t = a.sbuf("factor", [P, KT, H])
        idt = a.sbuf("ident", [P, P])
        wo_t = a.sbuf("wo", [P, CC, C])
        gb = a.sbuf("gain_bias", [P, 2])
        ones = a.sbuf("ones", [P, D])
        power = a.sbuf("power", [P, TT * HG])
        eps = a.sbuf("eps", [P, TT * HG])
        k_st = a.sbuf("k_parts", [P, GROUPS, HG, L], F32R)
        q_st = a.sbuf("q_parts", [P, HALVES, HG, HALF], F32R)
        v_t = a.sbuf("v", [P, GROUPS, KT, P])
        decayed = a.sbuf("decayed", [P, P_RING, 2, HALF])
        magnitude = a.sbuf("magnitude", [P, A_RING, 2, HALF])
        o_sb = a.sbuf("o", [P, HALF])
        m_sb = a.sbuf("row_sums", [P, HALF])
        total = a.sbuf("total", [P, TT, HG])
        clipped = a.sbuf("clipped", [P, TT, HG])
        recip = a.sbuf("recip", [P, TT, HG])
        scale = a.sbuf("scale", [P, TT, HG])
        o_sum = a.sbuf("o_sum", [P, TT * HG])
        centred = a.sbuf("centred", [P, TT * HG, D])
        squared = a.sbuf("squared", [P, TT * HG, D])
        var_sum = a.sbuf("var_sum", [P, TT * HG])
        scale_sq = a.sbuf("scale_sq", [P, TT * HG])
        var_scaled = a.sbuf("var_scaled", [P, TT * HG])
        var_eps = a.sbuf("var_eps", [P, TT * HG])
        rstd = a.sbuf("rstd", [P, TT * HG])
        gain = a.sbuf("gain", [P, TT * HG])
        normed = a.sbuf("normed", [P, TT * HG, D])
        gelu_t = a.sbuf("gelu", [P, GROUPS, HALVES, HALF])
        x_res = a.sbuf("x_residual", [P, HALVES, TT, C])
        x_out = a.sbuf("x_out", [P, HALVES, TT, C])
        ps = a.psum("scores", [P, 2, 2, HALF])
        po = a.psum("o_acc", [P, HALF])
        pm = a.psum("row_sum_acc", [P, HALF])
        px = a.psum("turn_a", [P, HALF])
        py = a.psum("turn_b", [P, HALF])

        consts, set_up = a.sem("consts_loaded"), a.sem("set_up")
        k_loaded = [a.sem(f"k_loaded{i}") for i in range(GROUPS)]
        q_loaded = [a.sem(f"q_loaded{i}") for i in range(HALVES)]
        x_loaded = [a.sem(f"x_loaded{i}") for i in range(HALVES)]
        x_stored = [a.sem(f"x_stored{i}") for i in range(HALVES)]
        scores, decayed_s, magnitude_s = a.sem("scores_ready"), a.sem("decayed_ready"), a.sem("magnitude_ready")
        values, row_sums = a.sem("values_added"), a.sem("row_sums_added")
        o_out, m_out = a.sem("o_copied"), a.sem("row_sums_copied")
        o_turned, m_turned = a.sem("o_turned"), a.sem("row_sums_turned")
        total_s, clip_s, recip_s, scale_s = (a.sem(n) for n in ("total", "clipped", "recip", "scale"))
        o_sum_s, centred_s, squared_s, var_s = (a.sem(n) for n in ("o_sum", "centred", "squared", "var_sum"))
        pool_chain = a.sem("pool_chain")
        rstd_s, normed_s = a.sem("rstd_ready"), a.sem("normed_ready")
        back_s, gelu_s = a.sem("normed_turned"), a.sem("gelu_ready")
        out_s, x_out_s = a.sem("projected"), a.sem("x_out_ready")

        xv = x.rearrange("(b h t p) c -> b h p t c", p=P, t=TT, h=HALVES)
        x1v = x1.rearrange("(b h t p) c -> b h p t c", p=P, t=TT, h=HALVES)
        vv = v_in.rearrange("(b k p) c -> b p k c", p=P, k=KT)
        split = lambda y: y.rearrange("b (g h d) l -> b g d h l", d=D, h=HG)

        def of_batch(ap, b, rest, names):
            if isinstance(b, int):
                return ap[(b, *rest)]
            inner = names.split()
            return ap[(bass.ds(b, 1), *rest)].rearrange(f"o {names} -> (o {inner[0]}) {' '.join(inner[1:])}")

        def batches(engine, body):
            over_batches(engine, body)

        block = ctx.enter_context(nc.Block())

        @block.sync
        def _(sp):
            rows = lambda n: slice(n * D, (n + 1) * D)

            def load_kv(b, g):
                for n, y in enumerate((k_hi, k_hi, k_lo, k_lo)):
                    sp.dma_start(k_st[rows(n), g].bitcast(F32), of_batch(split(y), b, (g,), "d h l"))\
                        .then_inc(k_loaded[g], 16)
                sp.dma_start(v_t[:, g], of_batch(vv, b, (slice(None), slice(None), slice(g * P, (g + 1) * P)), "p k c"))\
                    .then_inc(k_loaded[g], 16)

            def load_q(b, g, h):
                for n, y in enumerate((q_hi, q_lo, q_hi, q_lo)):
                    src = of_batch(split(y), b, (g, slice(None), slice(None), slice(h * HALF, (h + 1) * HALF)), "d h l")
                    sp.dma_start(q_st[rows(n), h].bitcast(F32), src).then_inc(q_loaded[h], 16)

            def load_x(b, h):
                sp.dma_start(x_res[:, h], of_batch(xv, b, (h,), "p t c")).then_inc(x_loaded[h], 16)

            load_kv(0, 0)
            load_q(0, 0, 0)
            sp.dma_start(decay_t[:, 0:HG], decay[:, 0:HG]).then_inc(consts, 16)
            sp.dma_start(decay_t[:, HG:H], decay[:, HG:H]).then_inc(consts, 16)
            for dst, src in ((factor_t, factor), (idt, ident)):
                sp.dma_start(dst[:], src).then_inc(consts, 16)
            sp.dma_start(wo_t[:], wo.rearrange("(k p) c -> p k c", p=P)).then_inc(consts, 16)
            for n, y in enumerate((ln_g, ln_b)):
                for h in range(HG):
                    sp.dma_start(gb[h * D:(h + 1) * D, n:n + 1], y.rearrange("(d o) -> d o", o=1)).then_inc(consts, 16)
            load_q(0, 0, 1)
            load_kv(0, 1)
            load_x(0, 0)
            load_x(0, 1)

            def store(b, h):
                sp.wait_ge(x_out_s, 2 * (2 * b + h + 1))
                sp.dma_start(of_batch(x1v, b, (h,), "p t c"), x_out[:, h]).then_inc(x_stored[h], 16)

            def body(b, first, last):
                for k in range(UNITS):
                    g, h, u = k // HALVES, k % HALVES, UNITS * b + k
                    if k < HALVES and not first:
                        store(b - 1, k)
                        load_x(b, k)
                    sp.wait_ge(scores, STEPS * (u + 1))
                    if g == 0:
                        load_q(b, 1, h)
                    elif not last:
                        load_q(b + 1, 0, h)
                    if h == HALVES - 1 and not last:
                        sp.wait_ge(values, STEPS * (u + 1))
                        load_kv(b + 1, g)

            batches(sp, body)
            for h in range(HALVES):
                store(B - 1, h)
            for h in range(HALVES):
                sp.wait_ge(x_stored[h], 16 * B)

        @block.gpsimd
        def _(pool):
            nc.gpsimd.memset(power[:], -0.5).then_inc(set_up, 1)
            nc.gpsimd.memset(ones[:], 1.0).then_inc(set_up, 1)
            nc.gpsimd.memset(eps[:], 1e-5).then_inc(set_up, 1)
            pool.wait_ge(set_up, 3)

            def norm(u):
                wide = lambda y: y[:].unsqueeze(2).broadcast_to([P, TT * HG, D])
                pool.wait_ge(scale_s, u + 1)
                flat = scale[:].rearrange("p t h -> p (t h)")
                nc.gpsimd.tensor_tensor(scale_sq[:], flat, flat, ALU.mult).then_inc(pool_chain, 1)
                pool.wait_ge(var_s, u + 1)
                pool.wait_ge(pool_chain, 4 * u + 1)
                nc.gpsimd.tensor_tensor(var_scaled[:], var_sum[:], scale_sq[:], ALU.mult).then_inc(pool_chain, 1)
                pool.wait_ge(pool_chain, 4 * u + 2)
                nc.gpsimd.tensor_tensor(var_eps[:], var_scaled[:], eps[:], ALU.add).then_inc(pool_chain, 1)
                pool.wait_ge(pool_chain, 4 * u + 3)
                nc.gpsimd.tensor_tensor(rstd[:], var_eps[:], power[:], ALU.pow).then_inc(rstd_s, 1)
                pool.wait_ge(rstd_s, u + 1)
                nc.gpsimd.tensor_tensor(gain[:], rstd[:], flat, ALU.mult).then_inc(pool_chain, 1)
                pool.wait_ge(pool_chain, 4 * u + 4)
                after(pool, back_s, u)
                nc.gpsimd.tensor_tensor(normed[:], centred[:], wide(gain), ALU.mult).then_inc(normed_s, 1)

            def body(b, first, last):
                for k in range(UNITS):
                    norm(UNITS * b + k)

            batches(pool, body)

        @block.vector
        def _(dve):
            dve.wait_ge(consts, 16 * (5 + 2 * HG))

            def decay_step(u, k, i, first):
                g, h, kt, pair = k // HALVES, k % HALVES, i // PAIRS, i % PAIRS
                n = STEPS * u + i
                dve.wait_ge(scores, n + 1)
                if not (first and k == 0 and i < P_RING):
                    dve.wait_ge(values, n - P_RING + 1)
                    dve.wait_ge(magnitude_s, n - P_RING + 1)
                at = (h * HALF // N2 - ROWS * kt + SPAN - N1) * N2
                nc.vector.tensor_tensor(decayed[:, i % P_RING], ps[:, i % 2],
                                        decay_t[:, HG * g + 2 * pair:HG * g + 2 * pair + 2, at:at + HALF],
                                        ALU.mult).then_inc(decayed_s, 1)

            def rest(u, k, i):
                g, h = k // HALVES, k % HALVES
                if i == 0:
                    dve.wait_ge(values, STEPS * (u + 1))
                    after(dve, o_turned, u)
                    nc.vector.tensor_copy(o_sb[:], po[:]).then_inc(o_out, 1)
                if i == 4:
                    dve.wait_ge(o_turned, u + 1)
                    nc.vector.tensor_reduce(o_sum[:], px[:].rearrange("p (n d) -> p n d", d=D), AX.X, ALU.add)\
                        .then_inc(o_sum_s, 1)
                if i == 5:
                    dve.wait_ge(m_turned, u + 1)
                    fac = factor_t[:, TT * h:TT * h + TT, HG * g:HG * g + HG]
                    nc.vector.tensor_tensor(total[:], py[:].rearrange("p (t h d) -> p t h d", t=TT, d=D)[:, :, :, 0],
                                            fac, ALU.mult).then_inc(total_s, 1)
                    dve.wait_ge(total_s, u + 1)
                    nc.vector.tensor_scalar(clipped[:], total[:], 1.0, 50000.0, ALU.max, ALU.min).then_inc(clip_s, 1)
                    dve.wait_ge(clip_s, u + 1)
                    nc.vector.reciprocal(recip[:], clipped[:]).then_inc(recip_s, 1)
                    dve.wait_ge(recip_s, u + 1)
                    after(dve, normed_s, u)
                    nc.vector.tensor_tensor(scale[:], recip[:], fac, ALU.mult).then_inc(scale_s, 1)
                if i == 6:
                    dve.wait_ge(o_sum_s, u + 1)
                    nc.vector.scalar_tensor_tensor(out=centred[:], in0=o_sum[:].unsqueeze(2).broadcast_to([P, TT * HG, D]),
                                                   scalar=-1.0 / D, in1=px[:].rearrange("p (n d) -> p n d", d=D),
                                                   op0=ALU.mult, op1=ALU.add).then_inc(centred_s, 1)
                if i == 8:
                    dve.wait_ge(squared_s, u + 1)
                    nc.vector.tensor_reduce(var_sum[:], squared[:], AX.X, ALU.add).then_inc(var_s, 1)

            def add_residual(b, h, n, first):
                m = 2 * (2 * b + h) + n
                dve.wait_ge(out_s, m + 1)
                if n == 0:
                    dve.wait_ge(x_loaded[h], 16 * (b + 1))
                    after(dve, x_stored[h], 16 * b)
                bank = (py, px)[n]
                nc.vector.tensor_tensor(x_out[:, h, 2 * n:2 * n + 2], bank[:].rearrange("p (t c) -> p t c", t=2),
                                        x_res[:, h, 2 * n:2 * n + 2], ALU.add).then_inc(x_out_s, 1)

            def body(b, first, last):
                for k in range(UNITS):
                    u = UNITS * b + k
                    for i in range(STEPS):
                        decay_step(u, k, i, first)
                        if k > 0:
                            rest(u - 1, k - 1, i)
                        elif not first:
                            rest(u - 1, UNITS - 1, i)
                        if i == STEPS - 1 and k == UNITS - 1:
                            add_residual(b, 0, 0, first)
                        if i == STEPS - 1 and k == 0 and not first:
                            add_residual(b - 1, 1, 0, first)
                        if i == 1 and k == 0 and not first:
                            add_residual(b - 1, 0, 1, first)
                        if i == 1 and k == 1 and not first:
                            add_residual(b - 1, 1, 1, first)

            batches(dve, body)
            for i in range(STEPS):
                rest(UNITS * B - 1, UNITS - 1, i)
                if i == 1:
                    add_residual(B - 1, 0, 1, False)
            add_residual(B - 1, 1, 0, False)
            add_residual(B - 1, 1, 1, False)

        @block.scalar
        def _(act):
            act.wait_ge(consts, 16 * (5 + 2 * HG))

            def rest(u, k, i):
                g, h = k // HALVES, k % HALVES
                if i == 0:
                    act.wait_ge(row_sums, STEPS * (u + 1))
                    after(act, m_turned, u)
                    nc.scalar.activation(m_sb[:], pm[:], ACT.Copy).then_inc(m_out, 1)
                if i == 7:
                    act.wait_ge(centred_s, u + 1)
                    after(act, var_s, u)
                    nc.scalar.activation(squared[:], centred[:], ACT.Square, scale=D ** -0.5).then_inc(squared_s, 1)
                if i == 13:
                    act.wait_ge(back_s, u + 1)
                    nc.scalar.activation(gelu_t[:, g, h], px[:], ACT.Gelu, bias=gb[:, 1:2], scale=gb[:, 0:1])\
                        .then_inc(gelu_s, 1)

            def body(b, first, last):
                for k in range(UNITS):
                    u = UNITS * b + k
                    for i in range(STEPS):
                        n = STEPS * u + i
                        act.wait_ge(decayed_s, n + 1)
                        if not (first and k == 0 and i < A_RING):
                            act.wait_ge(row_sums, n - A_RING + 1)
                        nc.scalar.activation(magnitude[:, i % A_RING], decayed[:, i % P_RING], ACT.Abs)\
                            .then_inc(magnitude_s, 1)
                        if k > 0:
                            rest(u - 1, k - 1, i)
                        elif not first:
                            rest(u - 1, UNITS - 1, i)

            batches(act, body)
            for i in range(STEPS):
                rest(UNITS * B - 1, UNITS - 1, i)

        @block.tensor
        def _(pe):
            pe.wait_ge(set_up, 3)
            pe.wait_ge(consts, 16 * (5 + 2 * HG))

            def score(b, k, i, first):
                g, h, kt, pair = k // HALVES, k % HALVES, i // PAIRS, i % PAIRS
                u = UNITS * b + k
                if i == 0:
                    pe.wait_ge(q_loaded[h], 64 * (2 * b + g + 1))
                    if h == 0:
                        pe.wait_ge(k_loaded[g], 80 * (b + 1))
                if not (first and k == 0 and i < 2):
                    pe.wait_ge(decayed_s, STEPS * u + i - 1)
                for j in range(2):
                    head = 2 * pair + j
                    last = nc.tensor.matmul(ps[:, i % 2, j], k_st[:, g, head, kt * P:(kt + 1) * P],
                                            q_st[:, h, head], start=True, stop=True)
                last.then_inc(scores, 1)

            def value(u, k, i, first):
                g, kt, pair = k // HALVES, i // PAIRS, i % PAIRS
                pe.wait_ge(decayed_s, STEPS * u + i + 1)
                if i == 0:
                    after(pe, o_out, u)
                for j in range(2):
                    head = 2 * pair + j
                    last = nc.tensor.matmul(po[head * D:(head + 1) * D, :], v_t[:, g, kt, head * D:(head + 1) * D],
                                            decayed[:, i % P_RING, j], start=kt == 0, stop=kt == KT - 1)
                last.then_inc(values, 1)

            def row_sum(u, i):
                kt, pair = i // PAIRS, i % PAIRS
                pe.wait_ge(magnitude_s, STEPS * u + i + 1)
                if i == 0:
                    after(pe, m_out, u)
                for j in range(2):
                    head = 2 * pair + j
                    last = nc.tensor.matmul(pm[head * D:(head + 1) * D, :], ones[:],
                                            magnitude[:, i % A_RING, j], start=kt == 0, stop=kt == KT - 1)
                last.then_inc(row_sums, 1)

            def turn(out, src):
                for t in range(TT):
                    last = nc.tensor.transpose(out[:, t * P:(t + 1) * P], src(t), idt[:])
                return last

            def rest(b, k, i):
                u = UNITS * b + k
                g, h = k // HALVES, k % HALVES
                if i == 2:
                    pe.wait_ge(o_out, u + 1)
                    after(pe, gelu_s, u)
                    after(pe, x_out_s, 4 * b + 2 * (k == UNITS - 1))
                    turn(px, lambda t: o_sb[:, t * P:(t + 1) * P]).then_inc(o_turned, 1)
                if i == 3:
                    pe.wait_ge(m_out, u + 1)
                    after(pe, scale_s, u)
                    turn(py, lambda t: m_sb[:, t * P:(t + 1) * P]).then_inc(m_turned, 1)
                if i == 12:
                    pe.wait_ge(normed_s, u + 1)
                    turn(px, lambda t: normed[:, t * HG:(t + 1) * HG].rearrange("p h d -> p (h d)"))\
                        .then_inc(back_s, 1)
                if i in (14, 15) and g == GROUPS - 1:
                    if i == 14:
                        pe.wait_ge(scale_s, u + 1)
                        pe.wait_ge(gelu_s, u + 1)
                    bank = (py, px)[i - 14]
                    for t in (2 * (i - 14), 2 * (i - 14) + 1):
                        for c in range(CC):
                            last = nc.tensor.matmul(bank[:, (t % 2) * C:(t % 2 + 1) * C],
                                                    gelu_t[:, c, h, t * P:(t + 1) * P], wo_t[:, c],
                                                    start=c == 0, stop=c == CC - 1)
                    last.then_inc(out_s, 1)

            score(0, 0, 0, True)
            score(0, 0, 1, True)

            def body(b, first, last_batch):
                for k in range(UNITS):
                    u = UNITS * b + k
                    for i in range(STEPS):
                        value(u, k, i, first)
                        if i + 2 < STEPS:
                            score(b, k, i + 2, first)
                        elif k + 1 < UNITS:
                            score(b, k + 1, i + 2 - STEPS, False)
                        elif not last_batch:
                            score(b + 1, 0, i + 2 - STEPS, False)
                        if i > 0:
                            row_sum(u, i - 1)
                        elif not (first and k == 0):
                            row_sum(u - 1, STEPS - 1)
                        if k > 0:
                            rest(b, k - 1, i)
                        elif not first:
                            rest(b - 1, UNITS - 1, i)

            batches(pe, body)
            row_sum(UNITS * B - 1, STEPS - 1)
            for i in range(STEPS):
                rest(B - 1, UNITS - 1, i)


SLOTS = 2 * T
TILES = SLOTS // P + EXPERTS
TOKEN_TILES = T // P
HK = HID // P


def route(nc, x1, gate_w, gate_b, w1, w2, upper, ident, w1_hi, w1_lo, w2_hi, w2_lo,
          slots, weights, tile_expert, xn_out, slot_rows):
    JS = T // HALF
    PIECES = 2 * EXPERTS
    ZERO = 1024
    assert PIECES == JS
    with ExitStack() as ctx:
        a = Names(nc, ctx, "route")
        x_in = a.sbuf("x_in", [P, 2, TT, C])
        stats = a.sbuf("stats", [P, TT, 6])
        mean_var = a.sbuf("mean_var", [P, TT, 2])
        rstd_in = a.sbuf("rstd_in", [P, TT])
        rstd = a.sbuf("rstd", [P, TT])
        power = a.sbuf("power", [P, TT])
        xn = a.sbuf("xn", [P, 2, TT, C])
        xt = a.sbuf("xt", [P, 2, CC, HALF])
        stage = a.sbuf("w_stage", [P, 2, CC * HID])
        idt = a.sbuf("ident", [P, P])
        up = a.sbuf("upper", [P, P])
        ones = a.sbuf("ones", [P, P])
        gate = a.sbuf("gate", [P, CC, EXPERTS])
        bias = a.sbuf("gate_bias", [P, EXPERTS])
        number = a.sbuf("expert_number", [P, EXPERTS])
        tile_no = a.sbuf("tile_number", [P, TILES])
        zero = a.sbuf("zero", [P, ZERO])
        wide = [P, TOKEN_TILES, EXPERTS]
        logits = a.sbuf("logits", wide)
        top = a.sbuf("top", [P, TOKEN_TILES])
        shifted = a.sbuf("shifted", wide)
        expd = a.sbuf("exp", wide)
        denom = a.sbuf("denom", [P, TOKEN_TILES])
        recip = a.sbuf("recip", [P, TOKEN_TILES])
        probs = a.sbuf("probs", wide)
        equal = a.sbuf("equal", wide)
        ranked = a.sbuf("ranked", wide)
        least = a.sbuf("least", [P, TOKEN_TILES])
        chosen = [a.sbuf(f"chosen{i}", wide) for i in range(2)]
        left = a.sbuf("left", wide)
        both = a.sbuf("both", wide)
        total = a.sbuf("total", wide)
        scans = [a.sbuf(f"scan{i}", wide) for i in range(2)]
        small = [a.sbuf(f"small{i}", [P, EXPERTS]) for i in range(6)]
        whole = a.sbuf("whole", [P, EXPERTS], mybir.dt.int32)
        shift = a.sbuf("shift", [P, EXPERTS], mybir.dt.int32)
        slot_f = equal
        picked = ranked
        slot_sum = a.sbuf("slot_sum", [P, TOKEN_TILES])
        index = a.sbuf("index", [P, 4, 2], mybir.dt.uint32)
        past = a.sbuf("past", [P, TILES, EXPERTS])
        past_sum = a.sbuf("past_sum", [P, TILES])
        past_cap = a.sbuf("past_cap", [P, TILES])
        xs = x_in[:, 0]
        pt = a.psum("x_turned", [P, 2, CC, HALF])
        pl = a.psum("logit_acc", [P, 2, HALF])
        pr = a.psum("rank", [P, HALF])
        pc = a.psum("counts", [P, HALF])

        consts, set_up, zeroed = a.sem("consts_loaded"), a.sem("set_up"), a.sem("slots_zeroed")
        x_loaded = [a.sem(f"x_loaded{i}") for i in range(2)]
        w_loaded = [a.sem(f"w_loaded{i}") for i in range(2)]
        stats_done, moments_done, eps_added, rstd_ready = (
            a.sem(n) for n in ("stats_done", "moments_done", "eps_added", "rstd_ready"))
        xn_ready, xt_acc, xt_ready = a.sem("xn_ready"), a.sem("xt_turned"), a.sem("xt_ready")
        xn_stored = [a.sem(f"xn_stored{i}") for i in range(2)]
        logit_acc, logit_ready = a.sem("logit_acc"), a.sem("logit_ready")
        w_hi_s, w_lo_s = a.sem("w_hi_ready"), a.sem("w_lo_ready")
        chain, exp_s, counted, shift_set = a.sem("chain"), a.sem("exp_ready"), a.sem("counted"), a.sem("shift_set")
        index_s = a.sem("index_ready")
        passed = a.sem("waits_passed")
        both_s, slots_s = a.sem("both_ready"), a.sem("slots_ready")
        xs_loaded = [a.sem(f"xs_loaded{i}") for i in range(4)]
        xs_sent = [a.sem(f"xs_sent{i}") for i in range(4)]

        xv = x1.rearrange("(n t p) c -> n p t c", p=P, t=TT)
        xnv = xn_out.rearrange("(n t p) c -> n p t c", p=P, t=TT)
        xn_tiles = xn_out.rearrange("(n p) c -> n p c", p=P)
        w1v = w1.rearrange("e (k p) n -> e p k n", p=P)
        w2v = w2.rearrange("e (k p) n -> e p k n", p=P)
        CONSTS = 5
        block = ctx.enter_context(nc.Block())

        @block.sync
        def _(sp):
            sp.dma_start(x_in[:, 0], xv[0]).then_inc(x_loaded[0], 16)
            sp.dma_start(x_in[:, 1], xv[1]).then_inc(x_loaded[1], 16)
            sp.dma_start(idt[:], ident).then_inc(consts, 16)
            sp.dma_start(up[:], upper).then_inc(consts, 16)
            sp.dma_start(gate[:], gate_w.rearrange("(k p) e -> p k e", p=P)).then_inc(consts, 16)
            sp.dma_start(bias[:], gate_b.partition_broadcast(P)).then_inc(consts, 16)
            for n in range(2):
                sp.dma_start(stage[:, n], (w1v, w2v)[n][0].rearrange("p k n -> p k n")).then_inc(w_loaded[n], 16)
            sp.wait_ge(set_up, 5)
            flat = slot_rows.rearrange("(p n) c -> p (n c)", p=P)
            for n in range(0, TILES * C, ZERO):
                sp.dma_start(flat[:, n:n + ZERO], zero[:, 0:min(ZERO, TILES * C - n)]).then_inc(zeroed, 16)
            for j in range(JS):
                h = j % 2
                sp.wait_ge(xn_ready, j + 1)
                sp.dma_start(xnv[j], xn[:, h]).then_inc(xn_stored[h], 16)
                if j + 2 < JS:
                    sp.dma_start(x_in[:, h], xv[j + 2]).then_inc(x_loaded[h], 16)
                    sp.wait_ge(w_lo_s, j + 1)
                    sp.dma_start(stage[:, h].rearrange("p (k n) -> p k n", k=(CC, HK)[h]),
                                 (w1v, w2v)[h][j // 2 + 1]).then_inc(w_loaded[h], 16)
            for h in range(2):
                sp.wait_ge(xn_stored[h], 16 * JS // 2)
            for t in range(4):
                sp.dma_start(xs[:, t], xn_tiles[t]).then_inc(xs_loaded[t], 16)
            with sp.Fori(0, TOKEN_TILES // 4 - 1) as r:
                for t in range(4):
                    sp.wait_ge(xs_sent[t], 32 * r + 32)
                    sp.dma_start(xs[:, t], xn_tiles[bass.ds(4 * r + 4 + t, 1)].rearrange("o p c -> (o p) c"))\
                        .then_inc(xs_loaded[t], 16)

        @block.gpsimd
        def _(pool):
            nc.gpsimd.memset(power[:], -0.5).then_inc(set_up, 1)
            nc.gpsimd.memset(ones[:], 1.0).then_inc(set_up, 1)
            nc.gpsimd.memset(zero[:], 0.0).then_inc(set_up, 1)
            nc.gpsimd.iota(number[:], [[1, EXPERTS]], base=-EXPERTS, channel_multiplier=0,
                           allow_small_or_imprecise_dtypes=True).then_inc(set_up, 1)
            nc.gpsimd.iota(tile_no[:], [[1, TILES]], base=0, channel_multiplier=0,
                           allow_small_or_imprecise_dtypes=True).then_inc(set_up, 1)
            pool.wait_ge(set_up, 5)
            for j in range(JS):
                h = j % 2
                pool.wait_ge(moments_done, j + 1)
                nc.gpsimd.tensor_scalar(rstd_in[:], mean_var[:, :, 1], 1.0, 1e-5, ALU.mult, ALU.add)\
                    .then_inc(eps_added, 1)
                pool.wait_ge(eps_added, j + 1)
                nc.gpsimd.tensor_tensor(rstd[:], rstd_in[:], power[:], ALU.pow).then_inc(rstd_ready, 1)
                hi, lo, k = ((w1_hi, w1_lo, CC), (w2_hi, w2_lo, HK))[h]
                pool.wait_ge(w_hi_s, j + 1)
                nc.gpsimd.tensor_tensor(lo[:, j // 2], stage[:, h].rearrange("p (k n) -> p k n", k=k),
                                        hi[:, j // 2].bitcast(F32), ALU.subtract).then_inc(w_lo_s, 1)
            pool.wait_ge(slots_s, 2)
            pool.wait_ge(zeroed, 16 * (-(-TILES * C // ZERO)))
            with pool.Fori(0, TOKEN_TILES // 4) as r:
                for t in range(4):
                    pool.wait_ge(xs_loaded[t], 16 * r + 16)
                    nc.gpsimd.tensor_copy(index[:, t], slots[:, :, bass.ds(4 * r + t, 1)].rearrange("p n o -> p (n o)"))\
                        .then_inc(index_s, 1)
                    pool.wait_ge(index_s, 4 * r + t + 1)
                    pool.sem_inc(passed, 1)
                    for n in range(2):
                        nc.gpsimd.indirect_dma_start(slot_rows, bass.IndirectOffsetOnAxis(index[:, t, n:n + 1], 0),
                                                     xs[:, t], None).then_inc(xs_sent[t], 16)
            for t in range(4):
                pool.wait_ge(xs_sent[t], 32 * TOKEN_TILES // 4)

        @block.scalar
        def _(act):
            for j in range(JS):
                h = j % 2
                hi, k = ((w1_hi, CC), (w2_hi, HK))[h]
                act.wait_ge(w_loaded[h], 16 * (j // 2 + 1))
                nc.scalar.activation(hi[:, j // 2], stage[:, h].rearrange("p (k n) -> p k n", k=k), ACT.Copy)\
                    .then_inc(w_hi_s, 1)
                act.wait_ge(xt_acc, j + 1)
                after(act, logit_acc, j - 1)
                nc.scalar.activation(xt[:, h], pt[:, h], ACT.Copy).then_inc(xt_ready, 1)
            act.wait_ge(chain, 2)
            nc.scalar.activation(expd[:], shifted[:], ACT.Exp).then_inc(exp_s, 1)

        @block.tensor
        def _(pe):
            pe.wait_ge(consts, 64)
            def logit(j):
                h = j % 2
                pe.wait_ge(xt_ready, j + 1)
                after(pe, logit_ready, j - 1)
                for t in range(TT):
                    for c in range(CC):
                        last = nc.tensor.matmul(pl[:, h, t * EXPERTS:(t + 1) * EXPERTS], xt[:, h, c, t * P:(t + 1) * P], gate[:, c],
                                                start=c == 0, stop=c == CC - 1)
                last.then_inc(logit_acc, 1)

            for j in range(JS):
                h = j % 2
                pe.wait_ge(xn_ready, j + 1)
                after(pe, xt_ready, j - 1)
                for c in range(CC):
                    for t in range(TT):
                        last = nc.tensor.transpose(pt[:, h, c, t * P:(t + 1) * P], xn[:, h, t, c * P:(c + 1) * P], idt[:])
                last.then_inc(xt_acc, 1)
                if j:
                    logit(j - 1)
            logit(JS - 1)
            pe.wait_ge(both_s, 1)
            pe.wait_ge(set_up, 5)
            flat = both[:].rearrange("p t e -> p (t e)")
            nc.tensor.matmul(pr[:], up[:], flat, start=True, stop=True)
            nc.tensor.matmul(pc[:], ones[:], flat, start=True, stop=True).then_inc(counted, 1)

        @block.vector
        def _(dve):
            def stage1(j):
                h = j % 2
                dve.wait_ge(x_loaded[h], 16 * (j // 2 + 1))
                after(dve, moments_done, j)
                for t in range(TT):
                    last = nc.vector.bn_stats(stats[:, t], x_in[:, h, t])
                last.then_inc(stats_done, 1)
                dve.wait_ge(stats_done, j + 1)
                after(dve, xn_ready, j)
                for t in range(TT):
                    last = nc.vector.bn_aggr(mean_var[:, t], stats[:, t])
                last.then_inc(moments_done, 1)

            def stage2(j):
                h = j % 2
                dve.wait_ge(rstd_ready, j + 1)
                if j >= 2:
                    dve.wait_ge(xt_acc, j - 1)
                    dve.wait_ge(xn_stored[h], 16 * (j // 2))
                for t in range(TT):
                    last = nc.vector.tensor_scalar(xn[:, h, t], x_in[:, h, t], mean_var[:, t, 0:1], rstd[:, t:t + 1],
                                                   ALU.subtract, ALU.mult)
                last.then_inc(xn_ready, 1)

            def stage3(j):
                h = j % 2
                dve.wait_ge(logit_acc, j + 1)
                nc.vector.tensor_tensor(logits[:, j * TT:(j + 1) * TT],
                                        pl[:, h, 0:TT * EXPERTS].rearrange("p (t e) -> p t e", t=TT),
                                        bias[:].unsqueeze(1).broadcast_to([P, TT, EXPERTS]), ALU.add)\
                    .then_inc(logit_ready, 1)

            dve.wait_ge(consts, 64)
            dve.wait_ge(set_up, 5)
            for j in range(JS):
                stage1(j)
                stage2(j)
                if j >= 2:
                    stage3(j - 2)
            stage3(JS - 2)
            stage3(JS - 1)
            dve.wait_ge(logit_ready, JS)

            count = [0]

            def link(ins):
                count[0] += 1
                ins.then_inc(chain, 1)
                dve.wait_ge(chain, count[0])

            spread = lambda y: y[:].unsqueeze(2).broadcast_to(wide)
            over = lambda y: y[:].unsqueeze(1).broadcast_to(wide)
            V = nc.vector
            link(V.tensor_reduce(top[:], logits[:], AX.X, ALU.max))
            link(V.tensor_tensor(shifted[:], logits[:], spread(top), ALU.subtract))
            dve.wait_ge(exp_s, 1)
            link(V.tensor_reduce(denom[:], expd[:], AX.X, ALU.add))
            link(V.reciprocal(recip[:], denom[:]))
            link(V.tensor_tensor(probs[:], expd[:], spread(recip), ALU.mult))
            rest = probs
            for n in range(2):
                link(V.tensor_reduce(weights[:, n], rest[:], AX.X, ALU.max))
                link(V.tensor_tensor(equal[:], rest[:], weights[:, n].unsqueeze(2).broadcast_to(wide), ALU.is_equal))
                link(V.tensor_tensor(ranked[:], equal[:], over(number), ALU.mult))
                link(V.tensor_reduce(least[:], ranked[:], AX.X, ALU.min))
                link(V.tensor_tensor(chosen[n][:], over(number), spread(least), ALU.is_equal))
                if n == 0:
                    link(V.scalar_tensor_tensor(out=left[:], in0=chosen[0][:], scalar=-4.0, in1=probs[:],
                                                op0=ALU.mult, op1=ALU.add))
                    rest = left
            V.tensor_tensor(both[:], chosen[0][:], chosen[1][:], ALU.add).then_inc(both_s, 1)
            dve.wait_ge(counted, 1)
            flat = lambda y: y[:].rearrange("p t e -> p (t e)")
            link(V.tensor_copy(flat(total), pc[:]))
            link(V.tensor_copy(flat(scans[0]), pc[:]))
            at, step = 0, 1
            while step < TOKEN_TILES:
                src, dst = scans[at], scans[1 - at]
                link(V.tensor_copy(dst[:, 0:step], src[:, 0:step]))
                link(V.tensor_tensor(dst[:, step:], src[:, step:], src[:, 0:TOKEN_TILES - step], ALU.add))
                at, step = 1 - at, 2 * step
            running = scans[at]
            counts = running[:, TOKEN_TILES - 1]
            link(V.tensor_scalar(whole[:], counts, float(P - 1), None, ALU.add))
            link(V.tensor_scalar(shift[:], whole[:], P.bit_length() - 1, None, ALU.logical_shift_right))
            link(V.tensor_copy(small[0][:], shift[:]))
            link(V.tensor_copy(small[1][:], small[0][:]))
            now, step = 1, 1
            while step < EXPERTS:
                src, dst = small[now], small[now + 1]
                link(V.tensor_copy(dst[:, 0:step], src[:, 0:step]))
                link(V.tensor_tensor(dst[:, step:], src[:, step:], src[:, 0:EXPERTS - step], ALU.add))
                now, step = now + 1, 2 * step
            ends, starts = small[now], small[now + 1]
            link(V.tensor_tensor(starts[:], ends[:], small[0][:], ALU.subtract))
            link(V.scalar_tensor_tensor(out=slot_f[:], in0=over(starts), scalar=float(P), in1=running[:],
                                        op0=ALU.mult, op1=ALU.add))
            link(V.tensor_tensor(picked[:], slot_f[:], total[:], ALU.subtract))
            link(V.tensor_tensor(flat(slot_f), flat(picked), pr[:], ALU.add))
            for n in range(2):
                link(V.tensor_tensor(picked[:], slot_f[:], chosen[n][:], ALU.mult))
                link(V.tensor_reduce(slot_sum[:], picked[:], AX.X, ALU.add))
                link(V.tensor_copy(slots[:, n], slot_sum[:]))
            link(V.tensor_tensor(past[:], tile_no[:].unsqueeze(2).broadcast_to([P, TILES, EXPERTS]),
                                 ends[:].unsqueeze(1).broadcast_to([P, TILES, EXPERTS]), ALU.is_ge))
            link(V.tensor_reduce(past_sum[:], past[:], AX.X, ALU.add))
            link(V.tensor_scalar(past_cap[:], past_sum[:], float(EXPERTS - 1), None, ALU.min))
            V.tensor_copy(tile_expert[:], past_cap[:]).then_inc(slots_s, 2)


def experts(nc, b1, b2, ident, w1_hi, w1_lo, w2_hi, w2_lo, tile_expert, slot_rows, slot_out):
    with ExitStack() as ctx:
        a = Names(nc, ctx, "exp")
        idt = a.sbuf("ident", [P, P])
        b1_t = a.sbuf("b1", [P, EXPERTS, HID])
        b2_t = a.sbuf("b2", [P, EXPERTS, C])
        x_in = a.sbuf("x_in", [P, 2, C])
        x_hi = a.sbuf("x_hi", [P, 2, CC, P], F32R)
        x_lo = a.sbuf("x_lo", [P, 2, CC, P], F32R)
        pre = a.sbuf("pre", [P, 2, HID])
        act_t = a.sbuf("gelu", [P, 2, HID])
        h_hi = a.sbuf("h_hi", [P, 2, HK, P], F32R)
        h_lo = a.sbuf("h_lo", [P, 2, HK, P], F32R)
        y = a.sbuf("y", [P, 2, C])
        px = a.psum("x_turned", [P, HALF])[:, 0:CC * P].rearrange("p (k n) -> p k n", k=CC)
        ph = a.psum("hidden", [P, 2, HID])
        pt = a.psum("hidden_turned", [P, 2, HK, P])
        py = a.psum("y_acc", [P, 2, HALF])
        consts = a.sem("consts_loaded")
        x_loaded = [a.sem(f"x_loaded{i}") for i in range(2)]
        y_stored = [a.sem(f"y_stored{i}") for i in range(2)]
        x_turned, x_hi_s, x_lo_s = a.sem("x_turned"), a.sem("x_hi_ready"), a.sem("x_lo_ready")
        hidden, pre_s, gelu_s = a.sem("hidden"), a.sem("pre_ready"), a.sem("gelu_ready")
        h_turned, h_hi_s, h_lo_s = a.sem("h_turned"), a.sem("h_hi_ready"), a.sem("h_lo_ready")
        y_acc, y_s = a.sem("y_acc"), a.sem("y_ready")
        rows_in = slot_rows.rearrange("(n p) c -> n p c", p=P)
        rows_out = slot_out.rearrange("(n p) c -> n p c", p=P)
        LAST = TILES - 1

        def tile(ap, i):
            return ap[i] if isinstance(i, int) else ap[bass.ds(i, 1)].rearrange("o p c -> (o p) c")

        def over_tiles(engine, body):
            for i in range(4):
                body(i, i % 2)
            with engine.Fori(2, TILES // 2 - 1) as r:
                body(2 * r, 0)
                body(2 * r + 1, 1)
            for i in range(TILES - 2, TILES + 2):
                body(i, i % 2)

        def exists(i):
            return not isinstance(i, int) or 0 <= i <= LAST

        def expert_of(engine, i):
            at = tile_expert[0:1, i:i + 1] if isinstance(i, int) else tile_expert[0:1, bass.ds(i, 1)]
            return engine.value_load(at, min_val=0, max_val=EXPERTS - 1)

        block = ctx.enter_context(nc.Block())

        @block.sync
        def _(sp):
            sp.dma_start(idt[:], ident).then_inc(consts, 16)
            sp.dma_start(x_in[:, 0], tile(rows_in, 0)).then_inc(x_loaded[0], 16)
            sp.dma_start(b1_t[:], b1.partition_broadcast(P)).then_inc(consts, 16)
            sp.dma_start(b2_t[:], b2.partition_broadcast(P)).then_inc(consts, 16)
            sp.dma_start(x_in[:, 1], tile(rows_in, 1)).then_inc(x_loaded[1], 16)

            def body(i, s):
                if exists(i + 2):
                    sp.wait_ge(x_turned, i + 1)
                    sp.dma_start(x_in[:, s], tile(rows_in, i + 2)).then_inc(x_loaded[s], 16)
                if exists(i - 2):
                    sp.wait_ge(y_s, i - 1)
                    sp.dma_start(tile(rows_out, i - 2), y[:, s]).then_inc(y_stored[s], 16)

            for i in range(4):
                body(i, i % 2)
            with sp.Fori(2, TILES // 2 - 1) as r:
                body(2 * r, 0)
                body(2 * r + 1, 1)
            for i in range(TILES - 2, TILES + 2):
                body(i, i % 2)
            for s in range(2):
                sp.wait_ge(y_stored[s], 16 * TILES // 2)

        @block.tensor
        def _(pe):
            def turn_x(i, s):
                pe.wait_ge(x_loaded[s], 16 * (i // 2 + 1) if isinstance(i, int) else 8 * i + (16 if s == 0 else 8))
                after(pe, x_lo_s, i)
                for c in range(CC):
                    last = nc.tensor.transpose(px[:, c], x_in[:, s, c * P:(c + 1) * P], idt[:])
                last.then_inc(x_turned, 1)

            def three(out, xs, ws, e, chunks, s):
                n, steps = 0, 3 * chunks
                for k in range(chunks):
                    for w, xx in ((ws[0], xs[0]), (ws[0], xs[1]), (ws[1], xs[0])):
                        last = nc.tensor.matmul(out, xx[:, s, k], w[:, bass.ds(e, 1), k].rearrange("p o n -> p (o n)"),
                                                start=n == 0, stop=n == steps - 1)
                        n += 1
                return last

            pe.wait_ge(consts, 48)
            turn_x(0, 0)

            def body(i, s):
                if exists(i):
                    e = expert_of(pe, i)
                    pe.wait_ge(x_lo_s, i + 1)
                    after(pe, pre_s, i - 1)
                    three(ph[:, s], (x_hi, x_lo), (w1_hi, w1_lo), e, CC, s).then_inc(hidden, 1)
                if exists(i + 1):
                    turn_x(i + 1, 1 - s)
                if exists(i - 1):
                    pe.wait_ge(gelu_s, i)
                    after(pe, h_lo_s, i - 2)
                    for k in range(HK):
                        last = nc.tensor.transpose(pt[:, 1 - s, k], act_t[:, 1 - s, k * P:(k + 1) * P], idt[:])
                    last.then_inc(h_turned, 1)
                if exists(i - 2):
                    e = expert_of(pe, i - 2)
                    pe.wait_ge(h_lo_s, i - 1)
                    after(pe, y_s, i - 3)
                    three(py[:, s, 0:C], (h_hi, h_lo), (w2_hi, w2_lo), e, HK, s).then_inc(y_acc, 1)

            over_tiles(pe, body)

        @block.scalar
        def _(act):
            def x_high(i, s):
                act.wait_ge(x_turned, i + 1)
                after(act, hidden, i - 1)
                nc.scalar.activation(x_hi[:, s], px, ACT.Copy).then_inc(x_hi_s, 1)

            x_high(0, 0)

            def body(i, s):
                if exists(i + 1):
                    x_high(i + 1, 1 - s)
                if exists(i - 1):
                    act.wait_ge(h_turned, i)
                    after(act, y_acc, i - 3)
                    nc.scalar.activation(h_hi[:, 1 - s], pt[:, 1 - s], ACT.Copy).then_inc(h_hi_s, 1)
                if exists(i):
                    act.wait_ge(pre_s, i + 1)
                    after(act, h_turned, i - 1)
                    nc.scalar.activation(act_t[:, s], pre[:, s], ACT.Gelu).then_inc(gelu_s, 1)

            over_tiles(act, body)

        @block.vector
        def _(dve):
            def x_low(i, s):
                dve.wait_ge(x_hi_s, i + 1)
                nc.vector.tensor_tensor(x_lo[:, s], px, x_hi[:, s].bitcast(F32), ALU.subtract).then_inc(x_lo_s, 1)

            dve.wait_ge(consts, 48)
            x_low(0, 0)

            def body(i, s):
                if exists(i + 1):
                    x_low(i + 1, 1 - s)
                if exists(i - 1):
                    dve.wait_ge(h_hi_s, i)
                    nc.vector.tensor_tensor(h_lo[:, 1 - s], pt[:, 1 - s], h_hi[:, 1 - s].bitcast(F32), ALU.subtract)\
                        .then_inc(h_lo_s, 1)
                if exists(i):
                    e = expert_of(dve, i)
                    dve.wait_ge(hidden, i + 1)
                    after(dve, gelu_s, i - 1)
                    nc.vector.tensor_tensor(pre[:, s], ph[:, s], b1_t[:, bass.ds(e, 1)].rearrange("p o n -> p (o n)"),
                                            ALU.add).then_inc(pre_s, 1)
                if exists(i - 2):
                    e = expert_of(dve, i - 2)
                    dve.wait_ge(y_acc, i - 1)
                    if not (isinstance(i, int) and i - 2 < 2):
                        dve.wait_ge(y_stored[s], 16 * ((i - 2) // 2) if isinstance(i, int) else 8 * i - (16 if s == 0 else 24))
                    nc.vector.tensor_tensor(y[:, s], py[:, s, 0:C], b2_t[:, bass.ds(e, 1)].rearrange("p o n -> p (o n)"),
                                            ALU.add).then_inc(y_s, 1)

            over_tiles(dve, body)


def combine(nc, x1, slots, weights, slot_out, out):
    R = 4
    with ExitStack() as ctx:
        a = Names(nc, ctx, "comb")
        x_in = a.sbuf("x_in", [P, R, C])
        ys = a.sbuf("y", [P, R, 2, C])
        index = a.sbuf("index", [P, R, 2], mybir.dt.uint32)
        index_s = a.sem("index_ready")
        passed = a.sem("waits_passed")
        part = a.sbuf("part", [P, R, C])
        res = a.sbuf("res", [P, R, C])
        loaded = [a.sem(f"x_loaded{i}") for i in range(R)]
        gathered = [a.sem(f"y_gathered{i}") for i in range(R)]
        stored = [a.sem(f"stored{i}") for i in range(R)]
        part_s, res_s = a.sem("part_ready"), a.sem("res_ready")
        xv = x1.rearrange("(n p) c -> n p c", p=P)
        ov = out.rearrange("(n p) c -> n p c", p=P)
        ROUNDS = TOKEN_TILES // R
        block = ctx.enter_context(nc.Block())

        def rounds(engine, body):
            body(0, True)
            with engine.Fori(1, ROUNDS) as r:
                body(r, False)

        def at(ap, r, t):
            return ap[t] if isinstance(r, int) else ap[bass.ds(R * r + t, 1)].rearrange("o p c -> (o p) c")

        @block.sync
        def _(sp):
            def body(r, first):
                for t in range(R):
                    if not first:
                        sp.wait_ge(res_s, R * (r - 1) + t + 1)
                    sp.dma_start(x_in[:, t], at(xv, r, t)).then_inc(loaded[t], 16)
            rounds(sp, body)

        @block.scalar
        def _(act):
            def body(r, first):
                for t in range(R):
                    act.wait_ge(res_s, R * r + t + 1)
                    act.dma_start(at(ov, r, t), res[:, t]).then_inc(stored[t], 16)
            rounds(act, body)
            for t in range(R):
                act.wait_ge(stored[t], 16 * ROUNDS)

        @block.gpsimd
        def _(pool):
            def body(r, first):
                for t in range(R):
                    if not first:
                        pool.wait_ge(res_s, R * (r - 1) + t + 1)
                    cols = slots[:, :, t] if first else slots[:, :, bass.ds(R * r + t, 1)].rearrange("p n o -> p (n o)")
                    nc.gpsimd.tensor_copy(index[:, t], cols).then_inc(index_s, 1)
                    pool.wait_ge(index_s, R * r + t + 1)
                    pool.sem_inc(passed, 1)
                    for n in range(2):
                        nc.gpsimd.indirect_dma_start(ys[:, t, n], None, slot_out,
                                                     bass.IndirectOffsetOnAxis(index[:, t, n:n + 1], 0))\
                            .then_inc(gathered[t], 16)
            rounds(pool, body)

        @block.vector
        def _(dve):
            def body(r, first):
                for t in range(R):
                    w = lambda n: weights[:, n, t:t + 1] if first else weights[:, n, bass.ds(R * r + t, 1)]
                    dve.wait_ge(loaded[t], 16 * (r + 1))
                    dve.wait_ge(gathered[t], 32 * (r + 1))
                    nc.vector.scalar_tensor_tensor(out=part[:, t], in0=ys[:, t, 0], scalar=w(0), in1=x_in[:, t],
                                                   op0=ALU.mult, op1=ALU.add).then_inc(part_s, 1)
                    dve.wait_ge(part_s, R * r + t + 1)
                    if not first:
                        dve.wait_ge(stored[t], 16 * r)
                    nc.vector.scalar_tensor_tensor(out=res[:, t], in0=ys[:, t, 1], scalar=w(1), in1=part[:, t],
                                                   op0=ALU.mult, op1=ALU.add).then_inc(res_s, 1)
            rounds(dve, body)


def shape_constants():
    f = np.float32
    half = f(1.0) / (f(10000.0) ** np.linspace(0.0, 1.0, D // 2, dtype=f))
    angle = np.repeat(half, 2)
    index = (np.arange(N1, dtype=f)[:, None] + np.arange(N2, dtype=f)[None, :]).reshape(L)
    phase = (index[:, None] * angle[None, :]).astype(f)
    sign = np.where(np.arange(D) % 2 == 0, f(-1), f(1))
    cos = np.tile(np.cos(phase).astype(f).T, (HG, 1))
    sin = np.tile((np.sin(phase).astype(f) * sign).T, (HG, 1))
    decay = np.log(f(1.0) - f(2.0) ** (f(-2.0) - f(5.0) * np.arange(H, dtype=f) / f(H))).astype(f)
    row, col = np.divmod(np.arange(P), N2)
    rows_apart = np.abs(np.arange(SPAN)[None, :] - (SPAN - N1) - row[:, None])
    cols_apart = np.abs(np.arange(N2)[None, :] - col[:, None])
    apart = (rows_apart[:, None, :, None] + cols_apart[:, None, None, :]).astype(f)
    table = np.exp(apart * decay[None, :, None, None]).astype(f)
    line = np.exp(np.abs(np.arange(N1)[:, None] - np.arange(N1)[None, :]).astype(f) * decay[:, None, None])
    sums = line.astype(np.float64).sum(-1)
    total = (sums[:, :, None] * sums[:, None, :]).reshape(H, L)
    factor = (D ** -0.5 / np.sqrt(total)).astype(f)
    factor = factor.reshape(H, KT, P).transpose(2, 1, 0)
    return {"cos": cos, "sin": sin, "decay": table.reshape(P, H, SPAN * N2),
            "factor": np.ascontiguousarray(factor), "ident": np.eye(P, dtype=f),
            "upper": np.triu(np.ones((P, P), dtype=f), 1)}


def block_program(nc, io):
    scratch = lambda name, shape: nc.dram_tensor(name, shape, F32).ap()
    parts = [scratch(n, (B, C, L)) for n in ("q_hi", "q_lo", "k_hi", "k_lo")]
    v, x1, xn = (scratch(n, (T, C)) for n in ("v_rows", "x1_rows", "xn_rows"))
    slot_rows, slot_out = (scratch(n, (TILES * P, C)) for n in ("slot_rows", "slot_out"))
    project(nc, io["x"], io["wq"], io["wk"], io["wv"], io["cos"], io["sin"], io["ident"], *parts, v)
    retain(nc, io["x"], io["wo"], io["ln_g"], io["ln_b"], io["decay"], io["factor"], io["ident"], *parts, v, x1)
    with ExitStack() as ctx:
        a = Names(nc, ctx, "moe")
        w1p = [a.sbuf(f"w1_{n}", [P, EXPERTS, CC, HID], F32R) for n in ("hi", "lo")]
        w2p = [a.sbuf(f"w2_{n}", [P, EXPERTS, HK, C], F32R) for n in ("hi", "lo")]
        slots = a.sbuf("slots", [P, 2, TOKEN_TILES], mybir.dt.uint32)
        weights = a.sbuf("weights", [P, 2, TOKEN_TILES])
        tile_expert = a.sbuf("tile_expert", [P, TILES], mybir.dt.int32)
        route(nc, x1, io["gate_w"], io["gate_b"], io["w1"], io["w2"], io["upper"], io["ident"],
              *w1p, *w2p, slots, weights, tile_expert, xn, slot_rows)
        experts(nc, io["b1"], io["b2"], io["ident"], *w1p, *w2p, tile_expert, slot_rows, slot_out)
        combine(nc, x1, slots, weights, slot_out, io["out"])


def kernel(x, L0_conv_Wq, L0_conv_Wk, L0_conv_Wv, L0_conv_Wo, L0_conv_ln_g, L0_conv_ln_b,
           L0_ffn_gate_w, L0_ffn_gate_b, L0_ffn_W1, L0_ffn_b1, L0_ffn_W2, L0_ffn_b2):
    import concourse.bacc as bacc
    from concourse.bass_utils import run_bass_kernel_spmd

    turned = lambda w: np.ascontiguousarray(np.asarray(w).T)
    arrays = {
        "x": np.ascontiguousarray(np.asarray(x)).reshape(T, C),
        "wq": turned(L0_conv_Wq), "wk": turned(L0_conv_Wk), "wv": turned(L0_conv_Wv), "wo": turned(L0_conv_Wo),
        "ln_g": np.asarray(L0_conv_ln_g), "ln_b": np.asarray(L0_conv_ln_b),
        "gate_w": np.asarray(L0_ffn_gate_w), "gate_b": np.asarray(L0_ffn_gate_b),
        "w1": np.asarray(L0_ffn_W1), "b1": np.asarray(L0_ffn_b1),
        "w2": np.asarray(L0_ffn_W2), "b2": np.asarray(L0_ffn_b2),
        **shape_constants(),
    }
    nc = bacc.Bacc("TRN2", target_bir_lowering=False, num_devices=1)
    io = {n: nc.dram_tensor(n, a.shape, mybir.dt.from_np(a.dtype), kind="ExternalInput").ap()
          for n, a in arrays.items()}
    io["out"] = nc.dram_tensor("out", (T, C), F32, kind="ExternalOutput").ap()
    block_program(nc, io)
    result = run_bass_kernel_spmd(nc, [arrays], core_ids=[0])
    return result.results[0]["out"].reshape(B, N1, N2, C)
```

```python
from contextlib import ExitStack

import numpy as np

import concourse.bass as bass
from concourse import mybir
from concourse.alu_op_type import AluOpType as ALU

F32 = mybir.dt.float32
F32R = mybir.dt.float32r
ACT = mybir.ActivationFunctionType
AX = mybir.AxisListType

B, N1, N2, C = 8, 32, 32, 256
L = N1 * N2
H, D = 8, C // 8
T = B * L
P = 128
HALF = 512
CC = C // P
HG = P // D
TT = HALF // P
ROWS = P // N2
KT = L // P
SPAN = N1 + (KT - 1) * ROWS
EXPERTS, HID = 8, 512
SWAP = [i ^ 1 for i in range(D)]


def after(engine, semaphore, value):
    if not (isinstance(value, int) and value <= 0):
        engine.wait_ge(semaphore, value)


def over_batches(engine, body):
    body(0, True, False)
    with engine.Fori(1, B - 2) as b:
        body(b, False, False)
    body(B - 2, False, False)
    body(B - 1, False, True)


class Names:

    def __init__(self, nc, ctx, phase):
        self.nc, self.ctx, self.phase = nc, ctx, phase

    def sbuf(self, name, shape, dtype=F32):
        return self.ctx.enter_context(self.nc.sbuf_tensor(f"{self.phase}_{name}", shape, dtype))

    def psum(self, name, shape):
        return self.ctx.enter_context(self.nc.psum_tensor(f"{self.phase}_{name}", shape, F32))

    def sem(self, name):
        return self.ctx.enter_context(self.nc.semaphore(f"{self.phase}_{name}"))


class RetainConstants:

    def __init__(self, nc, ctx):
        a = Names(nc, ctx, "tables")
        self.decay = a.sbuf("decay", [P, H, SPAN * N2])
        self.factor = a.sbuf("factor", [P, KT, H])
        self.ident = a.sbuf("ident", [P, P])
        self.wo = a.sbuf("wo", [P, CC, C])
        self.gain_bias = a.sbuf("gain_bias", [P, 2])
        self.small_loaded, self.decay_loaded = a.sem("small_loaded"), a.sem("decay_loaded")
        self.SMALL, self.DECAY = 16 * (3 + 2 * HG), 16 * H

    def load_small(self, sp, io):
        for dst, src in ((self.factor, io["factor"]), (self.ident, io["ident"])):
            sp.dma_start(dst[:], src).then_inc(self.small_loaded, 16)
        sp.dma_start(self.wo[:], io["wo"].rearrange("(k p) c -> p k c", p=P)).then_inc(self.small_loaded, 16)
        for n, y in enumerate((io["ln_g"], io["ln_b"])):
            for h in range(HG):
                sp.dma_start(self.gain_bias[h * D:(h + 1) * D, n:n + 1], y.rearrange("(d o) -> d o", o=1))\
                    .then_inc(self.small_loaded, 16)

    def load_decay(self, sp, io, h):
        at = slice(h, h + 1) if isinstance(h, int) else bass.ds(h, 1)
        sp.dma_start(self.decay[:, at], io["decay"][:, at]).then_inc(self.decay_loaded, 16)

    def wait(self, engine):
        engine.wait_ge(self.small_loaded, self.SMALL)
        engine.wait_ge(self.decay_loaded, self.DECAY)


def project(nc, io, tables, q_hi, q_lo, k_hi, k_lo, v_out):
    x, wq, wk, wv, cos, sin, ident = (io[n] for n in ("x", "wq", "wk", "wv", "cos", "sin", "ident"))
    assert B == H
    PIECES = 2 * CC
    R = PIECES
    with ExitStack() as ctx:
        a = Names(nc, ctx, "proj")
        wf = a.sbuf("w_float", [P, 3, CC, C])
        w_hi = a.sbuf("w_hi", [P, 3, CC, C], F32R)
        w_lo = a.sbuf("w_lo", [P, 3, CC, C], F32R)
        cos_t = a.sbuf("cos", [P, L])
        sin_t = a.sbuf("sin", [P, L])
        idt = a.sbuf("ident", [P, P])
        power = a.sbuf("power", [P, TT])
        eps = a.sbuf("eps", [P, TT])
        x_in = a.sbuf("x_in", [P, 2, TT, C])
        stats = a.sbuf("stats", [P, TT, 6])
        mean_var = a.sbuf("mean_var", [P, TT, 2])
        rstd_in = a.sbuf("rstd_in", [P, TT])
        rstd = a.sbuf("rstd", [P, TT])
        xn = a.sbuf("xn", [P, TT, C])
        x_hi = a.sbuf("x_hi", [P, 2, CC, HALF], F32R)
        x_lo = a.sbuf("x_lo", [P, 2, CC, HALF], F32R)
        by_cos = a.sbuf("by_cos", [P, R, HALF])
        swapped = a.sbuf("swapped", [P, 2, HALF])
        by_sin = a.sbuf("by_sin", [P, R, HALF])
        turned = a.sbuf("turned", [P, R, HALF])
        t_hi = a.sbuf("turned_hi", [P, R, HALF], F32R)
        t_lo = a.sbuf("turned_lo", [P, R, HALF], F32R)
        v_sb = a.sbuf("v", [P, 2, TT, C])
        pt = a.psum("x_turned", [P, CC, HALF])
        pa = a.psum("product", [P, R, HALF])
        pv = a.psum("v_acc", [P, CC, HALF])

        consts = a.sem("consts_loaded")
        power_set = a.sem("power_set")
        passed = a.sem("waits_passed")
        w_hi_ready, w_ready = a.sem("w_hi_ready"), a.sem("w_ready")
        x_loaded = [a.sem(f"x_loaded{i}") for i in range(2)]
        stats_done, moments_done = a.sem("stats_done"), a.sem("moments_done")
        eps_added, rstd_ready = a.sem("eps_added"), a.sem("rstd_ready")
        xn_ready, xt_ready = a.sem("xn_ready"), a.sem("xt_ready")
        x_hi_ready, x_lo_ready = a.sem("x_hi_ready"), a.sem("x_lo_ready")
        products = a.sem("products_ready")
        cos_done, swap_done, sin_done = a.sem("cos_done"), a.sem("swap_done"), a.sem("sin_done")
        turned_ready = a.sem("turned_ready")
        hi_ready, lo_ready = a.sem("hi_ready"), a.sem("lo_ready")
        stored = [a.sem(f"parts_stored{i}") for i in range(R)]
        v_acc_ready, v_ready = a.sem("v_acc_ready"), a.sem("v_ready")
        v_stored = [a.sem(f"v_stored{i}") for i in range(2)]

        xv = x.rearrange("(n t p) c -> n p t c", p=P, t=TT)
        vv = v_out.rearrange("(n t p) c -> n p t c", p=P, t=TT)
        parts = [(hi.rearrange("b (c p) l -> b c p l", p=P), lo.rearrange("b (c p) l -> b c p l", p=P))
                 for hi, lo in ((q_hi, q_lo), (k_hi, k_lo))]
        def one(i, n):
            return i if isinstance(i, int) else bass.ds(i, n)

        def block_of(ap, j):
            return ap[j] if isinstance(j, int) else ap[bass.ds(j, 1)].rearrange("o p t c -> (o p) t c")

        block = ctx.enter_context(nc.Block())

        @block.sync
        def _(sp):
            for j in range(2):
                sp.dma_start(x_in[:, j], block_of(xv, j)).then_inc(x_loaded[j], 16)
            for n, w in enumerate((wq, wk, wv)):
                sp.dma_start(wf[:, n], w.rearrange("(k p) c -> p k c", p=P)).then_inc(consts, 16)
            for dst, src in ((cos_t, cos), (sin_t, sin), (idt, ident)):
                sp.dma_start(dst[:], src).then_inc(consts, 16)
            sp.wait_ge(xn_ready, 1)
            sp.dma_start(x_in[:, 0], block_of(xv, 2)).then_inc(x_loaded[0], 16)
            tables.load_small(sp, io)

            def body(b, first, last):
                for h in range(2):
                    j = 2 * b + h
                    if h == 1:
                        tables.load_decay(sp, io, b)
                    for m in range(PIECES):
                        n = PIECES * j + m
                        for part, src, ready in ((0, t_hi, hi_ready), (1, t_lo, lo_ready)):
                            sp.wait_ge(ready, n + 1)
                            dst = parts[m // CC][part]
                            dst = dst[b, m % CC] if isinstance(b, int) else \
                                dst[bass.ds(b, 1), m % CC].rearrange("o p l -> (o p) l")
                            sp.dma_start(dst[:, h * HALF:(h + 1) * HALF], src[:, m].bitcast(F32))\
                                .then_inc(stored[m], 16)
                        if m == 1 and not last and not (isinstance(b, int) and b == B - 2 and h == 1):
                            sp.wait_ge(xn_ready, j + 2)
                            sp.dma_start(x_in[:, 1 - h], block_of(xv, j + 3)).then_inc(x_loaded[1 - h], 16)
                    sp.wait_ge(v_ready, 2 * (j + 1))
                    sp.dma_start(block_of(vv, j), v_sb[:, h]).then_inc(v_stored[h], 16)

            over_batches(sp, body)
            for i in range(R):
                sp.wait_ge(stored[i], 2 * B * 32)
            for i in range(2):
                sp.wait_ge(v_stored[i], B * 16)

        @block.gpsimd
        def _(pool):
            nc.gpsimd.memset(power[:], -0.5).then_inc(power_set, 1)
            nc.gpsimd.memset(eps[:], 1e-6).then_inc(power_set, 1)
            pool.wait_ge(power_set, 2)

            def scale_of(j):
                pool.wait_ge(moments_done, j + 1)
                after(pool, xn_ready, j)
                nc.gpsimd.tensor_tensor(rstd_in[:], mean_var[:, :, 1], eps[:], ALU.add)\
                    .then_inc(eps_added, 1)
                pool.wait_ge(eps_added, j + 1)
                nc.gpsimd.tensor_tensor(rstd[:], rstd_in[:], power[:], ALU.pow).then_inc(rstd_ready, 1)

            scale_of(0)

            def low_part(n, i):
                pool.wait_ge(hi_ready, n + 1)
                if isinstance(n, int):
                    after(pool, stored[i], 32 * (n // PIECES))
                else:
                    pool.wait_ge(stored[i], 8 * (n - i))
                nc.gpsimd.tensor_tensor(t_lo[:, i], turned[:, i], t_hi[:, i].bitcast(F32), ALU.subtract)\
                    .then_inc(lo_ready, 1)

            def body(b, first, last):
                for h in range(2):
                    j = 2 * b + h
                    for m in range(PIECES):
                        n, i = PIECES * j + m, m
                        if m == 0 and not (last and h == 1):
                            scale_of(j + 1)
                        pool.wait_ge(sin_done, n + 1)
                        if not (first and h == 0):
                            pool.wait_ge(lo_ready, n - R + 1)
                        nc.gpsimd.tensor_tensor(turned[:, i], by_cos[:, i], by_sin[:, i], ALU.add)\
                            .then_inc(turned_ready, 1)
                        if not (first and h == 0 and m == 0):
                            low_part(n - 1, (i - 1) % R)

            over_batches(pool, body)
            low_part(PIECES * 2 * B - 1, R - 1)

        @block.vector
        def _(dve):
            dve.wait_ge(consts, 6 * 16)
            nc.vector.tensor_copy(w_hi[:], wf[:]).then_inc(w_hi_ready, 1)
            dve.wait_ge(w_hi_ready, 1)
            nc.vector.tensor_tensor(w_lo[:], wf[:], w_hi[:].bitcast(F32), ALU.subtract).then_inc(w_ready, 1)

            def moments(j, h):
                dve.wait_ge(x_loaded[h], 16 * (j // 2 + 1) if isinstance(j, int) else 8 * j + (16 if h == 0 else 8))
                after(dve, moments_done, j)
                for t in range(TT):
                    last = nc.vector.bn_stats(stats[:, t], x_in[:, h, t])
                last.then_inc(stats_done, 1)
                dve.wait_ge(stats_done, j + 1)
                after(dve, xn_ready, j)
                after(dve, rstd_ready, j)
                dve.sem_inc(passed, 1)
                for t in range(TT):
                    last = nc.vector.bn_aggr(mean_var[:, t], stats[:, t])
                last.then_inc(moments_done, 1)

            def norm(j, h):
                dve.wait_ge(rstd_ready, j + 1)
                after(dve, xt_ready, 2 * j)
                for t in range(TT):
                    last = nc.vector.tensor_scalar(xn[:, t], x_in[:, h, t], mean_var[:, t, 0:1], rstd[:, t:t + 1],
                                                   ALU.subtract, ALU.mult)
                last.then_inc(xn_ready, 1)

            def low_part(j, h):
                for c in range(CC):
                    dve.wait_ge(x_hi_ready, CC * j + c + 1)
                    nc.vector.tensor_tensor(x_lo[:, h, c], pt[:, c], x_hi[:, h, c].bitcast(F32), ALU.subtract)\
                        .then_inc(x_lo_ready, 1)

            moments(0, 0)
            norm(0, 0)
            moments(1, 1)
            low_part(0, 0)

            def body(b, first, last):
                for h in range(2):
                    j = 2 * b + h
                    ahead = not (last and h == 1)
                    for m in range(PIECES):
                        n, i = PIECES * j + m, m
                        dve.wait_ge(products, n + 1)
                        if not (first and h == 0):
                            dve.wait_ge(turned_ready, n - R + 1)
                        at = slice(h * HALF, (h + 1) * HALF)
                        dve.sem_inc(passed, 1)
                        nc.vector.stream_shuffle(swapped[:, i % 2], pa[:, i], SWAP).then_inc(swap_done, 1)
                        nc.vector.tensor_tensor(by_cos[:, i], pa[:, i], cos_t[:, at], ALU.mult).then_inc(cos_done, 1)
                        dve.wait_ge(swap_done, n + 1)
                        nc.vector.tensor_tensor(by_sin[:, i], swapped[:, i % 2], sin_t[:, at], ALU.mult)\
                            .then_inc(sin_done, 1)
                        if ahead:
                            if m == 0:
                                norm(j + 1, 1 - h)
                            if m == 2:
                                low_part(j + 1, 1 - h)
                        if m == 3 and not last:
                            moments(j + 2, h)

            over_batches(dve, body)

        @block.scalar
        def _(act):
            def high_part(j, h):
                for c in range(CC):
                    act.wait_ge(xt_ready, CC * j + c + 1)
                    nc.scalar.activation(x_hi[:, h, c], pt[:, c], ACT.Copy).then_inc(x_hi_ready, 1)

            high_part(0, 0)

            def body(b, first, last):
                for h in range(2):
                    j = 2 * b + h
                    for m in range(PIECES):
                        n, i = PIECES * j + m, m
                        if m == 2 and not (last and h == 1):
                            high_part(j + 1, 1 - h)
                        act.wait_ge(turned_ready, n + 1)
                        after(act, stored[i], 32 * j)
                        nc.scalar.activation(t_hi[:, i], turned[:, i], ACT.Copy).then_inc(hi_ready, 1)
                        if m % 2:
                            c = m // 2
                            if c == 0 and not first:
                                act.wait_ge(v_stored[h], 16 * b)
                            act.wait_ge(v_acc_ready, CC * j + c + 1)
                            nc.scalar.activation(v_sb[:, h, 2 * c:2 * c + 2, :],
                                                 pv[:, c].rearrange("p (t c) -> p t c", t=2), ACT.Copy)\
                                .then_inc(v_ready, 1)

            over_batches(act, body)

        @block.tensor
        def _(pe):
            def turn(j, h):
                pe.wait_ge(xn_ready, j + 1)
                after(pe, x_lo_ready, CC * j)
                for c in range(CC):
                    for t in range(TT):
                        last = nc.tensor.transpose(pt[:, c, t * P:(t + 1) * P], xn[:, t, c * P:(c + 1) * P], idt[:])
                    last.then_inc(xt_ready, 1)

            def three(out, pairs):
                for n, (l, r) in enumerate(pairs):
                    last = nc.tensor.matmul(out, l, r, start=n == 0, stop=n == len(pairs) - 1)
                return last

            pe.wait_ge(consts, 6 * 16)
            turn(0, 0)
            pe.wait_ge(w_ready, 1)

            assert TT == PIECES
            def body(b, first, last):
                for h in range(2):
                    j = 2 * b + h
                    pe.wait_ge(x_lo_ready, CC * (j + 1))
                    for m in range(PIECES):
                        n, i = PIECES * j + m, m
                        kind, c = m // CC, m % CC
                        cols = slice(c * P, (c + 1) * P)
                        if not (first and h == 0):
                            pe.wait_ge(cos_done, n - R + 1)
                        three(pa[:, i], [(w[:, kind, k, cols], y[:, h, k]) for k in range(CC)
                                         for w, y in ((w_hi, x_hi), (w_hi, x_lo), (w_lo, x_hi))]).then_inc(products, 1)
                        if m == 2 and not (last and h == 1):
                            turn(j + 1, 1 - h)
                        t, c = m, m // 2
                        if t % 2 == 0 and not (first and h == 0):
                            pe.wait_ge(v_ready, CC * (j - 1) + c + 1)
                        rows = slice(t * P, (t + 1) * P)
                        done = three(pv[:, c, (t % 2) * C:(t % 2 + 1) * C],
                                     [(y[:, h, k, rows], w[:, 2, k])
                                      for k in range(CC) for w, y in ((w_hi, x_hi), (w_hi, x_lo), (w_lo, x_hi))])
                        if t % 2:
                            done.then_inc(v_acc_ready, 1)

            over_batches(pe, body)


def retain(nc, x, tables, q_hi, q_lo, k_hi, k_lo, v_in, x1):
    HALVES, GROUPS, PAIRS = L // HALF, H // HG, HG // 2
    UNITS = GROUPS * HALVES
    STEPS = KT * PAIRS
    P_RING = 4
    ADDED = (0, 1, 8, 9)
    SLOT = (0, 1, 2, 3, 6, 7, 6, 7, 4, 5, 6, 7, 0, 1, 2, 3)
    ROW_SUMS = {4: 5, 5: 6, 6: 7, 7: 8, 0: 9, 1: 10, 12: 13, 13: 14, 14: 15, 15: 16, 8: 17, 9: 18}
    TAKEN = {i: n + 1 for n, i in enumerate(ROW_SUMS)}
    SUMS = len(ROW_SUMS)
    assert KT == 8 and PAIRS == 2
    with ExitStack() as ctx:
        a = Names(nc, ctx, "ret")
        decay_t, factor_t, idt, wo_t, gb = tables.decay, tables.factor, tables.ident, tables.wo, tables.gain_bias
        ones = a.sbuf("ones", [P, D])
        power = a.sbuf("power", [P, TT * HG])
        eps = a.sbuf("eps", [P, TT * HG])
        k_st = a.sbuf("k_parts", [P, GROUPS, HG, L], F32R)
        q_st = a.sbuf("q_parts", [P, HALVES, HG, HALF], F32R)
        v_t = a.sbuf("v", [P, GROUPS, KT, P])
        decayed = a.sbuf("decayed", [P, P_RING, 2, HALF])
        magnitude = a.sbuf("magnitude", [P, max(SLOT) + 1, 2, HALF])
        o_sb = a.sbuf("o", [P, HALF])
        m_sb = a.sbuf("row_sums", [P, HALF])
        total = a.sbuf("total", [P, TT, HG])
        clipped = a.sbuf("clipped", [P, TT, HG])
        recip = a.sbuf("recip", [P, TT, HG])
        scale = a.sbuf("scale", [P, TT, HG])
        o_sum = a.sbuf("o_sum", [P, TT * HG])
        centred = a.sbuf("centred", [P, TT * HG, D])
        squared = a.sbuf("squared", [P, TT * HG, D])
        var_sum = a.sbuf("var_sum", [P, TT * HG])
        scale_sq = a.sbuf("scale_sq", [P, TT * HG])
        var_scaled = a.sbuf("var_scaled", [P, TT * HG])
        var_eps = a.sbuf("var_eps", [P, TT * HG])
        rstd = a.sbuf("rstd", [P, TT * HG])
        gain = a.sbuf("gain", [P, TT * HG])
        normed = a.sbuf("normed", [P, TT * HG, D])
        gelu_t = a.sbuf("gelu", [P, GROUPS, HALVES, HALF])
        x_res = a.sbuf("x_residual", [P, HALVES, TT, C])
        x_out = a.sbuf("x_out", [P, HALVES, TT, C])
        ps = a.psum("scores", [P, 2, 2, HALF])
        po = a.psum("o_acc", [P, HALF])
        pm = a.psum("row_sum_acc", [P, HALF])
        px = a.psum("turn_a", [P, HALF])
        py = a.psum("turn_b", [P, HALF])

        set_up = a.sem("set_up")
        k_loaded = [a.sem(f"k_loaded{i}") for i in range(GROUPS)]
        q_loaded = [a.sem(f"q_loaded{i}") for i in range(HALVES)]
        x_loaded = [a.sem(f"x_loaded{i}") for i in range(HALVES)]
        x_stored = [a.sem(f"x_stored{i}") for i in range(HALVES)]
        scores, decayed_s, magnitude_s = a.sem("scores_ready"), a.sem("decayed_ready"), a.sem("magnitude_ready")
        added_s = a.sem("magnitudes_added")
        values, row_sums = a.sem("values_added"), a.sem("row_sums_added")
        o_out, m_out = a.sem("o_copied"), a.sem("row_sums_copied")
        o_turned, m_turned = a.sem("o_turned"), a.sem("row_sums_turned")
        total_s, clip_s, recip_s, scale_s = (a.sem(n) for n in ("total", "clipped", "recip", "scale"))
        o_sum_s, centred_s, squared_s, var_s = (a.sem(n) for n in ("o_sum", "centred", "squared", "var_sum"))
        pool_chain = a.sem("pool_chain")
        rstd_s, normed_s = a.sem("rstd_ready"), a.sem("normed_ready")
        back_s, gelu_s = a.sem("normed_turned"), a.sem("gelu_ready")
        out_s, x_out_s = a.sem("projected"), a.sem("x_out_ready")

        xv = x.rearrange("(b h t p) c -> b h p t c", p=P, t=TT, h=HALVES)
        x1v = x1.rearrange("(b h t p) c -> b h p t c", p=P, t=TT, h=HALVES)
        vv = v_in.rearrange("(b k p) c -> b p k c", p=P, k=KT)
        split = lambda y: y.rearrange("b (g h d) l -> b g d h l", d=D, h=HG)

        def of_batch(ap, b, rest, names):
            if isinstance(b, int):
                return ap[(b, *rest)]
            inner = names.split()
            return ap[(bass.ds(b, 1), *rest)].rearrange(f"o {names} -> (o {inner[0]}) {' '.join(inner[1:])}")

        def batches(engine, body):
            over_batches(engine, body)

        block = ctx.enter_context(nc.Block())

        @block.sync
        def _(sp):
            rows = lambda n: slice(n * D, (n + 1) * D)

            def load_kv(b, g):
                for n, y in enumerate((k_hi, k_hi, k_lo, k_lo)):
                    sp.dma_start(k_st[rows(n), g].bitcast(F32), of_batch(split(y), b, (g,), "d h l"))\
                        .then_inc(k_loaded[g], 16)
                sp.dma_start(v_t[:, g], of_batch(vv, b, (slice(None), slice(None), slice(g * P, (g + 1) * P)), "p k c"))\
                    .then_inc(k_loaded[g], 16)

            def load_q(b, g, h):
                for n, y in enumerate((q_hi, q_lo, q_hi, q_lo)):
                    src = of_batch(split(y), b, (g, slice(None), slice(None), slice(h * HALF, (h + 1) * HALF)), "d h l")
                    sp.dma_start(q_st[rows(n), h].bitcast(F32), src).then_inc(q_loaded[h], 16)

            def load_x(b, h):
                sp.dma_start(x_res[:, h], of_batch(xv, b, (h,), "p t c")).then_inc(x_loaded[h], 16)

            load_kv(0, 0)
            load_q(0, 0, 0)
            load_q(0, 0, 1)
            load_kv(0, 1)
            load_x(0, 0)
            load_x(0, 1)

            def store(b, h):
                sp.wait_ge(x_out_s, 2 * (2 * b + h + 1))
                sp.dma_start(of_batch(x1v, b, (h,), "p t c"), x_out[:, h]).then_inc(x_stored[h], 16)

            def body(b, first, last):
                for k in range(UNITS):
                    g, h, u = k // HALVES, k % HALVES, UNITS * b + k
                    if k < HALVES and not first:
                        store(b - 1, k)
                        load_x(b, k)
                    sp.wait_ge(scores, STEPS * (u + 1))
                    if g == 0:
                        load_q(b, 1, h)
                    elif not last:
                        load_q(b + 1, 0, h)
                    if h == HALVES - 1 and not last:
                        sp.wait_ge(values, STEPS * (u + 1))
                        load_kv(b + 1, g)

            batches(sp, body)
            for h in range(HALVES):
                store(B - 1, h)
            for h in range(HALVES):
                sp.wait_ge(x_stored[h], 16 * B)

        @block.gpsimd
        def _(pool):
            nc.gpsimd.memset(power[:], -0.5).then_inc(set_up, 1)
            nc.gpsimd.memset(ones[:], 1.0).then_inc(set_up, 1)
            nc.gpsimd.memset(eps[:], 1e-5).then_inc(set_up, 1)
            pool.wait_ge(set_up, 3)

            def norm(u):
                wide = lambda y: y[:].unsqueeze(2).broadcast_to([P, TT * HG, D])
                pool.wait_ge(scale_s, u + 1)
                flat = scale[:].rearrange("p t h -> p (t h)")
                nc.gpsimd.tensor_tensor(scale_sq[:], flat, flat, ALU.mult).then_inc(pool_chain, 1)
                pool.wait_ge(var_s, u + 1)
                pool.wait_ge(pool_chain, 4 * u + 1)
                nc.gpsimd.tensor_tensor(var_scaled[:], var_sum[:], scale_sq[:], ALU.mult).then_inc(pool_chain, 1)
                pool.wait_ge(pool_chain, 4 * u + 2)
                nc.gpsimd.tensor_tensor(var_eps[:], var_scaled[:], eps[:], ALU.add).then_inc(pool_chain, 1)
                pool.wait_ge(pool_chain, 4 * u + 3)
                nc.gpsimd.tensor_tensor(rstd[:], var_eps[:], power[:], ALU.pow).then_inc(rstd_s, 1)
                pool.wait_ge(rstd_s, u + 1)
                nc.gpsimd.tensor_tensor(gain[:], rstd[:], flat, ALU.mult).then_inc(pool_chain, 1)
                pool.wait_ge(pool_chain, 4 * u + 4)
                after(pool, back_s, u)
                nc.gpsimd.tensor_tensor(normed[:], centred[:], wide(gain), ALU.mult).then_inc(normed_s, 1)

            def add(u, n):
                i = ADDED[n]
                pool.wait_ge(magnitude_s, STEPS * u + i + PAIRS + 1)
                one, two = magnitude[:, SLOT[i]], magnitude[:, SLOT[i + PAIRS]]
                nc.gpsimd.tensor_tensor(one, one, two, ALU.add).then_inc(added_s, 1)

            def body(b, first, last):
                for k in range(UNITS):
                    u = UNITS * b + k
                    add(u, 0)
                    add(u, 1)
                    if not (first and k == 0):
                        norm(u - 1)
                    add(u, 2)
                    add(u, 3)

            batches(pool, body)
            norm(UNITS * B - 1)

        @block.vector
        def _(dve):
            tables.wait(dve)

            def decay_step(u, k, i, first):
                g, h, kt, pair = k // HALVES, k % HALVES, i // PAIRS, i % PAIRS
                n = STEPS * u + i
                dve.wait_ge(scores, n + 1)
                if not (first and k == 0 and i < P_RING):
                    dve.wait_ge(values, n - P_RING + 1)
                    dve.wait_ge(magnitude_s, n - P_RING + 1)
                at = (h * HALF // N2 - ROWS * kt + SPAN - N1) * N2
                nc.vector.tensor_tensor(decayed[:, i % P_RING], ps[:, i % 2],
                                        decay_t[:, HG * g + 2 * pair:HG * g + 2 * pair + 2, at:at + HALF],
                                        ALU.mult).then_inc(decayed_s, 1)

            def rest(u, k, i):
                g, h = k // HALVES, k % HALVES
                if i == 0:
                    dve.wait_ge(values, STEPS * (u + 1))
                    after(dve, o_turned, u)
                    nc.vector.tensor_copy(o_sb[:], po[:]).then_inc(o_out, 1)
                if i == 4:
                    dve.wait_ge(o_turned, u + 1)
                    nc.vector.tensor_reduce(o_sum[:], px[:].rearrange("p (n d) -> p n d", d=D), AX.X, ALU.add)\
                        .then_inc(o_sum_s, 1)
                if i == 7:
                    dve.wait_ge(m_turned, u + 1)
                    fac = factor_t[:, TT * h:TT * h + TT, HG * g:HG * g + HG]
                    nc.vector.tensor_tensor(total[:], py[:].rearrange("p (t h d) -> p t h d", t=TT, d=D)[:, :, :, 0],
                                            fac, ALU.mult).then_inc(total_s, 1)
                    dve.wait_ge(total_s, u + 1)
                    nc.vector.tensor_scalar(clipped[:], total[:], 1.0, 50000.0, ALU.max, ALU.min).then_inc(clip_s, 1)
                    dve.wait_ge(clip_s, u + 1)
                    nc.vector.reciprocal(recip[:], clipped[:]).then_inc(recip_s, 1)
                    dve.wait_ge(recip_s, u + 1)
                    after(dve, normed_s, u)
                    nc.vector.tensor_tensor(scale[:], recip[:], fac, ALU.mult).then_inc(scale_s, 1)
                if i == 5:
                    dve.wait_ge(o_sum_s, u + 1)
                    nc.vector.scalar_tensor_tensor(out=centred[:], in0=o_sum[:].unsqueeze(2).broadcast_to([P, TT * HG, D]),
                                                   scalar=-1.0 / D, in1=px[:].rearrange("p (n d) -> p n d", d=D),
                                                   op0=ALU.mult, op1=ALU.add).then_inc(centred_s, 1)
                if i == 8:
                    dve.wait_ge(squared_s, u + 1)
                    nc.vector.tensor_reduce(var_sum[:], squared[:], AX.X, ALU.add).then_inc(var_s, 1)

            def add_residual(b, h, n, first):
                m = 2 * (2 * b + h) + n
                dve.wait_ge(out_s, m + 1)
                if n == 0:
                    dve.wait_ge(x_loaded[h], 16 * (b + 1))
                    after(dve, x_stored[h], 16 * b)
                bank = (py, px)[n]
                nc.vector.tensor_tensor(x_out[:, h, 2 * n:2 * n + 2], bank[:].rearrange("p (t c) -> p t c", t=2),
                                        x_res[:, h, 2 * n:2 * n + 2], ALU.add).then_inc(x_out_s, 1)

            def body(b, first, last):
                for k in range(UNITS):
                    u = UNITS * b + k
                    for i in range(STEPS):
                        decay_step(u, k, i, first)
                        if k > 0:
                            rest(u - 1, k - 1, i)
                        elif not first:
                            rest(u - 1, UNITS - 1, i)
                        if i == STEPS - 1 and k == UNITS - 1:
                            add_residual(b, 0, 0, first)
                        if i == STEPS - 1 and k == 0 and not first:
                            add_residual(b - 1, 1, 0, first)
                        if i == 1 and k == 0 and not first:
                            add_residual(b - 1, 0, 1, first)
                        if i == 1 and k == 1 and not first:
                            add_residual(b - 1, 1, 1, first)

            batches(dve, body)
            for i in range(STEPS):
                rest(UNITS * B - 1, UNITS - 1, i)
                if i == 1:
                    add_residual(B - 1, 0, 1, False)
            add_residual(B - 1, 1, 0, False)
            add_residual(B - 1, 1, 1, False)

        @block.scalar
        def _(act):
            tables.wait(act)

            def rest(u, k, i):
                g, h = k // HALVES, k % HALVES
                if i == 3:
                    act.wait_ge(row_sums, SUMS * (u + 1))
                    after(act, m_turned, u)
                    nc.scalar.activation(m_sb[:], pm[:], ACT.Copy).then_inc(m_out, 1)
                if i == 6:
                    act.wait_ge(centred_s, u + 1)
                    after(act, var_s, u)
                    nc.scalar.activation(squared[:], centred[:], ACT.Square, scale=D ** -0.5).then_inc(squared_s, 1)
                if i == 13:
                    act.wait_ge(back_s, u + 1)
                    nc.scalar.activation(gelu_t[:, g, h], px[:], ACT.Gelu, bias=gb[:, 1:2], scale=gb[:, 0:1])\
                        .then_inc(gelu_s, 1)

            def slot_free(u, k, i, first):
                before = [j for j in range(i) if SLOT[j] == SLOT[i]]
                old = before[-1] if before else max(j for j in range(STEPS) if SLOT[j] == SLOT[i])
                v = u if before else u - 1
                if not before and first and k == 0:
                    return
                if old - PAIRS in ADDED:
                    act.wait_ge(added_s, len(ADDED) * v + ADDED.index(old - PAIRS) + 1)
                else:
                    act.wait_ge(row_sums, SUMS * v + TAKEN[old])

            def body(b, first, last):
                for k in range(UNITS):
                    u = UNITS * b + k
                    for i in range(STEPS):
                        n = STEPS * u + i
                        act.wait_ge(decayed_s, n + 1)
                        slot_free(u, k, i, first)
                        nc.scalar.activation(magnitude[:, SLOT[i]], decayed[:, i % P_RING], ACT.Abs)\
                            .then_inc(magnitude_s, 1)
                        if k > 0:
                            rest(u - 1, k - 1, i)
                        elif not first:
                            rest(u - 1, UNITS - 1, i)

            batches(act, body)
            for i in range(STEPS):
                rest(UNITS * B - 1, UNITS - 1, i)

        @block.tensor
        def _(pe):
            pe.wait_ge(set_up, 3)
            tables.wait(pe)

            def score(b, k, i, first):
                g, h, kt, pair = k // HALVES, k % HALVES, i // PAIRS, i % PAIRS
                u = UNITS * b + k
                if i == 0:
                    pe.wait_ge(q_loaded[h], 64 * (2 * b + g + 1))
                    if h == 0:
                        pe.wait_ge(k_loaded[g], 80 * (b + 1))
                if not (first and k == 0 and i < 2):
                    pe.wait_ge(decayed_s, STEPS * u + i - 1)
                for j in range(2):
                    head = 2 * pair + j
                    last = nc.tensor.matmul(ps[:, i % 2, j], k_st[:, g, head, kt * P:(kt + 1) * P],
                                            q_st[:, h, head], start=True, stop=True)
                last.then_inc(scores, 1)

            def value(u, k, i, first):
                g, kt, pair = k // HALVES, i // PAIRS, i % PAIRS
                pe.wait_ge(decayed_s, STEPS * u + i + 1)
                if i == 0:
                    after(pe, o_out, u)
                for j in range(2):
                    head = 2 * pair + j
                    last = nc.tensor.matmul(po[head * D:(head + 1) * D, :], v_t[:, g, kt, head * D:(head + 1) * D],
                                            decayed[:, i % P_RING, j], start=kt == 0, stop=kt == KT - 1)
                last.then_inc(values, 1)

            def row_sum(u, i):
                pair, order = i % PAIRS, list(ROW_SUMS)
                of_pair = [j for j in order if j % PAIRS == pair]
                if i in ADDED:
                    pe.wait_ge(added_s, len(ADDED) * u + ADDED.index(i) + 1)
                else:
                    pe.wait_ge(magnitude_s, STEPS * u + i + 1)
                if i == order[0]:
                    after(pe, m_out, u)
                for j in range(2):
                    head = 2 * pair + j
                    last = nc.tensor.matmul(pm[head * D:(head + 1) * D, :], ones[:], magnitude[:, SLOT[i], j],
                                            start=i == of_pair[0], stop=i == of_pair[-1])
                last.then_inc(row_sums, 1)

            def turn(out, src):
                for t in range(TT):
                    last = nc.tensor.transpose(out[:, t * P:(t + 1) * P], src(t), idt[:])
                return last

            def rest(b, k, i):
                u = UNITS * b + k
                g, h = k // HALVES, k % HALVES
                if i == 2:
                    pe.wait_ge(o_out, u + 1)
                    after(pe, gelu_s, u)
                    after(pe, x_out_s, 4 * b + 2 * (k == UNITS - 1))
                    turn(px, lambda t: o_sb[:, t * P:(t + 1) * P]).then_inc(o_turned, 1)
                if i == 5:
                    pe.wait_ge(m_out, u + 1)
                    after(pe, scale_s, u)
                    turn(py, lambda t: m_sb[:, t * P:(t + 1) * P]).then_inc(m_turned, 1)
                if i == 12:
                    pe.wait_ge(normed_s, u + 1)
                    turn(px, lambda t: normed[:, t * HG:(t + 1) * HG].rearrange("p h d -> p (h d)"))\
                        .then_inc(back_s, 1)
                if i in (14, 15) and g == GROUPS - 1:
                    if i == 14:
                        pe.wait_ge(scale_s, u + 1)
                        pe.wait_ge(gelu_s, u + 1)
                    bank = (py, px)[i - 14]
                    for t in (2 * (i - 14), 2 * (i - 14) + 1):
                        for c in range(CC):
                            last = nc.tensor.matmul(bank[:, (t % 2) * C:(t % 2 + 1) * C],
                                                    gelu_t[:, c, h, t * P:(t + 1) * P], wo_t[:, c],
                                                    start=c == 0, stop=c == CC - 1)
                    last.then_inc(out_s, 1)

            score(0, 0, 0, True)
            score(0, 0, 1, True)

            def body(b, first, last_batch):
                for k in range(UNITS):
                    u = UNITS * b + k
                    for i in range(STEPS):
                        if i + 2 < STEPS:
                            score(b, k, i + 2, first)
                        elif k + 1 < UNITS:
                            score(b, k + 1, i + 2 - STEPS, False)
                        elif not last_batch:
                            score(b + 1, 0, i + 2 - STEPS, False)
                        value(u, k, i, first)
                        for of, at in ROW_SUMS.items():
                            if at == i:
                                row_sum(u, of)
                            if at == i + STEPS and not (first and k == 0):
                                row_sum(u - 1, of)
                        if k > 0:
                            rest(b, k - 1, i)
                        elif not first:
                            rest(b - 1, UNITS - 1, i)

            batches(pe, body)
            for of, at in ROW_SUMS.items():
                if at >= STEPS:
                    row_sum(UNITS * B - 1, of)
            for i in range(STEPS):
                rest(B - 1, UNITS - 1, i)


SLOTS = 2 * T
TILES = SLOTS // P + EXPERTS
TOKEN_TILES = T // P
HK = HID // P
ROW = C + EXPERTS


def route(nc, out, gate_w, gate_b, w1, w2, upper, ident, w1_hi, w1_lo, w2_hi, w2_lo,
          tokens, tile_expert, rows):
    JS = T // HALF
    PIECES = 2 * EXPERTS
    XR = 4
    R = 8
    PAIRS = 2 * TOKEN_TILES
    assert PIECES == JS
    with ExitStack() as ctx:
        a = Names(nc, ctx, "route")
        I32 = mybir.dt.int32
        x_in = a.sbuf("x_in", [P, XR, TT, C])
        stats = a.sbuf("stats", [P, 2, TT, 6])
        mean_var = a.sbuf("mean_var", [P, 2, TT, 2])
        rstd_in = a.sbuf("rstd_in", [P, 2, TT])
        rstd = a.sbuf("rstd", [P, 2, TT])
        power = a.sbuf("power", [P, TT])
        eps = a.sbuf("eps", [P, TT])
        xn = a.sbuf("xn", [P, 2, TT, C])
        xt = a.sbuf("xt", [P, 2, CC, HALF])
        idt = a.sbuf("ident", [P, P])
        up = a.sbuf("upper", [P, P])
        ones = a.sbuf("ones", [P, P])
        gate = a.sbuf("gate", [P, CC, EXPERTS])
        bias = a.sbuf("gate_bias", [P, EXPERTS])
        number = a.sbuf("expert_number", [P, EXPERTS])
        tile_no = a.sbuf("tile_number", [P, TILES])
        place_no = a.sbuf("place_number", [P, P])
        token_1 = a.sbuf("token_plus_1", [P, TOKEN_TILES])
        spare_1 = a.sbuf("spare_plus_1", [P, 1])
        zero = a.sbuf("zero", [P, ROW])
        wide = [P, TOKEN_TILES, EXPERTS]
        logits = a.sbuf("logits", wide)
        top = a.sbuf("top", [P, TOKEN_TILES])
        shifted = a.sbuf("shifted", wide)
        expd = a.sbuf("exp", wide)
        denom = a.sbuf("denom", [P, TOKEN_TILES])
        recip = a.sbuf("recip", [P, TOKEN_TILES])
        probs = a.sbuf("probs", wide)
        equal = a.sbuf("equal", wide)
        ranked = a.sbuf("ranked", wide)
        least = a.sbuf("least", [P, TOKEN_TILES])
        largest = a.sbuf("largest", [P, 2, TOKEN_TILES])
        chosen = [a.sbuf(f"chosen{i}", wide) for i in range(2)]
        left = a.sbuf("left", wide)
        both = a.sbuf("both", wide)
        cw = a.sbuf("weights", wide)
        total = a.sbuf("total", wide)
        scans = [a.sbuf(f"scan{i}", wide) for i in range(2)]
        small = [a.sbuf(f"small{i}", [P, EXPERTS]) for i in range(6)]
        whole = a.sbuf("whole", [P, EXPERTS], I32)
        shift = a.sbuf("shift", [P, EXPERTS], I32)
        slot_f = equal
        picked = ranked
        slot_sum = a.sbuf("slot_sum", [P, 2, TOKEN_TILES])
        slot_i = a.sbuf("slot_int", [P, 2, TOKEN_TILES], I32)
        slot_t = a.sbuf("slot_tile_int", [P, 2, TOKEN_TILES], I32)
        slot_tile = a.sbuf("slot_tile", [P, 2, TOKEN_TILES])
        slot_place = a.sbuf("slot_place", [P, 2, TOKEN_TILES])
        past = a.sbuf("past", [P, TILES, EXPERTS])
        past_sum = a.sbuf("past_sum", [P, TILES])
        past_cap = a.sbuf("past_cap", [P, TILES])
        free = x_in[:].rearrange("p r t c -> p (r t c)")
        in_place = free[:, 0:R * P].rearrange("p (r n) -> p r n", r=R)
        in_tile = free[:, R * P:R * (P + TILES)].rearrange("p (r n) -> p r n", r=R)
        group_place = a.sbuf("group_place", [P, R // 2])
        table = a.sbuf("table", [P, TILES])
        empty = a.sbuf("empty", [P, TILES])
        pt = a.psum("x_turned", [P, 2, CC, HALF])
        pl = a.psum("logit_acc", [P, 2, HALF])
        pr = a.psum("rank", [P, HALF])
        pc = a.psum("counts", [P, HALF])
        p_table = pl[:, 0, 0:TILES]

        consts, set_up = a.sem("consts_loaded"), a.sem("set_up")
        x_loaded = [a.sem(f"x_loaded{i}") for i in range(XR)]
        w_loaded = [a.sem(f"w_loaded{i}") for i in range(2)]
        stats_done, moments_done, eps_added, rstd_ready = (
            a.sem(n) for n in ("stats_done", "moments_done", "eps_added", "rstd_ready"))
        xn_ready, xt_acc, xt_ready = a.sem("xn_ready"), a.sem("xt_turned"), a.sem("xt_ready")
        xn_stored = [a.sem(f"xn_stored{i}") for i in range(2)]
        spare_stored, cw_stored = a.sem("spare_stored"), a.sem("cw_stored")
        logit_acc, logit_ready = a.sem("logit_acc"), a.sem("logit_ready")
        w_hi_s, w_lo_s = a.sem("w_hi_ready"), a.sem("w_lo_ready")
        chain, exp_s, counted = a.sem("chain"), a.sem("exp_ready"), a.sem("counted")
        both_s, cw_s, slots_s = a.sem("both_ready"), a.sem("weights_ready"), a.sem("slots_ready")
        in_tile_s, even_s, odd_s = a.sem("in_tile_ready"), a.sem("even_place_ready"), a.sem("odd_place_ready")
        added_s, table_s, passed = a.sem("pairs_added"), a.sem("table_chain"), a.sem("waits_passed")
        place_s = a.sem("group_place_ready")

        xv = out[0:T].rearrange("(n t p) c -> n p t c", p=P, t=TT)
        xnv = rows[0:T].rearrange("(n t p) c -> n p t c", p=P, t=TT)
        w1v = w1.rearrange("e (k p) n -> e p k n", p=P)
        w2v = w2.rearrange("e (k p) n -> e p k n", p=P)
        weights = [(w1v, w1_hi, w1_lo), (w2v, w2_hi, w2_lo)]
        SET_UP = 9
        block = ctx.enter_context(nc.Block())

        @block.sync
        def _(sp):
            def load_w(j):
                src, _, lo = weights[j % 2]
                sp.dma_start(lo[:, j // 2].bitcast(F32), src[j // 2]).then_inc(w_loaded[j % 2], 16)

            for j in range(2):
                sp.dma_start(x_in[:, j], xv[j]).then_inc(x_loaded[j], 16)
            sp.dma_start(idt[:], ident).then_inc(consts, 16)
            sp.dma_start(up[:], upper).then_inc(consts, 16)
            sp.dma_start(gate[:], gate_w.rearrange("(k p) e -> p k e", p=P)).then_inc(consts, 16)
            sp.dma_start(bias[:], gate_b.partition_broadcast(P)).then_inc(consts, 16)
            for j in range(2, XR):
                sp.dma_start(x_in[:, j], xv[j]).then_inc(x_loaded[j], 16)
            load_w(0)
            load_w(1)
            for j in range(JS):
                h = j % 2
                sp.wait_ge(xn_ready, j + 1)
                sp.dma_start(xnv[j][:, :, 0:C], xn[:, h]).then_inc(xn_stored[h], 16)
                if j + XR < JS:
                    sp.dma_start(x_in[:, j % XR], xv[j + XR]).then_inc(x_loaded[j % XR], 16)
                if j + 2 < JS:
                    sp.wait_ge(w_hi_s, j + 1)
                    load_w(j + 2)
            sp.wait_ge(set_up, SET_UP)
            sp.dma_start(rows[T:T + P], zero[:]).then_inc(spare_stored, 16)
            sp.dma_start(out[T:T + P], zero[:, 0:C]).then_inc(spare_stored, 16)
            sp.wait_ge(cw_s, 1)
            sp.dma_start(rows[0:T, C:ROW].rearrange("(t p) e -> p t e", p=P), cw[:]).then_inc(cw_stored, 16)
            for h in range(2):
                sp.wait_ge(xn_stored[h], 16 * JS // 2)
            sp.wait_ge(spare_stored, 32)
            sp.wait_ge(cw_stored, 16)

        def groups(engine, body):
            body(0, True)
            with engine.Fori(1, PAIRS // R - 1) as q:
                body(q, False)
            body(PAIRS // R - 1, False)

        def column(ap, t):
            return ap[:, t:t + 1] if isinstance(t, int) else ap[:, bass.ds(t, 1)]

        @block.gpsimd
        def _(pool):
            count_up = dict(allow_small_or_imprecise_dtypes=True)
            nc.gpsimd.memset(power[:], -0.5).then_inc(set_up, 1)
            nc.gpsimd.memset(eps[:], 1e-5).then_inc(set_up, 1)
            nc.gpsimd.memset(ones[:], 1.0).then_inc(set_up, 1)
            nc.gpsimd.memset(zero[:], 0.0).then_inc(set_up, 1)
            nc.gpsimd.iota(number[:], [[1, EXPERTS]], base=-EXPERTS, channel_multiplier=0, **count_up).then_inc(set_up, 1)
            nc.gpsimd.iota(tile_no[:], [[1, TILES]], base=0, channel_multiplier=0, **count_up).then_inc(set_up, 1)
            nc.gpsimd.iota(place_no[:], [[1, P]], base=0, channel_multiplier=0, **count_up).then_inc(set_up, 1)
            nc.gpsimd.iota(token_1[:], [[P, TOKEN_TILES]], base=1, channel_multiplier=1, **count_up).then_inc(set_up, 1)
            nc.gpsimd.iota(spare_1[:], [[1, 1]], base=T + 1, channel_multiplier=1, **count_up).then_inc(set_up, 1)
            pool.wait_ge(set_up, SET_UP)

            def low_weights(j):
                _, hi, lo = weights[j % 2]
                pool.wait_ge(w_hi_s, j + 1)
                nc.gpsimd.tensor_tensor(lo[:, j // 2], lo[:, j // 2].bitcast(F32), hi[:, j // 2].bitcast(F32),
                                        ALU.subtract).then_inc(w_lo_s, 1)

            for j in range(JS):
                h = j % 2
                pool.wait_ge(moments_done, j + 1)
                after(pool, rstd_ready, j - 1)
                nc.gpsimd.tensor_tensor(rstd_in[:, h], mean_var[:, h, :, 1], eps[:], ALU.add).then_inc(eps_added, 1)
                pool.wait_ge(eps_added, j + 1)
                after(pool, xn_ready, j - 1)
                nc.gpsimd.tensor_tensor(rstd[:, h], rstd_in[:, h], power[:], ALU.pow).then_inc(rstd_ready, 1)
                if j > 0:
                    low_weights(j - 1)
            low_weights(JS - 1)
            pool.wait_ge(slots_s, 1)

            def body(q, first):
                if not first:
                    pool.wait_ge(odd_s, (R // 2) * q)
                pool.sem_inc(passed, 1)
                at = slice((R // 2) * q, (R // 2) * (q + 1)) if isinstance(q, int) else bass.ds((R // 2) * q, R // 2)
                nc.gpsimd.tensor_copy(group_place[:], slot_place[:, 1, at]).then_inc(place_s, 1)
                pool.wait_ge(place_s, q + 1)
                for k in range(1, R, 2):
                    if not first:
                        pool.wait_ge(added_s, R * (q - 1) + k + 1)
                    pool.sem_inc(passed, 1)
                    nc.gpsimd.tensor_scalar(in_place[:, k], place_no[:], group_place[:, k // 2:k // 2 + 1],
                                            None, ALU.is_equal).then_inc(odd_s, 1)

            groups(pool, body)

        @block.scalar
        def _(act):
            for j in range(JS):
                h = j % 2
                _, hi, lo = weights[h]
                act.wait_ge(xt_acc, j + 1)
                after(act, logit_acc, j - 1)
                nc.scalar.activation(xt[:, h], pt[:, h], ACT.Copy).then_inc(xt_ready, 1)
                act.wait_ge(w_loaded[h], 16 * (j // 2 + 1))
                nc.scalar.activation(hi[:, j // 2], lo[:, j // 2].bitcast(F32), ACT.Copy).then_inc(w_hi_s, 1)
            act.wait_ge(chain, 2)
            nc.scalar.activation(expd[:], shifted[:], ACT.Exp).then_inc(exp_s, 1)

        @block.tensor
        def _(pe):
            pe.wait_ge(consts, 64)

            def logit(j):
                h = j % 2
                pe.wait_ge(xt_ready, j + 1)
                after(pe, logit_ready, j - 1)
                for t in range(TT):
                    for c in range(CC):
                        last = nc.tensor.matmul(pl[:, h, t * EXPERTS:(t + 1) * EXPERTS],
                                                xt[:, h, c, t * P:(t + 1) * P], gate[:, c],
                                                start=c == 0, stop=c == CC - 1)
                last.then_inc(logit_acc, 1)

            for j in range(JS):
                h = j % 2
                pe.wait_ge(xn_ready, j + 1)
                after(pe, xt_ready, j - 1)
                for c in range(CC):
                    for t in range(TT):
                        last = nc.tensor.transpose(pt[:, h, c, t * P:(t + 1) * P], xn[:, h, t, c * P:(c + 1) * P], idt[:])
                last.then_inc(xt_acc, 1)
                if j:
                    logit(j - 1)
            logit(JS - 1)
            pe.wait_ge(both_s, 1)
            pe.wait_ge(set_up, SET_UP)
            flat = both[:].rearrange("p t e -> p (t e)")
            nc.tensor.matmul(pr[:], up[:], flat, start=True, stop=True)
            nc.tensor.matmul(pc[:], ones[:], flat, start=True, stop=True).then_inc(counted, 1)

            def body(q, first):
                for k in range(R):
                    pe.wait_ge(in_tile_s, R * q + k + 1)
                    pe.wait_ge((even_s, odd_s)[k % 2], (R // 2) * q + k // 2 + 1)
                    nc.tensor.matmul(p_table, in_place[:, k], in_tile[:, k], start=first and k == 0,
                                     stop=isinstance(q, int) and q == PAIRS // R - 1 and k == R - 1)\
                        .then_inc(added_s, 1)

            groups(pe, body)

        @block.vector
        def _(dve):
            def stage1(j):
                h = j % 2
                dve.wait_ge(x_loaded[j % XR], 16 * (j // XR + 1))
                after(dve, moments_done, j - 1)
                for t in range(TT):
                    last = nc.vector.bn_stats(stats[:, h, t], x_in[:, j % XR, t])
                last.then_inc(stats_done, 1)
                dve.wait_ge(stats_done, j + 1)
                after(dve, xn_ready, j - 1)
                after(dve, eps_added, j - 1)
                for t in range(TT):
                    last = nc.vector.bn_aggr(mean_var[:, h, t], stats[:, h, t])
                last.then_inc(moments_done, 1)

            def stage2(j):
                h = j % 2
                dve.wait_ge(rstd_ready, j + 1)
                if j >= 2:
                    dve.wait_ge(xt_acc, j - 1)
                    dve.wait_ge(xn_stored[h], 16 * (j // 2))
                for t in range(TT):
                    last = nc.vector.tensor_scalar(xn[:, h, t], x_in[:, j % XR, t], mean_var[:, h, t, 0:1],
                                                   rstd[:, h, t:t + 1], ALU.subtract, ALU.mult)
                last.then_inc(xn_ready, 1)

            def stage3(j):
                h = j % 2
                dve.wait_ge(logit_acc, j + 1)
                nc.vector.tensor_tensor(logits[:, j * TT:(j + 1) * TT],
                                        pl[:, h, 0:TT * EXPERTS].rearrange("p (t e) -> p t e", t=TT),
                                        bias[:].unsqueeze(1).broadcast_to([P, TT, EXPERTS]), ALU.add)\
                    .then_inc(logit_ready, 1)

            dve.wait_ge(consts, 64)
            dve.wait_ge(set_up, SET_UP)
            stage1(0)
            for j in range(JS):
                if j + 1 < JS:
                    stage1(j + 1)
                stage2(j)
                if j >= 2:
                    stage3(j - 2)
            stage3(JS - 2)
            stage3(JS - 1)
            dve.wait_ge(logit_ready, JS)

            count = [0]

            def link(ins):
                count[0] += 1
                ins.then_inc(chain, 1)
                dve.wait_ge(chain, count[0])

            spread = lambda y: y[:].unsqueeze(2).broadcast_to(wide)
            over = lambda y: y[:].unsqueeze(1).broadcast_to(wide)
            V = nc.vector
            link(V.tensor_reduce(top[:], logits[:], AX.X, ALU.max))
            link(V.tensor_tensor(shifted[:], logits[:], spread(top), ALU.subtract))
            dve.wait_ge(exp_s, 1)
            link(V.tensor_reduce(denom[:], expd[:], AX.X, ALU.add))
            link(V.reciprocal(recip[:], denom[:]))
            link(V.tensor_tensor(probs[:], expd[:], spread(recip), ALU.mult))
            rest = probs
            for n in range(2):
                link(V.tensor_reduce(largest[:, n], rest[:], AX.X, ALU.max))
                link(V.tensor_tensor(equal[:], rest[:], largest[:, n].unsqueeze(2).broadcast_to(wide), ALU.is_equal))
                link(V.tensor_tensor(ranked[:], equal[:], over(number), ALU.mult))
                link(V.tensor_reduce(least[:], ranked[:], AX.X, ALU.min))
                link(V.tensor_tensor(chosen[n][:], over(number), spread(least), ALU.is_equal))
                if n == 0:
                    link(V.scalar_tensor_tensor(out=left[:], in0=chosen[0][:], scalar=-4.0, in1=probs[:],
                                                op0=ALU.mult, op1=ALU.add))
                    rest = left
            V.tensor_tensor(both[:], chosen[0][:], chosen[1][:], ALU.add).then_inc(both_s, 1)
            dve.wait_ge(both_s, 1)
            V.tensor_tensor(cw[:], probs[:], both[:], ALU.mult).then_inc(cw_s, 1)
            dve.wait_ge(counted, 1)
            flat = lambda y: y[:].rearrange("p t e -> p (t e)")
            link(V.tensor_copy(flat(total), pc[:]))
            link(V.tensor_copy(flat(scans[0]), pc[:]))
            at, step = 0, 1
            while step < TOKEN_TILES:
                src, dst = scans[at], scans[1 - at]
                V.tensor_copy(dst[:, 0:step], src[:, 0:step])
                link(V.tensor_tensor(dst[:, step:], src[:, step:], src[:, 0:TOKEN_TILES - step], ALU.add))
                at, step = 1 - at, 2 * step
            running = scans[at]
            counts = running[:, TOKEN_TILES - 1]
            link(V.tensor_scalar(whole[:], counts, float(P - 1), None, ALU.add))
            link(V.tensor_scalar(shift[:], whole[:], P.bit_length() - 1, None, ALU.logical_shift_right))
            link(V.tensor_copy(small[0][:], shift[:]))
            link(V.tensor_copy(small[1][:], small[0][:]))
            now, step = 1, 1
            while step < EXPERTS:
                src, dst = small[now], small[now + 1]
                V.tensor_copy(dst[:, 0:step], src[:, 0:step])
                link(V.tensor_tensor(dst[:, step:], src[:, step:], src[:, 0:EXPERTS - step], ALU.add))
                now, step = now + 1, 2 * step
            ends, starts = small[now], small[now + 1]
            link(V.tensor_tensor(starts[:], ends[:], small[0][:], ALU.subtract))
            link(V.scalar_tensor_tensor(out=slot_f[:], in0=over(starts), scalar=float(P), in1=running[:],
                                        op0=ALU.mult, op1=ALU.add))
            link(V.tensor_tensor(picked[:], slot_f[:], total[:], ALU.subtract))
            link(V.tensor_tensor(flat(slot_f), flat(picked), pr[:], ALU.add))
            for n in range(2):
                link(V.tensor_tensor(picked[:], slot_f[:], chosen[n][:], ALU.mult))
                link(V.tensor_reduce(slot_sum[:, n], picked[:], AX.X, ALU.add))
            link(V.tensor_copy(slot_i[:], slot_sum[:]))
            link(V.tensor_scalar(slot_t[:], slot_i[:], P.bit_length() - 1, None, ALU.logical_shift_right))
            link(V.tensor_copy(slot_tile[:], slot_t[:]))
            link(V.scalar_tensor_tensor(out=slot_place[:], in0=slot_tile[:], scalar=-float(P), in1=slot_sum[:],
                                        op0=ALU.mult, op1=ALU.add))
            link(V.tensor_tensor(past[:], tile_no[:].unsqueeze(2).broadcast_to([P, TILES, EXPERTS]),
                                 ends[:].unsqueeze(1).broadcast_to([P, TILES, EXPERTS]), ALU.is_ge))
            V.tensor_reduce(past_sum[:], past[:], AX.X, ALU.add).then_inc(slots_s, 1)
            dve.wait_ge(slots_s, 1)
            link(V.tensor_scalar(past_cap[:], past_sum[:], float(EXPERTS - 1), None, ALU.min))
            V.tensor_copy(tile_expert[:], past_cap[:])

            def body(q, first):
                for k in range(R):
                    t = (R // 2) * q + k // 2
                    if not first:
                        dve.wait_ge(added_s, R * (q - 1) + k + 1)
                    if k % 2 == 0:
                        nc.vector.tensor_scalar(in_place[:, k], place_no[:], column(slot_place[:, 0], t), None,
                                                ALU.is_equal).then_inc(even_s, 1)
                    nc.vector.tensor_scalar(in_tile[:, k], tile_no[:], column(slot_tile[:, k % 2], t),
                                            column(token_1, t), ALU.is_equal, ALU.mult).then_inc(in_tile_s, 1)

            groups(dve, body)
            dve.wait_ge(added_s, PAIRS)
            nc.vector.tensor_copy(table[:], p_table).then_inc(table_s, 1)
            dve.wait_ge(table_s, 1)
            nc.vector.tensor_scalar(empty[:], table[:], 0.0, spare_1[:], ALU.is_equal, ALU.mult).then_inc(table_s, 1)
            dve.wait_ge(table_s, 2)
            nc.vector.scalar_tensor_tensor(out=past_sum[:], in0=table[:], scalar=-1.0, in1=empty[:],
                                           op0=ALU.add, op1=ALU.add).then_inc(table_s, 1)
            dve.wait_ge(table_s, 3)
            nc.vector.tensor_copy(tokens[:], past_sum[:])


def experts(nc, b1, b2, ident, w1_hi, w1_lo, w2_hi, w2_lo, tokens, tile_expert, rows, out):
    R, AHEAD = 8, 5
    ROUNDS = TILES // R
    assert TILES % R == 0
    with ExitStack() as ctx:
        a = Names(nc, ctx, "exp")
        U32 = mybir.dt.uint32
        idt = a.sbuf("ident", [P, P])
        b1_t = a.sbuf("b1", [P, EXPERTS, HID])
        b2_t = a.sbuf("b2", [P, EXPERTS, C])
        source = a.sbuf("source", [P, R, 1], U32)
        target = a.sbuf("target", [P, R, 1], U32)
        x_in = a.sbuf("x_in", [P, R, ROW])
        x_hi = a.sbuf("x_hi", [P, 2, CC, P], F32R)
        x_lo = a.sbuf("x_lo", [P, 2, CC, P], F32R)
        pre = a.sbuf("pre", [P, 2, HID])
        act_t = a.sbuf("gelu", [P, 2, HID])
        h_hi = a.sbuf("h_hi", [P, 2, HK, P], F32R)
        h_lo = a.sbuf("h_lo", [P, 2, HK, P], F32R)
        y_sum = a.sbuf("y_sum", [P, 2, C])
        y = a.sbuf("y", [P, 2, C])
        px = a.psum("x_turned", [P, HALF])[:, 0:CC * P].rearrange("p (k n) -> p k n", k=CC)
        ph = a.psum("hidden", [P, 2, HID])
        pt = a.psum("hidden_turned", [P, 2, HK, P])
        py = a.psum("y_acc", [P, 2, HALF])
        consts = a.sem("consts_loaded")
        x_loaded = [a.sem(f"x_gathered{i}") for i in range(R)]
        source_s, target_s, passed = a.sem("source_ready"), a.sem("target_ready"), a.sem("waits_passed")
        x_turned, x_hi_s, x_lo_s = a.sem("x_turned"), a.sem("x_hi_ready"), a.sem("x_lo_ready")
        hidden, pre_s, gelu_s = a.sem("hidden"), a.sem("pre_ready"), a.sem("gelu_ready")
        h_turned, h_hi_s, h_lo_s = a.sem("h_turned"), a.sem("h_hi_ready"), a.sem("h_lo_ready")
        y_acc, y_sum_s, y_s, added = a.sem("y_acc"), a.sem("y_sum_ready"), a.sem("y_ready"), a.sem("y_added")

        def over_tiles(engine, body):
            for i in range(R):
                body(i, i, 0)
            with engine.Fori(1, ROUNDS - 1) as r:
                for k in range(R):
                    body(R * r + k, k, r)
            for i in range(TILES - R, TILES + 2):
                body(i, i % R, i // R)

        def exists(i):
            return not isinstance(i, int) or 0 <= i < TILES

        def column(ap, i):
            return ap[:, i:i + 1] if isinstance(i, int) else ap[:, bass.ds(i, 1)]

        def expert_of(engine, i):
            return engine.value_load(column(tile_expert[0:1], i), min_val=0, max_val=EXPERTS - 1)

        def earlier_expert(engine, i, k, experts):
            return experts[k - 2] if k >= 2 else expert_of(engine, i - 2)

        block = ctx.enter_context(nc.Block())

        @block.sync
        def _(sp):
            sp.dma_start(idt[:], ident).then_inc(consts, 16)
            sp.dma_start(b1_t[:], b1.partition_broadcast(P)).then_inc(consts, 16)
            sp.dma_start(b2_t[:], b2.partition_broadcast(P)).then_inc(consts, 16)

        @block.gpsimd
        def _(pool):
            def gather(i, k):
                after(pool, y_s, i - R + 1)
                pool.sem_inc(passed, 1)
                nc.gpsimd.tensor_copy(source[:, k], column(tokens, i)).then_inc(source_s, 1)
                pool.wait_ge(source_s, i + 1)
                pool.sem_inc(passed, 1)
                nc.gpsimd.indirect_dma_start(x_in[:, k], None, rows, bass.IndirectOffsetOnAxis(source[:, k], 0))\
                    .then_inc(x_loaded[k], 16)

            for i in range(AHEAD):
                gather(i, i)

            def body(i, k, r):
                if exists(i + AHEAD):
                    gather(i + AHEAD, (k + AHEAD) % R)
                if exists(i - 2):
                    o = (k - 2) % R
                    after(pool, added, 16 * (i - 2))
                    pool.sem_inc(passed, 1)
                    nc.gpsimd.tensor_copy(target[:, o], column(tokens, i - 2)).then_inc(target_s, 1)
                    pool.wait_ge(target_s, i - 1)
                    pool.wait_ge(y_s, i - 1)
                    pool.sem_inc(passed, 1)
                    nc.gpsimd.indirect_dma_start(out, bass.IndirectOffsetOnAxis(target[:, o], 0), y[:, k % 2], None,
                                                 compute_op=ALU.add).then_inc(added, 16)

            over_tiles(pool, body)
            pool.wait_ge(added, 16 * TILES)

        @block.tensor
        def _(pe):
            def turn_x(i, k, r):
                pe.wait_ge(x_loaded[k], 16 * r + 16)
                after(pe, x_lo_s, i)
                for c in range(CC):
                    last = nc.tensor.transpose(px[:, c], x_in[:, k, c * P:(c + 1) * P], idt[:])
                last.then_inc(x_turned, 1)

            def three(out, xs, ws, e, chunks, s):
                n, steps = 0, 3 * chunks
                for k in range(chunks):
                    for w, xx in ((ws[0], xs[0]), (ws[0], xs[1]), (ws[1], xs[0])):
                        last = nc.tensor.matmul(out, xx[:, s, k], w[:, bass.ds(e, 1), k].rearrange("p o n -> p (o n)"),
                                                start=n == 0, stop=n == steps - 1)
                        n += 1
                return last

            pe.wait_ge(consts, 48)
            turn_x(0, 0, 0)

            es = {}

            def body(i, k, r):
                s = k % 2
                if exists(i):
                    e = es[k] = expert_of(pe, i)
                    pe.wait_ge(x_lo_s, i + 1)
                    after(pe, pre_s, i - 1)
                    three(ph[:, s], (x_hi, x_lo), (w1_hi, w1_lo), e, CC, s).then_inc(hidden, 1)
                if exists(i + 1):
                    turn_x(i + 1, (k + 1) % R, r + (k + 1) // R)
                if exists(i - 1):
                    pe.wait_ge(gelu_s, i)
                    after(pe, h_lo_s, i - 2)
                    for c in range(HK):
                        last = nc.tensor.transpose(pt[:, 1 - s, c], act_t[:, 1 - s, c * P:(c + 1) * P], idt[:])
                    last.then_inc(h_turned, 1)
                if exists(i - 2):
                    e = earlier_expert(pe, i, k, es)
                    pe.wait_ge(h_lo_s, i - 1)
                    after(pe, y_sum_s, i - 3)
                    three(py[:, s, 0:C], (h_hi, h_lo), (w2_hi, w2_lo), e, HK, s).then_inc(y_acc, 1)

            over_tiles(pe, body)

        @block.scalar
        def _(act):
            def x_high(i, s):
                act.wait_ge(x_turned, i + 1)
                after(act, hidden, i - 1)
                nc.scalar.activation(x_hi[:, s], px, ACT.Copy).then_inc(x_hi_s, 1)

            x_high(0, 0)

            def body(i, k, r):
                s = k % 2
                if exists(i + 1):
                    x_high(i + 1, 1 - s)
                if exists(i - 1):
                    act.wait_ge(h_turned, i)
                    after(act, y_acc, i - 3)
                    nc.scalar.activation(h_hi[:, 1 - s], pt[:, 1 - s], ACT.Copy).then_inc(h_hi_s, 1)
                if exists(i):
                    act.wait_ge(pre_s, i + 1)
                    after(act, h_turned, i - 1)
                    nc.scalar.activation(act_t[:, s], pre[:, s], ACT.Gelu).then_inc(gelu_s, 1)
                if exists(i - 2):
                    e = expert_of(act, i - 2)
                    act.wait_ge(y_sum_s, i - 1)
                    after(act, added, 16 * (i - 3))
                    nc.scalar.activation(y[:, s], y_sum[:, s], ACT.Copy,
                                         scale=x_in[:, (k - 2) % R, bass.ds(e + C, 1)]).then_inc(y_s, 1)

            over_tiles(act, body)

        @block.vector
        def _(dve):
            def x_low(i, s):
                dve.wait_ge(x_hi_s, i + 1)
                nc.vector.tensor_tensor(x_lo[:, s], px, x_hi[:, s].bitcast(F32), ALU.subtract).then_inc(x_lo_s, 1)

            dve.wait_ge(consts, 48)
            x_low(0, 0)

            es = {}

            def body(i, k, r):
                s = k % 2
                if exists(i + 1):
                    x_low(i + 1, 1 - s)
                if exists(i - 1):
                    dve.wait_ge(h_hi_s, i)
                    nc.vector.tensor_tensor(h_lo[:, 1 - s], pt[:, 1 - s], h_hi[:, 1 - s].bitcast(F32), ALU.subtract)\
                        .then_inc(h_lo_s, 1)
                if exists(i):
                    e = es[k] = expert_of(dve, i)
                    dve.wait_ge(hidden, i + 1)
                    after(dve, gelu_s, i - 1)
                    nc.vector.tensor_tensor(pre[:, s], ph[:, s], b1_t[:, bass.ds(e, 1)].rearrange("p o n -> p (o n)"),
                                            ALU.add).then_inc(pre_s, 1)
                if exists(i - 2):
                    e = earlier_expert(dve, i, k, es)
                    dve.wait_ge(y_acc, i - 1)
                    after(dve, y_s, i - 3)
                    nc.vector.tensor_tensor(y_sum[:, s], py[:, s, 0:C],
                                            b2_t[:, bass.ds(e, 1)].rearrange("p o n -> p (o n)"), ALU.add)\
                        .then_inc(y_sum_s, 1)

            over_tiles(dve, body)


def shape_constants():
    f = np.float32
    half = f(1.0) / (f(10000.0) ** np.linspace(0.0, 1.0, D // 2, dtype=f))
    angle = np.repeat(half, 2)
    index = (np.arange(N1, dtype=f)[:, None] + np.arange(N2, dtype=f)[None, :]).reshape(L)
    phase = (index[:, None] * angle[None, :]).astype(f)
    sign = np.where(np.arange(D) % 2 == 0, f(-1), f(1))
    cos = np.tile(np.cos(phase).astype(f).T, (HG, 1))
    sin = np.tile((np.sin(phase).astype(f) * sign).T, (HG, 1))
    decay = np.log(f(1.0) - f(2.0) ** (f(-2.0) - f(5.0) * np.arange(H, dtype=f) / f(H))).astype(f)
    row, col = np.divmod(np.arange(P), N2)
    rows_apart = np.abs(np.arange(SPAN)[None, :] - (SPAN - N1) - row[:, None])
    cols_apart = np.abs(np.arange(N2)[None, :] - col[:, None])
    apart = (rows_apart[:, None, :, None] + cols_apart[:, None, None, :]).astype(f)
    table = np.exp(apart * decay[None, :, None, None]).astype(f)
    line = np.exp(np.abs(np.arange(N1)[:, None] - np.arange(N1)[None, :]).astype(f) * decay[:, None, None])
    sums = line.astype(np.float64).sum(-1)
    total = (sums[:, :, None] * sums[:, None, :]).reshape(H, L)
    factor = (D ** -0.5 / np.sqrt(total)).astype(f)
    factor = factor.reshape(H, KT, P).transpose(2, 1, 0)
    return {"cos": cos, "sin": sin, "decay": table.reshape(P, H, SPAN * N2),
            "factor": np.ascontiguousarray(factor), "ident": np.eye(P, dtype=f),
            "upper": np.triu(np.ones((P, P), dtype=f), 1)}


def block_program(nc, io):
    scratch = lambda name, shape: nc.dram_tensor(name, shape, F32).ap()
    parts = [scratch(n, (B, C, L)) for n in ("q_hi", "q_lo", "k_hi", "k_lo")]
    v = scratch("v_rows", (T, C))
    rows = scratch("token_rows", (T + P, ROW))
    out = io["out"]
    with ExitStack() as ctx:
        tables = RetainConstants(nc, ctx)
        project(nc, io, tables, *parts, v)
        retain(nc, io["x"], tables, *parts, v, out[0:T])
    with ExitStack() as ctx:
        a = Names(nc, ctx, "moe")
        w1p = [a.sbuf(f"w1_{n}", [P, EXPERTS, CC, HID], F32R) for n in ("hi", "lo")]
        w2p = [a.sbuf(f"w2_{n}", [P, EXPERTS, HK, C], F32R) for n in ("hi", "lo")]
        tokens = a.sbuf("tokens", [P, TILES], mybir.dt.uint32)
        tile_expert = a.sbuf("tile_expert", [P, TILES], mybir.dt.int32)
        route(nc, out, io["gate_w"], io["gate_b"], io["w1"], io["w2"], io["upper"], io["ident"],
              *w1p, *w2p, tokens, tile_expert, rows)
        experts(nc, io["b1"], io["b2"], io["ident"], *w1p, *w2p, tokens, tile_expert, rows, out)


def kernel(x, L0_conv_Wq, L0_conv_Wk, L0_conv_Wv, L0_conv_Wo, L0_conv_ln_g, L0_conv_ln_b,
           L0_ffn_gate_w, L0_ffn_gate_b, L0_ffn_W1, L0_ffn_b1, L0_ffn_W2, L0_ffn_b2):
    import concourse.bacc as bacc
    from concourse.bass_utils import run_bass_kernel_spmd

    turned = lambda w: np.ascontiguousarray(np.asarray(w).T)
    arrays = {
        "x": np.ascontiguousarray(np.asarray(x)).reshape(T, C),
        "wq": turned(L0_conv_Wq), "wk": turned(L0_conv_Wk), "wv": turned(L0_conv_Wv), "wo": turned(L0_conv_Wo),
        "ln_g": np.asarray(L0_conv_ln_g), "ln_b": np.asarray(L0_conv_ln_b),
        "gate_w": np.asarray(L0_ffn_gate_w), "gate_b": np.asarray(L0_ffn_gate_b),
        "w1": np.asarray(L0_ffn_W1), "b1": np.asarray(L0_ffn_b1),
        "w2": np.asarray(L0_ffn_W2), "b2": np.asarray(L0_ffn_b2),
        **shape_constants(),
    }
    nc = bacc.Bacc("TRN2", target_bir_lowering=False, num_devices=1)
    io = {n: nc.dram_tensor(n, a.shape, mybir.dt.from_np(a.dtype), kind="ExternalInput").ap()
          for n, a in arrays.items()}
    io["out"] = nc.dram_tensor("out", (T + P, C), F32, kind="ExternalOutput").ap()
    block_program(nc, io)
    result = run_bass_kernel_spmd(nc, [arrays], core_ids=[0])
    return result.results[0]["out"][:T].reshape(B, N1, N2, C)
```

```python
from contextlib import ExitStack

import numpy as np

import concourse.bass as bass
from concourse import mybir
from concourse.alu_op_type import AluOpType as ALU

F32 = mybir.dt.float32
F32R = mybir.dt.float32r
ACT = mybir.ActivationFunctionType
AX = mybir.AxisListType

B, N1, N2, C = 8, 32, 32, 256
L = N1 * N2
H, D = 8, C // 8
T = B * L
P = 128
HALF = 512
CC = C // P
HG = P // D
TT = HALF // P
ROWS = P // N2
KT = L // P
SPAN = N1 + (KT - 1) * ROWS
EXPERTS, HID = 8, 512
SWAP = [i ^ 1 for i in range(D)]


def after(engine, semaphore, value):
    if not (isinstance(value, int) and value <= 0):
        engine.wait_ge(semaphore, value)


def over_batches(engine, body):
    body(0, True, False)
    with engine.Fori(1, B - 2) as b:
        body(b, False, False)
    body(B - 2, False, False)
    body(B - 1, False, True)


class Names:

    def __init__(self, nc, ctx, phase):
        self.nc, self.ctx, self.phase = nc, ctx, phase

    def sbuf(self, name, shape, dtype=F32):
        return self.ctx.enter_context(self.nc.sbuf_tensor(f"{self.phase}_{name}", shape, dtype))

    def psum(self, name, shape):
        return self.ctx.enter_context(self.nc.psum_tensor(f"{self.phase}_{name}", shape, F32))

    def sem(self, name):
        return self.ctx.enter_context(self.nc.semaphore(f"{self.phase}_{name}"))


class RetainConstants:

    def __init__(self, nc, ctx):
        a = Names(nc, ctx, "tables")
        self.decay = a.sbuf("decay", [P, H, SPAN * N2])
        self.factor = a.sbuf("factor", [P, KT, H])
        self.ident = a.sbuf("ident", [P, P])
        self.wo = a.sbuf("wo", [P, CC, C])
        self.gain_bias = a.sbuf("gain_bias", [P, 2])
        self.small_loaded, self.decay_loaded = a.sem("small_loaded"), a.sem("decay_loaded")
        self.SMALL, self.DECAY = 16 * (3 + 2 * HG), 16 * H

    def load_small(self, sp, io):
        for dst, src in ((self.factor, io["factor"]), (self.ident, io["ident"])):
            sp.dma_start(dst[:], src).then_inc(self.small_loaded, 16)
        sp.dma_start(self.wo[:], io["wo"].rearrange("(k p) c -> p k c", p=P)).then_inc(self.small_loaded, 16)
        for n, y in enumerate((io["ln_g"], io["ln_b"])):
            for h in range(HG):
                sp.dma_start(self.gain_bias[h * D:(h + 1) * D, n:n + 1], y.rearrange("(d o) -> d o", o=1))\
                    .then_inc(self.small_loaded, 16)

    def load_decay(self, sp, io, h):
        at = slice(h, h + 1) if isinstance(h, int) else bass.ds(h, 1)
        sp.dma_start(self.decay[:, at], io["decay"][:, at]).then_inc(self.decay_loaded, 16)

    def wait(self, engine):
        engine.wait_ge(self.small_loaded, self.SMALL)
        engine.wait_ge(self.decay_loaded, self.DECAY)


def of_batch(ap, b, rest, names):
    if isinstance(b, int):
        return ap[(b, *rest)]
    inner = names.split()
    return ap[(bass.ds(b, 1), *rest)].rearrange(f"o {names} -> (o {inner[0]}) {' '.join(inner[1:])}")


class Operands:

    def __init__(self, nc, ctx, q_hi, q_lo, k_hi, k_lo, v):
        self.names = Names(nc, ctx, "operands")
        split = lambda y: y.rearrange("b (g h d) l -> b g d h l", d=D, h=HG)
        self.q_src = [split(y) for y in (q_hi, q_lo, q_hi, q_lo)]
        self.k_src = [split(y) for y in (k_hi, k_hi, k_lo, k_lo)]
        self.v_src = v.rearrange("(b k p) c -> b p k c", p=P, k=KT)
        self.q, self.k, self.v, self.q_loaded, self.k_loaded, self.v_loaded = ([] for _ in range(6))
        self.allocate(self.names)

    def allocate(self, a):
        n = len(self.q)
        self.q.append(a.sbuf(f"q{n}", [P, HG, HALF], F32R))
        self.k.append(a.sbuf(f"k{n}", [P, HG, L], F32R))
        self.v.append(a.sbuf(f"v{n}", [P, KT, P]))
        for sems, name in ((self.q_loaded, "q"), (self.k_loaded, "k"), (self.v_loaded, "v")):
            sems.append(a.sem(f"{name}{n}_loaded"))

    def load_kv(self, sp, b, g, which=range(5)):
        for n, y in enumerate(self.k_src):
            if n not in which:
                continue
            sp.dma_start(self.k[g][n * D:(n + 1) * D].bitcast(F32), of_batch(y, b, (g,), "d h l"))\
                .then_inc(self.k_loaded[g], 16)
        if 4 not in which:
            return
        sp.dma_start(self.v[g][:], of_batch(self.v_src, b, (slice(None), slice(None), slice(g * P, (g + 1) * P)), "p k c"))\
            .then_inc(self.v_loaded[g], 16)

    def load_first(self, sp, n):
        if 0 <= n < 4:
            self.load_q(sp, 0, 0, 0, (n,))
        elif 4 <= n < 9:
            self.load_kv(sp, 0, 0, (n - 4,))

    def load_q(self, sp, b, g, h, which=range(4)):
        for n, y in enumerate(self.q_src):
            if n not in which:
                continue
            src = of_batch(y, b, (g, slice(None), slice(None), slice(h * HALF, (h + 1) * HALF)), "d h l")
            sp.dma_start(self.q[h][n * D:(n + 1) * D].bitcast(F32), src).then_inc(self.q_loaded[h], 16)


def project(nc, io, tables, operands, q_hi, q_lo, k_hi, k_lo, v_out):
    x, wq, wk, wv, cos, sin, ident = (io[n] for n in ("x", "wq", "wk", "wv", "cos", "sin", "ident"))
    assert B == H
    PIECES = 2 * CC
    R = PIECES
    BY_POOL = 3
    with ExitStack() as ctx:
        a = Names(nc, ctx, "proj")
        wf = a.sbuf("w_float", [P, 3, CC, C])
        w_hi = a.sbuf("w_hi", [P, 3, CC, C], F32R)
        w_lo = a.sbuf("w_lo", [P, 3, CC, C], F32R)
        cos_t = a.sbuf("cos", [P, L])
        sin_t = a.sbuf("sin", [P, L])
        idt = a.sbuf("ident", [P, P])
        power = a.sbuf("power", [P, TT])
        eps = a.sbuf("eps", [P, TT])
        x_in = a.sbuf("x_in", [P, 2, TT, C])
        stats = a.sbuf("stats", [P, TT, 6])
        mean_var = a.sbuf("mean_var", [P, TT, 2])
        rstd_in = a.sbuf("rstd_in", [P, TT])
        rstd = a.sbuf("rstd", [P, TT])
        none = a.sbuf("none", [P, TT])
        product = a.sbuf("mean_by_rstd", [P, TT])
        shift = a.sbuf("shift", [P, TT])
        xn = a.sbuf("xn", [P, TT, C])
        x_hi = a.sbuf("x_hi", [P, 2, CC, HALF], F32R)
        x_lo = a.sbuf("x_lo", [P, 2, CC, HALF], F32R)
        by_cos = a.sbuf("by_cos", [P, R, HALF])
        swapped = a.sbuf("swapped", [P, 2, HALF])
        by_sin = a.sbuf("by_sin", [P, R, HALF])
        turned = a.sbuf("turned", [P, R, HALF])
        t_hi = a.sbuf("turned_hi", [P, R, HALF], F32R)
        t_lo = a.sbuf("turned_lo", [P, R, HALF], F32R)
        v_sb = a.sbuf("v", [P, 2, TT, C])
        pt = a.psum("x_turned", [P, CC, HALF])
        pa = a.psum("product", [P, R, HALF])
        pv = a.psum("v_acc", [P, CC, HALF])

        power_set = a.sem("power_set")
        passed = a.sem("waits_passed")
        w_hi_ready, w_ready = a.sem("w_hi_ready"), a.sem("w_ready")
        x_loaded = [a.sem(f"x_loaded{i}") for i in range(2)]
        stats_done, moments_done = a.sem("stats_done"), a.sem("moments_done")
        eps_added, rstd_ready = a.sem("eps_added"), a.sem("rstd_ready")
        xn_ready, xt_ready = a.sem("xn_ready"), a.sem("xt_ready")
        x_hi_ready, x_lo_ready = a.sem("x_hi_ready"), a.sem("x_lo_ready")
        products = a.sem("products_ready")
        cos_done, swap_done, sin_done = a.sem("cos_done"), a.sem("swap_done"), a.sem("sin_done")
        turned_by_pool = a.sem("turned_by_pool")
        hi_ready, lo_ready = a.sem("hi_ready"), a.sem("lo_ready")
        stored = [a.sem(f"parts_stored{i}") for i in range(R)]
        v_acc_ready, v_ready = a.sem("v_acc_ready"), a.sem("v_ready")
        v_stored = [a.sem(f"v_stored{i}") for i in range(2)]

        xv = x.rearrange("(n t p) c -> n p t c", p=P, t=TT)
        vv = v_out.rearrange("(n t p) c -> n p t c", p=P, t=TT)
        parts = [(hi.rearrange("b (c p) l -> b c p l", p=P), lo.rearrange("b (c p) l -> b c p l", p=P))
                 for hi, lo in ((q_hi, q_lo), (k_hi, k_lo))]
        def one(i, n):
            return i if isinstance(i, int) else bass.ds(i, n)

        def block_of(ap, j):
            return ap[j] if isinstance(j, int) else ap[bass.ds(j, 1)].rearrange("o p t c -> (o p) t c")

        ident_loaded, w_loaded, angles_loaded = (a.sem(n) for n in ("ident_loaded", "w_loaded", "angles_loaded"))
        product_ready, shift_ready = a.sem("product_ready"), a.sem("shift_ready")
        turned_by_dve = a.sem("turned_by_dve")

        def wait_turned(engine, j, m):
            if m < BY_POOL:
                engine.wait_ge(turned_by_pool, BY_POOL * j + m + 1)
            else:
                engine.wait_ge(turned_by_dve, (PIECES - BY_POOL) * j + m - BY_POOL + 1)

        block = ctx.enter_context(nc.Block())

        @block.sync
        def _(sp):
            for j in range(2):
                sp.dma_start(x_in[:, j], block_of(xv, j)).then_inc(x_loaded[j], 16)
                if j == 0:
                    sp.dma_start(idt[:], ident).then_inc(ident_loaded, 16)
            for n, w in enumerate((wq, wk, wv)):
                sp.dma_start(wf[:, n], w.rearrange("(k p) c -> p k c", p=P)).then_inc(w_loaded, 16)
            for dst, src in ((cos_t, cos), (sin_t, sin)):
                sp.dma_start(dst[:], src).then_inc(angles_loaded, 16)
            sp.wait_ge(xn_ready, 1)
            sp.dma_start(x_in[:, 0], block_of(xv, 2)).then_inc(x_loaded[0], 16)
            tables.load_small(sp, io)

            def body(b, first, last):
                for h in range(2):
                    j = 2 * b + h
                    if h == 1 and not last:
                        tables.load_decay(sp, io, b)
                    if h == 0 and first:
                        tables.load_decay(sp, io, B - 1)
                    for m in range(PIECES):
                        n = PIECES * j + m
                        if isinstance(b, int) and b == B - 2 and h == 0:
                            sp.wait_ge(stored[m], 32 * j)
                            if m < 2:
                                sp.wait_ge(v_stored[m], 16 * b)
                        if isinstance(b, int) and b >= B - 2:
                            operands.load_first(sp, PIECES * (j - 2 * (B - 2)) + m - (PIECES - 1))
                        for part, src, ready in ((0, t_hi, hi_ready), (1, t_lo, lo_ready)):
                            sp.wait_ge(ready, n + 1)
                            dst = parts[m // CC][part]
                            dst = dst[b, m % CC] if isinstance(b, int) else \
                                dst[bass.ds(b, 1), m % CC].rearrange("o p l -> (o p) l")
                            sp.dma_start(dst[:, h * HALF:(h + 1) * HALF], src[:, m].bitcast(F32))\
                                .then_inc(stored[m], 16)
                        if m == 1 and not last and not (isinstance(b, int) and b == B - 2 and h == 1):
                            sp.wait_ge(xn_ready, j + 2)
                            sp.dma_start(x_in[:, 1 - h], block_of(xv, j + 3)).then_inc(x_loaded[1 - h], 16)
                    sp.wait_ge(v_ready, 2 * (j + 1))
                    sp.dma_start(block_of(vv, j), v_sb[:, h]).then_inc(v_stored[h], 16)

            over_batches(sp, body)
            for i in range(R):
                sp.wait_ge(stored[i], 2 * B * 32)
            for i in range(2):
                sp.wait_ge(v_stored[i], B * 16)

        @block.gpsimd
        def _(pool):
            nc.gpsimd.memset(power[:], -0.5).then_inc(power_set, 1)
            nc.gpsimd.memset(eps[:], 1e-6).then_inc(power_set, 1)
            nc.gpsimd.memset(none[:], 0.0).then_inc(power_set, 1)
            pool.wait_ge(power_set, 3)

            def scale_of(j):
                pool.wait_ge(moments_done, j + 1)
                after(pool, xn_ready, j)
                nc.gpsimd.tensor_tensor(rstd_in[:], mean_var[:, :, 1], eps[:], ALU.add)\
                    .then_inc(eps_added, 1)
                pool.wait_ge(eps_added, j + 1)
                nc.gpsimd.tensor_tensor(rstd[:], rstd_in[:], power[:], ALU.pow).then_inc(rstd_ready, 1)
                pool.wait_ge(rstd_ready, j + 1)
                nc.gpsimd.tensor_tensor(product[:], mean_var[:, :, 0], rstd[:], ALU.mult).then_inc(product_ready, 1)
                pool.wait_ge(product_ready, j + 1)
                nc.gpsimd.tensor_tensor(shift[:], none[:], product[:], ALU.subtract).then_inc(shift_ready, 1)

            scale_of(0)
            scale_of(1)

            def low_part(n, i):
                pool.wait_ge(hi_ready, n + 1)
                if isinstance(n, int):
                    after(pool, stored[i], 32 * (n // PIECES))
                else:
                    pool.wait_ge(stored[i], 8 * (n - i))
                nc.gpsimd.tensor_tensor(t_lo[:, i], turned[:, i], t_hi[:, i].bitcast(F32), ALU.subtract)\
                    .then_inc(lo_ready, 1)

            def body(b, first, last):
                for h in range(2):
                    j = 2 * b + h
                    for m in range(PIECES):
                        n, i = PIECES * j + m, m
                        if m == 3 and not last:
                            scale_of(j + 2)
                        if m < BY_POOL:
                            pool.wait_ge(sin_done, n + 1)
                            if not (first and h == 0):
                                pool.wait_ge(lo_ready, n - R + 1)
                            nc.gpsimd.tensor_tensor(turned[:, i], by_cos[:, i], by_sin[:, i], ALU.add)\
                                .then_inc(turned_by_pool, 1)
                        if not (first and h == 0 and m == 0):
                            low_part(n - 1, (i - 1) % R)

            over_batches(pool, body)
            low_part(PIECES * 2 * B - 1, R - 1)

        @block.vector
        def _(dve):
            def moments(j, h):
                dve.wait_ge(x_loaded[h], 16 * (j // 2 + 1) if isinstance(j, int) else 8 * j + (16 if h == 0 else 8))
                after(dve, moments_done, j)
                for t in range(TT):
                    last = nc.vector.bn_stats(stats[:, t], x_in[:, h, t])
                last.then_inc(stats_done, 1)
                dve.wait_ge(stats_done, j + 1)
                after(dve, shift_ready, j)
                dve.sem_inc(passed, 1)
                for t in range(TT):
                    last = nc.vector.bn_aggr(mean_var[:, t], stats[:, t])
                last.then_inc(moments_done, 1)

            def low_part(j, h):
                for c in range(CC):
                    dve.wait_ge(x_hi_ready, CC * j + c + 1)
                    nc.vector.tensor_tensor(x_lo[:, h, c], pt[:, c], x_hi[:, h, c].bitcast(F32), ALU.subtract)\
                        .then_inc(x_lo_ready, 1)

            moments(0, 0)
            moments(1, 1)
            for n in range(3):
                if n == 0:
                    dve.wait_ge(w_loaded, 3 * 16)
                nc.vector.tensor_copy(w_hi[:, n], wf[:, n]).then_inc(w_hi_ready, 1)
                dve.wait_ge(w_hi_ready, n + 1)
                nc.vector.tensor_tensor(w_lo[:, n], wf[:, n], w_hi[:, n].bitcast(F32), ALU.subtract)\
                    .then_inc(w_ready, 1)
            low_part(0, 0)
            dve.wait_ge(angles_loaded, 2 * 16)

            def body(b, first, last):
                for h in range(2):
                    j = 2 * b + h
                    ahead = not (last and h == 1)
                    for m in range(PIECES):
                        n, i = PIECES * j + m, m
                        dve.wait_ge(products, n + 1)
                        if not (first and h == 0):
                            wait_turned(dve, j - 1, m)
                        at = slice(h * HALF, (h + 1) * HALF)
                        dve.sem_inc(passed, 1)
                        nc.vector.stream_shuffle(swapped[:, i % 2], pa[:, i], SWAP).then_inc(swap_done, 1)
                        nc.vector.tensor_tensor(by_cos[:, i], pa[:, i], cos_t[:, at], ALU.mult).then_inc(cos_done, 1)
                        dve.wait_ge(swap_done, n + 1)
                        nc.vector.tensor_tensor(by_sin[:, i], swapped[:, i % 2], sin_t[:, at], ALU.mult)\
                            .then_inc(sin_done, 1)
                        if m >= BY_POOL:
                            dve.wait_ge(cos_done, n + 1)
                            dve.wait_ge(sin_done, n + 1)
                            if not (first and h == 0):
                                dve.wait_ge(lo_ready, n - R + 1)
                            nc.vector.tensor_tensor(turned[:, i], by_cos[:, i], by_sin[:, i], ALU.add)\
                                .then_inc(turned_by_dve, 1)
                        if ahead:
                            if m == 2:
                                low_part(j + 1, 1 - h)
                        if m == 1 and not last:
                            moments(j + 2, h)

            over_batches(dve, body)

        @block.scalar
        def _(act):
            def norm(j, h):
                act.wait_ge(shift_ready, j + 1)
                after(act, xt_ready, 2 * j)
                for t in range(TT):
                    last = nc.scalar.activation(xn[:, t], x_in[:, h, t], ACT.Identity, bias=shift[:, t:t + 1],
                                                scale=rstd[:, t:t + 1])
                last.then_inc(xn_ready, 1)

            def high_part(j, h):
                for c in range(CC):
                    act.wait_ge(xt_ready, CC * j + c + 1)
                    nc.scalar.activation(x_hi[:, h, c], pt[:, c], ACT.Copy).then_inc(x_hi_ready, 1)

            norm(0, 0)
            high_part(0, 0)
            norm(1, 1)

            def body(b, first, last):
                for h in range(2):
                    j = 2 * b + h
                    for m in range(PIECES):
                        n, i = PIECES * j + m, m
                        if m == 2 and not (last and h == 1):
                            high_part(j + 1, 1 - h)
                        wait_turned(act, j, m)
                        after(act, stored[i], 32 * j)
                        nc.scalar.activation(t_hi[:, i], turned[:, i], ACT.Copy).then_inc(hi_ready, 1)
                        if m % 2:
                            c = m // 2
                            if c == 0 and not first:
                                act.wait_ge(v_stored[h], 16 * b)
                            act.wait_ge(v_acc_ready, CC * j + c + 1)
                            nc.scalar.activation(v_sb[:, h, 2 * c:2 * c + 2, :],
                                                 pv[:, c].rearrange("p (t c) -> p t c", t=2), ACT.Copy)\
                                .then_inc(v_ready, 1)
                        if m == 3 and not last:
                            norm(j + 2, h)

            over_batches(act, body)

        @block.tensor
        def _(pe):
            def turn(j, h):
                pe.wait_ge(xn_ready, j + 1)
                after(pe, x_lo_ready, CC * j)
                for c in range(CC):
                    for t in range(TT):
                        last = nc.tensor.transpose(pt[:, c, t * P:(t + 1) * P], xn[:, t, c * P:(c + 1) * P], idt[:])
                    last.then_inc(xt_ready, 1)

            def three(out, pairs):
                for n, (l, r) in enumerate(pairs):
                    last = nc.tensor.matmul(out, l, r, start=n == 0, stop=n == len(pairs) - 1)
                return last

            pe.wait_ge(ident_loaded, 16)
            turn(0, 0)
            pe.wait_ge(w_ready, 3)

            assert TT == PIECES

            def body(b, first, last):
                for h in range(2):
                    j = 2 * b + h
                    pe.wait_ge(x_lo_ready, CC * (j + 1))
                    for m in range(PIECES):
                        n, i = PIECES * j + m, m
                        kind, c = m // CC, m % CC
                        cols = slice(c * P, (c + 1) * P)
                        if not (first and h == 0):
                            pe.wait_ge(cos_done, n - R + 1)
                        three(pa[:, i], [(w[:, kind, k, cols], y[:, h, k]) for k in range(CC)
                                         for w, y in ((w_hi, x_hi), (w_hi, x_lo), (w_lo, x_hi))]).then_inc(products, 1)
                        if m == 2 and not (last and h == 1):
                            turn(j + 1, 1 - h)
                        t, c = m, m // 2
                        if t % 2 == 0 and not (first and h == 0):
                            pe.wait_ge(v_ready, CC * (j - 1) + c + 1)
                        rows = slice(t * P, (t + 1) * P)
                        done = three(pv[:, c, (t % 2) * C:(t % 2 + 1) * C],
                                     [(y[:, h, k, rows], w[:, 2, k])
                                      for k in range(CC) for w, y in ((w_hi, x_hi), (w_hi, x_lo), (w_lo, x_hi))])
                        if t % 2:
                            done.then_inc(v_acc_ready, 1)

            over_batches(pe, body)


def retain(nc, x, tables, operands, x1):
    HALVES, GROUPS, PAIRS = L // HALF, H // HG, HG // 2
    UNITS = GROUPS * HALVES
    STEPS = KT * PAIRS
    P_RING = 4
    ADDED = (0, 1, 8, 9)
    SLOT = (0, 1, 2, 3, 4, 5, 6, 7, 8, 9, 2, 3, 0, 1, 0, 1)
    ROW_SUMS = {4: 5, 5: 6, 6: 7, 7: 8, 0: 9, 1: 10, 12: 13, 13: 14, 14: 15, 15: 16, 8: 17, 9: 18}
    TAKEN = {i: n + 1 for n, i in enumerate(ROW_SUMS)}
    SUMS = len(ROW_SUMS)
    PROJECT_AT = ((7, 10), (7, 10), (7, 10), (14, 15))
    assert KT == 8 and PAIRS == 2 and UNITS == 4 and TT == 4
    with ExitStack() as ctx:
        a = Names(nc, ctx, "ret")
        decay_t, factor_t, idt, wo_t, gb = tables.decay, tables.factor, tables.ident, tables.wo, tables.gain_bias
        ones = a.sbuf("ones", [P, D])
        power = a.sbuf("power", [P, TT * HG])
        eps = a.sbuf("eps", [P, TT * HG])
        operands.allocate(a)
        k_st, q_st, v_t = operands.k, operands.q, operands.v
        k_loaded, q_loaded, v_loaded = operands.k_loaded, operands.q_loaded, operands.v_loaded
        decayed = a.sbuf("decayed", [P, P_RING, 2, HALF])
        magnitude = a.sbuf("magnitude", [P, max(SLOT) + 1, 2, HALF])
        o_sb = a.sbuf("o", [P, HALF])
        m_sb = a.sbuf("row_sums", [P, HALF])
        total = a.sbuf("total", [P, TT, HG])
        clipped = a.sbuf("clipped", [P, TT, HG])
        recip = a.sbuf("recip", [P, TT, HG])
        scale = a.sbuf("scale", [P, TT, HG])
        o_sum = a.sbuf("o_sum", [P, TT * HG])
        centred = a.sbuf("centred", [P, TT * HG, D])
        squared = a.sbuf("squared", [P, TT * HG, D])
        var_sum = a.sbuf("var_sum", [P, TT * HG])
        scale_sq = a.sbuf("scale_sq", [P, TT * HG])
        var_scaled = a.sbuf("var_scaled", [P, TT * HG])
        var_eps = a.sbuf("var_eps", [P, TT * HG])
        rstd = a.sbuf("rstd", [P, TT * HG])
        gain = a.sbuf("gain", [P, TT * HG])
        normed = a.sbuf("normed", [P, TT * HG, D])
        gelu_t = a.sbuf("gelu", [P, GROUPS, HALVES, HALF])
        x_res = a.sbuf("x_residual", [P, HALVES, TT, C])
        x_out = x_res
        ps = a.psum("scores", [P, 2, 2, HALF])
        po = a.psum("o_acc", [P, HALF])
        pm = a.psum("row_sum_acc", [P, HALF])
        px = a.psum("turn_a", [P, HALF])
        py = a.psum("turn_b", [P, HALF])

        set_up, passed = a.sem("set_up"), a.sem("waits_passed")
        x_loaded = [a.sem(f"x_loaded{i}") for i in range(HALVES)]
        x_stored = [a.sem(f"x_stored{i}") for i in range(HALVES)]
        scores, decayed_s, magnitude_s = a.sem("scores_ready"), a.sem("decayed_ready"), a.sem("magnitude_ready")
        added_s = a.sem("magnitudes_added")
        values, row_sums = a.sem("values_added"), a.sem("row_sums_added")
        o_out, m_out = a.sem("o_copied"), a.sem("row_sums_copied")
        o_turned, m_turned = a.sem("o_turned"), a.sem("row_sums_turned")
        total_s, clip_s, recip_s, scale_s = (a.sem(n) for n in ("total", "clipped", "recip", "scale"))
        o_sum_s, centred_s, squared_s, var_s = (a.sem(n) for n in ("o_sum", "centred", "squared", "var_sum"))
        pool_chain = a.sem("pool_chain")
        rstd_s, normed_s = a.sem("rstd_ready"), a.sem("normed_ready")
        back_s, gelu_s = a.sem("normed_turned"), a.sem("gelu_ready")
        out_s, x_out_s = a.sem("projected"), a.sem("x_out_ready")

        xv = x.rearrange("(b h t p) c -> b h p t c", p=P, t=TT, h=HALVES)
        x1v = x1.rearrange("(b h t p) c -> b h p t c", p=P, t=TT, h=HALVES)
        block = ctx.enter_context(nc.Block())

        @block.sync
        def _(sp):
            load_q = lambda *at: operands.load_q(sp, *at)
            load_kv = lambda *at: operands.load_kv(sp, *at)

            def load_x(b, h):
                sp.dma_start(x_res[:, h], of_batch(xv, b, (h,), "p t c")).then_inc(x_loaded[h], 16)

            load_q(0, 0, 1)
            load_kv(0, 1)
            load_x(0, 0)
            load_x(0, 1)

            def store(b, h):
                sp.wait_ge(x_out_s, 2 * (2 * b + h + 1))
                sp.dma_start(of_batch(x1v, b, (h,), "p t c"), x_out[:, h]).then_inc(x_stored[h], 16)

            def body(b, first, last):
                for k in range(UNITS):
                    g, h, u = k // HALVES, k % HALVES, UNITS * b + k
                    if k in (1, 2) and not first:
                        store(b - 1, k - 1)
                        sp.wait_ge(x_stored[k - 1], 16 * b)
                        sp.sem_inc(passed, 1)
                        load_x(b, k - 1)
                    sp.wait_ge(scores, STEPS * (u + 1))
                    if g == 0:
                        load_q(b, 1, h)
                    elif not last:
                        load_q(b + 1, 0, h)
                    if h == HALVES - 1 and not last:
                        sp.wait_ge(values, STEPS * (u + 1))
                        load_kv(b + 1, g)

            over_batches(sp, body)
            for h in range(HALVES):
                store(B - 1, h)
            for h in range(HALVES):
                sp.wait_ge(x_stored[h], 16 * B)

        @block.gpsimd
        def _(pool):
            nc.gpsimd.memset(power[:], -0.5).then_inc(set_up, 1)
            nc.gpsimd.memset(ones[:], 1.0).then_inc(set_up, 1)
            nc.gpsimd.memset(eps[:], 1e-5).then_inc(set_up, 1)
            pool.wait_ge(set_up, 3)

            def norm(u):
                wide = lambda y: y[:].unsqueeze(2).broadcast_to([P, TT * HG, D])
                pool.wait_ge(scale_s, u + 1)
                flat = scale[:].rearrange("p t h -> p (t h)")
                nc.gpsimd.tensor_tensor(scale_sq[:], flat, flat, ALU.mult).then_inc(pool_chain, 1)
                pool.wait_ge(var_s, u + 1)
                pool.wait_ge(pool_chain, 4 * u + 1)
                nc.gpsimd.tensor_tensor(var_scaled[:], var_sum[:], scale_sq[:], ALU.mult).then_inc(pool_chain, 1)
                pool.wait_ge(pool_chain, 4 * u + 2)
                nc.gpsimd.tensor_tensor(var_eps[:], var_scaled[:], eps[:], ALU.add).then_inc(pool_chain, 1)
                pool.wait_ge(pool_chain, 4 * u + 3)
                nc.gpsimd.tensor_tensor(rstd[:], var_eps[:], power[:], ALU.pow).then_inc(rstd_s, 1)
                pool.wait_ge(rstd_s, u + 1)
                nc.gpsimd.tensor_tensor(gain[:], rstd[:], flat, ALU.mult).then_inc(pool_chain, 1)
                pool.wait_ge(pool_chain, 4 * u + 4)
                after(pool, back_s, u)
                nc.gpsimd.tensor_tensor(normed[:], centred[:], wide(gain), ALU.mult).then_inc(normed_s, 1)

            def add(u, n):
                i = ADDED[n]
                pool.wait_ge(magnitude_s, STEPS * u + i + PAIRS + 1)
                one, two = magnitude[:, SLOT[i]], magnitude[:, SLOT[i + PAIRS]]
                nc.gpsimd.tensor_tensor(one, one, two, ALU.add).then_inc(added_s, 1)

            def body(b, first, last):
                for k in range(UNITS):
                    u = UNITS * b + k
                    add(u, 0)
                    add(u, 1)
                    if not (first and k == 0):
                        norm(u - 1)
                    for n in range(2, len(ADDED)):
                        add(u, n)

            over_batches(pool, body)
            norm(UNITS * B - 1)

        @block.vector
        def _(dve):
            tables.wait(dve)

            def decay_step(u, k, i, first):
                g, h, kt, pair = k // HALVES, k % HALVES, i // PAIRS, i % PAIRS
                n = STEPS * u + i
                dve.wait_ge(scores, n + 1)
                if not (first and k == 0 and i < P_RING):
                    dve.wait_ge(values, n - P_RING + 1)
                    dve.wait_ge(magnitude_s, n - P_RING + 1)
                at = (h * HALF // N2 - ROWS * kt + SPAN - N1) * N2
                nc.vector.tensor_tensor(decayed[:, i % P_RING], ps[:, i % 2],
                                        decay_t[:, HG * g + 2 * pair:HG * g + 2 * pair + 2, at:at + HALF],
                                        ALU.mult).then_inc(decayed_s, 1)

            def rest(u, k, i):
                g, h = k // HALVES, k % HALVES
                if i == 0:
                    dve.wait_ge(values, STEPS * (u + 1))
                    after(dve, o_turned, u)
                    nc.vector.tensor_copy(o_sb[:], po[:]).then_inc(o_out, 1)
                if i == 4:
                    dve.wait_ge(o_turned, u + 1)
                    nc.vector.tensor_reduce(o_sum[:], px[:].rearrange("p (n d) -> p n d", d=D), AX.X, ALU.add)\
                        .then_inc(o_sum_s, 1)
                if i == 7:
                    dve.wait_ge(m_turned, u + 1)
                    fac = factor_t[:, TT * h:TT * h + TT, HG * g:HG * g + HG]
                    nc.vector.tensor_tensor(total[:], py[:].rearrange("p (t h d) -> p t h d", t=TT, d=D)[:, :, :, 0],
                                            fac, ALU.mult).then_inc(total_s, 1)
                    dve.wait_ge(total_s, u + 1)
                    nc.vector.tensor_scalar(clipped[:], total[:], 1.0, 50000.0, ALU.max, ALU.min).then_inc(clip_s, 1)
                    dve.wait_ge(clip_s, u + 1)
                    nc.vector.reciprocal(recip[:], clipped[:]).then_inc(recip_s, 1)
                    dve.wait_ge(recip_s, u + 1)
                    after(dve, normed_s, u)
                    nc.vector.tensor_tensor(scale[:], recip[:], fac, ALU.mult).then_inc(scale_s, 1)
                if i == 5:
                    dve.wait_ge(o_sum_s, u + 1)
                    nc.vector.scalar_tensor_tensor(out=centred[:], in0=o_sum[:].unsqueeze(2).broadcast_to([P, TT * HG, D]),
                                                   scalar=-1.0 / D, in1=px[:].rearrange("p (n d) -> p n d", d=D),
                                                   op0=ALU.mult, op1=ALU.add).then_inc(centred_s, 1)
                if i == 8:
                    dve.wait_ge(squared_s, u + 1)
                    nc.vector.tensor_reduce(var_sum[:], squared[:], AX.X, ALU.add).then_inc(var_s, 1)

            def add_residual(b, h, n):
                m = UNITS * b + 2 * h + n
                dve.wait_ge(out_s, m + 1)
                if n == 0:
                    dve.wait_ge(x_loaded[h], 16 * (b + 1))
                nc.vector.tensor_tensor(x_out[:, h, 2 * n:2 * n + 2], py[:].rearrange("p (t c) -> p t c", t=2),
                                        x_res[:, h, 2 * n:2 * n + 2], ALU.add).then_inc(x_out_s, 1)

            def body(b, first, last):
                for k in range(UNITS):
                    u = UNITS * b + k
                    for i in range(STEPS):
                        decay_step(u, k, i, first)
                        if k > 0:
                            rest(u - 1, k - 1, i)
                        elif not first:
                            rest(u - 1, UNITS - 1, i)
                        if i == 0 and k == 0 and not first:
                            add_residual(b - 1, 0, 0)
                        if i == 13 and k < UNITS - 1 and not first:
                            add_residual(b - 1, (k + 1) // 2, (k + 1) % 2)

            over_batches(dve, body)
            for i in range(STEPS):
                rest(UNITS * B - 1, UNITS - 1, i)
                if i == 0:
                    add_residual(B - 1, 0, 0)
                if i == 13:
                    add_residual(B - 1, 0, 1)
            add_residual(B - 1, 1, 0)
            add_residual(B - 1, 1, 1)

        @block.scalar
        def _(act):
            tables.wait(act)

            def rest(u, k, i):
                g, h = k // HALVES, k % HALVES
                if i == 3:
                    act.wait_ge(row_sums, SUMS * (u + 1))
                    after(act, m_turned, u)
                    nc.scalar.activation(m_sb[:], pm[:], ACT.Copy).then_inc(m_out, 1)
                if i == 6:
                    act.wait_ge(centred_s, u + 1)
                    after(act, var_s, u)
                    nc.scalar.activation(squared[:], centred[:], ACT.Square, scale=D ** -0.5).then_inc(squared_s, 1)
                if i == 13:
                    act.wait_ge(back_s, u + 1)
                    if k < HALVES:
                        after(act, out_s, u - 2 + k)
                    nc.scalar.activation(gelu_t[:, g, h], px[:], ACT.Gelu, bias=gb[:, 1:2], scale=gb[:, 0:1])\
                        .then_inc(gelu_s, 1)

            def slot_free(u, k, i, first):
                before = [j for j in range(i) if SLOT[j] == SLOT[i]]
                old = before[-1] if before else max(j for j in range(STEPS) if SLOT[j] == SLOT[i])
                v = u if before else u - 1
                if not before and first and k == 0:
                    return
                if old - PAIRS in ADDED:
                    act.wait_ge(added_s, len(ADDED) * v + ADDED.index(old - PAIRS) + 1)
                else:
                    act.wait_ge(row_sums, SUMS * v + TAKEN[old])

            def body(b, first, last):
                for k in range(UNITS):
                    u = UNITS * b + k
                    for i in range(STEPS):
                        n = STEPS * u + i
                        act.wait_ge(decayed_s, n + 1)
                        slot_free(u, k, i, first)
                        nc.scalar.activation(magnitude[:, SLOT[i]], decayed[:, i % P_RING], ACT.Abs)\
                            .then_inc(magnitude_s, 1)
                        if k > 0:
                            rest(u - 1, k - 1, i)
                        elif not first:
                            rest(u - 1, UNITS - 1, i)

            over_batches(act, body)
            for i in range(STEPS):
                rest(UNITS * B - 1, UNITS - 1, i)

        @block.tensor
        def _(pe):
            pe.wait_ge(set_up, 3)
            tables.wait(pe)

            def score(b, k, i, first):
                g, h, kt, pair = k // HALVES, k % HALVES, i // PAIRS, i % PAIRS
                u = UNITS * b + k
                if i == 0:
                    pe.wait_ge(q_loaded[h], 64 * (2 * b + g + 1))
                    if h == 0:
                        pe.wait_ge(k_loaded[g], 64 * (b + 1))
                if not (first and k == 0 and i < 2):
                    pe.wait_ge(decayed_s, STEPS * u + i - 1)
                for j in range(2):
                    head = 2 * pair + j
                    last = nc.tensor.matmul(ps[:, i % 2, j], k_st[g][:, head, kt * P:(kt + 1) * P],
                                            q_st[h][:, head], start=True, stop=True)
                last.then_inc(scores, 1)

            def value(u, k, i, first):
                g, kt, pair = k // HALVES, i // PAIRS, i % PAIRS
                pe.wait_ge(decayed_s, STEPS * u + i + 1)
                if i == 0:
                    after(pe, o_out, u)
                for j in range(2):
                    head = 2 * pair + j
                    last = nc.tensor.matmul(po[head * D:(head + 1) * D, :], v_t[g][:, kt, head * D:(head + 1) * D],
                                            decayed[:, i % P_RING, j], start=kt == 0, stop=kt == KT - 1)
                last.then_inc(values, 1)

            def row_sum(u, i):
                pair, order = i % PAIRS, list(ROW_SUMS)
                of_pair = [j for j in order if j % PAIRS == pair]
                if i in ADDED:
                    pe.wait_ge(added_s, len(ADDED) * u + ADDED.index(i) + 1)
                else:
                    pe.wait_ge(magnitude_s, STEPS * u + i + 1)
                if i == order[0]:
                    after(pe, m_out, u)
                for j in range(2):
                    head = 2 * pair + j
                    last = nc.tensor.matmul(pm[head * D:(head + 1) * D, :], ones[:], magnitude[:, SLOT[i], j],
                                            start=i == of_pair[0], stop=i == of_pair[-1])
                last.then_inc(row_sums, 1)

            def turn(out, src):
                for t in range(TT):
                    last = nc.tensor.transpose(out[:, t * P:(t + 1) * P], src(t), idt[:])
                return last

            def rest(b, k, i):
                u = UNITS * b + k
                g, h = k // HALVES, k % HALVES
                if i == 2:
                    pe.wait_ge(o_out, u + 1)
                    after(pe, gelu_s, u)
                    turn(px, lambda t: o_sb[:, t * P:(t + 1) * P]).then_inc(o_turned, 1)
                if i == 5:
                    pe.wait_ge(m_out, u + 1)
                    after(pe, scale_s, u)
                    after(pe, x_out_s, u - 2)
                    turn(py, lambda t: m_sb[:, t * P:(t + 1) * P]).then_inc(m_turned, 1)
                if i == 12:
                    pe.wait_ge(normed_s, u + 1)
                    turn(px, lambda t: normed[:, t * HG:(t + 1) * HG].rearrange("p h d -> p (h d)"))\
                        .then_inc(back_s, 1)

            def project_tile(u, p, half):
                h, t = p // 2, 2 * (p % 2) + half
                if half == 0:
                    pe.wait_ge(scale_s, u)
                    pe.wait_ge(gelu_s, u if p == 0 else u - 1)
                for c in range(CC):
                    last = nc.tensor.matmul(py[:, half * C:(half + 1) * C], gelu_t[:, c, h, t * P:(t + 1) * P],
                                            wo_t[:, c], start=c == 0, stop=c == CC - 1)
                if half == 1:
                    last.then_inc(out_s, 1)

            score(0, 0, 0, True)
            score(0, 0, 1, True)

            def body(b, first, last_batch):
                for k in range(UNITS):
                    u = UNITS * b + k
                    for i in range(STEPS):
                        if i + 2 < STEPS:
                            score(b, k, i + 2, first)
                        elif k + 1 < UNITS:
                            score(b, k + 1, i + 2 - STEPS, False)
                        elif not last_batch:
                            score(b + 1, 0, i + 2 - STEPS, False)
                        if i == 0 and k % HALVES == 0:
                            pe.wait_ge(v_loaded[k // HALVES], 16 * (b + 1))
                        value(u, k, i, first)
                        for of, at in ROW_SUMS.items():
                            if at == i:
                                row_sum(u, of)
                            if at == i + STEPS and not (first and k == 0):
                                row_sum(u - 1, of)
                        if k > 0:
                            rest(b, k - 1, i)
                        elif not first:
                            rest(b - 1, UNITS - 1, i)
                        if i in PROJECT_AT[k] and (k == UNITS - 1 or not first):
                            project_tile(u, (k + 1) % UNITS, PROJECT_AT[k].index(i))

            over_batches(pe, body)
            for of, at in ROW_SUMS.items():
                if at >= STEPS:
                    row_sum(UNITS * B - 1, of)
            for i in range(STEPS):
                rest(B - 1, UNITS - 1, i)
                if i in PROJECT_AT[0]:
                    project_tile(UNITS * B, 1, PROJECT_AT[0].index(i))
            pe.wait_ge(gelu_s, UNITS * B)
            for p in (2, 3):
                pe.wait_ge(x_out_s, UNITS * (B - 1) + p)
                for half in range(2):
                    project_tile(UNITS * B, p, half)


SLOTS = 2 * T
TILES = SLOTS // P + EXPERTS
TOKEN_TILES = T // P
HK = HID // P
PACK, LAG = 4, 2
PACKED = TILES // PACK + 1
ROW = C + EXPERTS


def route(nc, out, gate_w, gate_b, w1, w2, upper, ident, b1, idt, b1_t, b1_loaded, w1_hi, w1_lo, w2_hi, w2_lo,
          tokens, packed_experts, rows):
    JS = T // HALF
    PIECES = 2 * EXPERTS
    XR = 4
    R = 8
    BY_ACT = (2, 6)
    BY_POOL = (1, 3, 5, 7)
    BY_DVE = (0, 4)
    PAIRS = 2 * TOKEN_TILES
    assert PIECES == JS
    with ExitStack() as ctx:
        a = Names(nc, ctx, "route")
        I32 = mybir.dt.int32
        x_in = a.sbuf("x_in", [P, XR, TT, C])
        stats = a.sbuf("stats", [P, 2, TT, 6])
        mean_var = a.sbuf("mean_var", [P, 2, TT, 2])
        rstd_in = a.sbuf("rstd_in", [P, 2, TT])
        rstd = a.sbuf("rstd", [P, 2, TT])
        power = a.sbuf("power", [P, TT])
        eps = a.sbuf("eps", [P, TT])
        xn = b1_t[:, 0:EXPERTS // 2].rearrange("p e n -> p (e n)").rearrange("p (h t c) -> p h t c", h=2, t=TT)
        xt = b1_t[:, EXPERTS // 2:EXPERTS].rearrange("p e n -> p (e n)").rearrange("p (h k n) -> p h k n", h=2, k=CC)
        assert EXPERTS * HID // 2 == 2 * TT * C == 2 * CC * HALF
        lt = a.sbuf("logits_across", [P, 2, HALF])
        up = a.sbuf("upper", [P, P])
        ones = a.sbuf("ones", [P, P])
        gate = a.sbuf("gate", [P, CC, EXPERTS])
        bias = a.sbuf("gate_bias", [P, EXPERTS])
        number = a.sbuf("expert_number", [P, EXPERTS])
        tile_no = a.sbuf("tile_number", [P, TILES])
        place_no = a.sbuf("place_number", [P, P])
        token_1 = a.sbuf("token_plus_1", [P, TOKEN_TILES])
        spare_1 = a.sbuf("spare_plus_1", [P, 1])
        zero = a.sbuf("zero", [P, ROW])
        wide = [P, TOKEN_TILES, EXPERTS]
        logits = a.sbuf("logits", wide)
        top = a.sbuf("top", [P, TOKEN_TILES])
        shifted = a.sbuf("shifted", wide)
        expd = a.sbuf("exp", wide)
        denom = a.sbuf("denom", [P, TOKEN_TILES])
        recip = a.sbuf("recip", [P, TOKEN_TILES])
        probs = a.sbuf("probs", wide)
        equal = a.sbuf("equal", wide)
        ranked = a.sbuf("ranked", wide)
        least = a.sbuf("least", [P, TOKEN_TILES])
        largest = a.sbuf("largest", [P, 2, TOKEN_TILES])
        chosen = [a.sbuf(f"chosen{i}", wide) for i in range(2)]
        left = a.sbuf("left", wide)
        both = a.sbuf("both", wide)
        cw = a.sbuf("weights", wide)
        total = a.sbuf("total", wide)
        scans = [a.sbuf(f"scan{i}", wide) for i in range(2)]
        small = [a.sbuf(f"small{i}", [P, EXPERTS]) for i in range(6)]
        whole = a.sbuf("whole", [P, EXPERTS], I32)
        shift = a.sbuf("shift", [P, EXPERTS], I32)
        slot_f = equal
        picked = ranked
        slot_sum = a.sbuf("slot_sum", [P, 2, TOKEN_TILES])
        slot_i = a.sbuf("slot_int", [P, 2, TOKEN_TILES], I32)
        slot_t = a.sbuf("slot_tile_int", [P, 2, TOKEN_TILES], I32)
        slot_tile = a.sbuf("slot_tile", [P, 2, TOKEN_TILES])
        slot_place = a.sbuf("slot_place", [P, 2, TOKEN_TILES])
        past_sum = a.sbuf("past_sum", [P, TILES])
        digits = a.sbuf("digits", [P, PACKED + 1, PACK])
        packing = [a.sbuf(f"packing{i}", [P, PACKED]) for i in range(2)]
        free = x_in[:].rearrange("p r t c -> p (r t c)")
        FREE = R * (P + TILES) + TILES * EXPERTS
        in_place = free[:, 0:R * P].rearrange("p (r n) -> p r n", r=R)
        in_tile = free[:, R * P:R * (P + TILES)].rearrange("p (r n) -> p r n", r=R)
        distance = free[:, FREE:FREE + len(BY_ACT) * P].rearrange("p (n c) -> p n c", n=len(BY_ACT))
        past = free[:, R * (P + TILES):R * (P + TILES) + TILES * EXPERTS].rearrange("p (n e) -> p n e", e=EXPERTS)
        group_place = a.sbuf("group_place", [P, R // 2])
        table = a.sbuf("table", [P, TILES])
        empty = a.sbuf("empty", [P, TILES])
        pt = a.psum("x_turned", [P, 2, CC, HALF])
        pl = a.psum("logit_acc", [P, 2, HALF])
        pr = a.psum("rank", [P, HALF])
        pc = a.psum("counts", [P, HALF])
        p_table = pl[:, 0, 0:TILES]

        consts, set_up = a.sem("consts_loaded"), a.sem("set_up")
        x_loaded = [a.sem(f"x_loaded{i}") for i in range(XR)]
        w_loaded = [a.sem(f"w_loaded{i}") for i in range(2)]
        stats_done, moments_done, eps_added, rstd_ready = (
            a.sem(n) for n in ("stats_done", "moments_done", "eps_added", "rstd_ready"))
        xn_ready, xt_acc, xt_ready = a.sem("xn_ready"), a.sem("xt_turned"), a.sem("xt_ready")
        xn_stored = [a.sem(f"xn_stored{i}") for i in range(2)]
        spare_stored, cw_stored = a.sem("spare_stored"), a.sem("cw_stored")
        logit_acc, lt_ready, logit_turned, logit_ready = (
            a.sem(n) for n in ("logit_acc", "logits_copied", "logits_turned", "logit_ready"))
        w_hi_s, w_lo_s = a.sem("w_hi_ready"), a.sem("w_lo_ready")
        chain, exp_s, counted = a.sem("chain"), a.sem("exp_ready"), a.sem("counted")
        both_s, cw_s, slots_s = a.sem("both_ready"), a.sem("weights_ready"), a.sem("slots_ready")
        distance_s, act_place_s = a.sem("distance_ready"), a.sem("act_place_ready")
        in_tile_s, dve_place_s, pool_place_s = a.sem("in_tile_ready"), a.sem("dve_place_ready"), a.sem("pool_place_ready")
        added_s, table_s, passed = a.sem("pairs_added"), a.sem("table_chain"), a.sem("waits_passed")
        place_s = a.sem("group_place_ready")

        xv = out[0:T].rearrange("(n t p) c -> n p t c", p=P, t=TT)
        xnv = rows[0:T].rearrange("(n t p) c -> n p t c", p=P, t=TT)
        w1v = w1.rearrange("e (k p) n -> e p k n", p=P)
        w2v = w2.rearrange("e (k p) n -> e p k n", p=P)
        weights = [(w1v, w1_hi, w1_lo), (w2v, w2_hi, w2_lo)]
        SET_UP = 10
        block = ctx.enter_context(nc.Block())

        @block.sync
        def _(sp):
            def load_w(j):
                src, _, lo = weights[j % 2]
                sp.dma_start(lo[:, j // 2].bitcast(F32), src[j // 2]).then_inc(w_loaded[j % 2], 16)

            sp.dma_start(x_in[:, 0], xv[0]).then_inc(x_loaded[0], 16)
            sp.dma_start(idt[:], ident).then_inc(consts, 16)
            sp.dma_start(x_in[:, 1], xv[1]).then_inc(x_loaded[1], 16)
            sp.dma_start(up[:], upper).then_inc(consts, 16)
            sp.dma_start(gate[:], gate_w.rearrange("(k p) e -> p k e", p=P)).then_inc(consts, 16)
            sp.dma_start(bias[:], gate_b.partition_broadcast(P)).then_inc(consts, 16)
            for j in range(2, XR):
                sp.dma_start(x_in[:, j], xv[j]).then_inc(x_loaded[j], 16)
            load_w(0)
            load_w(1)
            for j in range(JS):
                h = j % 2
                sp.wait_ge(xn_ready, j + 1)
                sp.dma_start(xnv[j][:, :, 0:C], xn[:, h]).then_inc(xn_stored[h], 16)
                if j + XR < JS:
                    sp.dma_start(x_in[:, j % XR], xv[j + XR]).then_inc(x_loaded[j % XR], 16)
                if j + 2 < JS:
                    sp.wait_ge(w_hi_s, j + 1)
                    load_w(j + 2)
            sp.wait_ge(set_up, SET_UP)
            sp.dma_start(rows[T:T + P], zero[:]).then_inc(spare_stored, 16)
            sp.dma_start(out[T:T + P], zero[:, 0:C]).then_inc(spare_stored, 16)
            sp.wait_ge(cw_s, 1)
            sp.dma_start(rows[0:T, C:ROW].rearrange("(t p) e -> p t e", p=P), cw[:]).then_inc(cw_stored, 16)
            for h in range(2):
                sp.wait_ge(xn_stored[h], 16 * JS // 2)
            sp.wait_ge(xt_acc, JS)
            sp.wait_ge(logit_acc, JS)
            sp.dma_start(b1_t[:], b1.partition_broadcast(P)).then_inc(b1_loaded, 16)
            sp.wait_ge(spare_stored, 32)
            sp.wait_ge(cw_stored, 16)

        def groups(engine, body):
            body(0, True)
            with engine.Fori(1, PAIRS // R - 1) as q:
                body(q, False)
            body(PAIRS // R - 1, False)

        def column(ap, t):
            return ap[:, t:t + 1] if isinstance(t, int) else ap[:, bass.ds(t, 1)]

        @block.gpsimd
        def _(pool):
            count_up = dict(allow_small_or_imprecise_dtypes=True)
            nc.gpsimd.memset(power[:], -0.5).then_inc(set_up, 1)
            nc.gpsimd.memset(eps[:], 1e-5).then_inc(set_up, 1)
            nc.gpsimd.memset(ones[:], 1.0).then_inc(set_up, 1)
            nc.gpsimd.memset(zero[:], 0.0).then_inc(set_up, 1)
            nc.gpsimd.memset(digits[:], 0.0).then_inc(set_up, 1)
            nc.gpsimd.iota(number[:], [[1, EXPERTS]], base=-EXPERTS, channel_multiplier=0, **count_up).then_inc(set_up, 1)
            nc.gpsimd.iota(tile_no[:], [[1, TILES]], base=0, channel_multiplier=0, **count_up).then_inc(set_up, 1)
            nc.gpsimd.iota(place_no[:], [[1, P]], base=0, channel_multiplier=0, **count_up).then_inc(set_up, 1)
            nc.gpsimd.iota(token_1[:], [[P, TOKEN_TILES]], base=1, channel_multiplier=1, **count_up).then_inc(set_up, 1)
            nc.gpsimd.iota(spare_1[:], [[1, 1]], base=T + 1, channel_multiplier=1, **count_up).then_inc(set_up, 1)
            pool.wait_ge(set_up, SET_UP)

            def low_weights(j):
                _, hi, lo = weights[j % 2]
                pool.wait_ge(w_hi_s, j + 1)
                nc.gpsimd.tensor_tensor(lo[:, j // 2], lo[:, j // 2].bitcast(F32), hi[:, j // 2].bitcast(F32),
                                        ALU.subtract).then_inc(w_lo_s, 1)

            for j in range(JS):
                h = j % 2
                pool.wait_ge(moments_done, j + 1)
                after(pool, rstd_ready, j - 1)
                nc.gpsimd.tensor_tensor(rstd_in[:, h], mean_var[:, h, :, 1], eps[:], ALU.add).then_inc(eps_added, 1)
                pool.wait_ge(eps_added, j + 1)
                after(pool, xn_ready, j - 1)
                nc.gpsimd.tensor_tensor(rstd[:, h], rstd_in[:, h], power[:], ALU.pow).then_inc(rstd_ready, 1)
                if j > 0:
                    low_weights(j - 1)
            low_weights(JS - 1)
            pool.wait_ge(slots_s, 1)

            def body(q, first):
                if not first:
                    pool.wait_ge(pool_place_s, len(BY_POOL) * q)
                pool.sem_inc(passed, 1)
                at = slice((R // 2) * q, (R // 2) * (q + 1)) if isinstance(q, int) else bass.ds((R // 2) * q, R // 2)
                nc.gpsimd.tensor_copy(group_place[:], slot_place[:, 1, at]).then_inc(place_s, 1)
                pool.wait_ge(place_s, q + 1)
                for k in BY_POOL:
                    if not first:
                        pool.wait_ge(added_s, R * (q - 1) + k + 1)
                    pool.sem_inc(passed, 1)
                    nc.gpsimd.tensor_scalar(in_place[:, k], place_no[:], group_place[:, k // 2:k // 2 + 1],
                                            None, ALU.is_equal).then_inc(pool_place_s, 1)

            groups(pool, body)

        @block.scalar
        def _(act):
            def copy_logits(j):
                act.wait_ge(logit_acc, j + 1)
                after(act, logit_turned, j - 1)
                nc.scalar.activation(lt[0:EXPERTS, j % 2], pl[0:EXPERTS, j % 2], ACT.Copy).then_inc(lt_ready, 1)

            for j in range(JS):
                h = j % 2
                _, hi, lo = weights[h]
                act.wait_ge(xt_acc, j + 1)
                after(act, logit_acc, j - 1)
                nc.scalar.activation(xt[:, h], pt[:, h], ACT.Copy).then_inc(xt_ready, 1)
                act.wait_ge(w_loaded[h], 16 * (j // 2 + 1))
                nc.scalar.activation(hi[:, j // 2], lo[:, j // 2].bitcast(F32), ACT.Copy).then_inc(w_hi_s, 1)
                if j >= 1:
                    copy_logits(j - 1)
            copy_logits(JS - 1)
            act.wait_ge(chain, 2)
            nc.scalar.activation(expd[:], shifted[:], ACT.Exp).then_inc(exp_s, 1)
            act.wait_ge(slots_s, 1)

            def body(q, first):
                for n, k in enumerate(BY_ACT):
                    if not first:
                        act.wait_ge(act_place_s, len(BY_ACT) * (q - 1) + n + 1)
                    nc.scalar.activation(distance[:, n], place_no[:], ACT.Abs, scale=-1.0,
                                         bias=column(slot_place[:, k % 2], (R // 2) * q + k // 2)).then_inc(distance_s, 1)
                    act.wait_ge(distance_s, len(BY_ACT) * q + n + 1)
                    if not first:
                        act.wait_ge(added_s, R * (q - 1) + k + 1)
                    nc.scalar.activation(in_place[:, k], distance[:, n], ACT.Relu, scale=-1.0, bias=ones[:, 0:1])\
                        .then_inc(act_place_s, 1)

            groups(act, body)

        @block.tensor
        def _(pe):
            pe.wait_ge(consts, 64)

            def logit(j):
                h = j % 2
                pe.wait_ge(xt_ready, j + 1)
                after(pe, lt_ready, j - 1)
                for c in range(CC):
                    last = nc.tensor.matmul(pl[0:EXPERTS, h], gate[:, c], xt[:, h, c], start=c == 0, stop=c == CC - 1)
                last.then_inc(logit_acc, 1)

            def turn_back(j):
                h = j % 2
                pe.wait_ge(lt_ready, j + 1)
                after(pe, logit_ready, j - 1)
                for t in range(TT):
                    last = nc.tensor.transpose((pr, pc)[h][:, t * EXPERTS:(t + 1) * EXPERTS],
                                               lt[0:EXPERTS, h, t * P:(t + 1) * P], idt[0:EXPERTS, 0:EXPERTS])
                last.then_inc(logit_turned, 1)

            for j in range(JS):
                h = j % 2
                pe.wait_ge(xn_ready, j + 1)
                after(pe, xt_ready, j - 1)
                for c in range(CC):
                    for t in range(TT):
                        last = nc.tensor.transpose(pt[:, h, c, t * P:(t + 1) * P], xn[:, h, t, c * P:(c + 1) * P], idt[:])
                last.then_inc(xt_acc, 1)
                if j >= 1:
                    logit(j - 1)
                if j >= 2:
                    turn_back(j - 2)
            logit(JS - 1)
            turn_back(JS - 2)
            turn_back(JS - 1)
            pe.wait_ge(both_s, 1)
            pe.wait_ge(set_up, SET_UP)
            flat = both[:].rearrange("p t e -> p (t e)")
            nc.tensor.matmul(pr[:], up[:], flat, start=True, stop=True)
            nc.tensor.matmul(pc[:], ones[:], flat, start=True, stop=True).then_inc(counted, 1)

            def body(q, first):
                for k in range(R):
                    pe.wait_ge(in_tile_s, R * q + k + 1)
                    if k in BY_POOL:
                        pe.wait_ge(pool_place_s, len(BY_POOL) * q + BY_POOL.index(k) + 1)
                    elif k in BY_ACT:
                        pe.wait_ge(act_place_s, len(BY_ACT) * q + BY_ACT.index(k) + 1)
                    else:
                        pe.wait_ge(dve_place_s, len(BY_DVE) * q + BY_DVE.index(k) + 1)
                    nc.tensor.matmul(p_table, in_place[:, k], in_tile[:, k], start=first and k == 0,
                                     stop=isinstance(q, int) and q == PAIRS // R - 1 and k == R - 1)\
                        .then_inc(added_s, 1)

            groups(pe, body)

        @block.vector
        def _(dve):
            def stage1(j):
                h = j % 2
                dve.wait_ge(x_loaded[j % XR], 16 * (j // XR + 1))
                after(dve, moments_done, j - 1)
                for t in range(TT):
                    last = nc.vector.bn_stats(stats[:, h, t], x_in[:, j % XR, t])
                last.then_inc(stats_done, 1)
                dve.wait_ge(stats_done, j + 1)
                after(dve, xn_ready, j - 1)
                after(dve, eps_added, j - 1)
                for t in range(TT):
                    last = nc.vector.bn_aggr(mean_var[:, h, t], stats[:, h, t])
                last.then_inc(moments_done, 1)

            def stage2(j):
                h = j % 2
                dve.wait_ge(rstd_ready, j + 1)
                if j >= 2:
                    dve.wait_ge(xt_acc, j - 1)
                    dve.wait_ge(xn_stored[h], 16 * (j // 2))
                for t in range(TT):
                    last = nc.vector.tensor_scalar(xn[:, h, t], x_in[:, j % XR, t], mean_var[:, h, t, 0:1],
                                                   rstd[:, h, t:t + 1], ALU.subtract, ALU.mult)
                last.then_inc(xn_ready, 1)

            def stage3(j):
                h = j % 2
                dve.wait_ge(logit_turned, j + 1)
                nc.vector.tensor_tensor(logits[:, j * TT:(j + 1) * TT],
                                        (pr, pc)[h][:, 0:TT * EXPERTS].rearrange("p (t e) -> p t e", t=TT),
                                        bias[:].unsqueeze(1).broadcast_to([P, TT, EXPERTS]), ALU.add)\
                    .then_inc(logit_ready, 1)

            stage1(0)
            for j in range(JS):
                if j + 1 < JS:
                    stage1(j + 1)
                stage2(j)
                if j == 3:
                    dve.wait_ge(consts, 64)
                if j >= 3:
                    stage3(j - 3)
            stage3(JS - 3)
            stage3(JS - 2)
            stage3(JS - 1)
            dve.wait_ge(logit_ready, JS)
            dve.wait_ge(set_up, SET_UP)

            count = [0]

            def link(ins):
                count[0] += 1
                ins.then_inc(chain, 1)
                dve.wait_ge(chain, count[0])

            spread = lambda y: y[:].unsqueeze(2).broadcast_to(wide)
            over = lambda y: y[:].unsqueeze(1).broadcast_to(wide)
            V = nc.vector
            link(V.tensor_reduce(top[:], logits[:], AX.X, ALU.max))
            link(V.tensor_tensor(shifted[:], logits[:], spread(top), ALU.subtract))
            dve.wait_ge(exp_s, 1)
            link(V.tensor_reduce(denom[:], expd[:], AX.X, ALU.add))
            link(V.reciprocal(recip[:], denom[:]))
            link(V.tensor_tensor(probs[:], expd[:], spread(recip), ALU.mult))
            rest = probs
            for n in range(2):
                link(V.tensor_reduce(largest[:, n], rest[:], AX.X, ALU.max))
                link(V.tensor_tensor(equal[:], rest[:], largest[:, n].unsqueeze(2).broadcast_to(wide), ALU.is_equal))
                link(V.tensor_tensor(ranked[:], equal[:], over(number), ALU.mult))
                link(V.tensor_reduce(least[:], ranked[:], AX.X, ALU.min))
                link(V.tensor_tensor(chosen[n][:], over(number), spread(least), ALU.is_equal))
                if n == 0:
                    link(V.scalar_tensor_tensor(out=left[:], in0=chosen[0][:], scalar=-4.0, in1=probs[:],
                                                op0=ALU.mult, op1=ALU.add))
                    rest = left
            V.tensor_tensor(both[:], chosen[0][:], chosen[1][:], ALU.add).then_inc(both_s, 1)
            dve.wait_ge(both_s, 1)
            V.tensor_tensor(cw[:], probs[:], both[:], ALU.mult).then_inc(cw_s, 1)
            dve.wait_ge(counted, 1)
            flat = lambda y: y[:].rearrange("p t e -> p (t e)")
            link(V.tensor_copy(flat(total), pc[:]))
            link(V.tensor_copy(flat(scans[0]), pc[:]))
            at, step = 0, 1
            while step < TOKEN_TILES:
                src, dst = scans[at], scans[1 - at]
                V.tensor_copy(dst[:, 0:step], src[:, 0:step])
                link(V.tensor_tensor(dst[:, step:], src[:, step:], src[:, 0:TOKEN_TILES - step], ALU.add))
                at, step = 1 - at, 2 * step
            running = scans[at]
            counts = running[:, TOKEN_TILES - 1]
            link(V.tensor_scalar(whole[:], counts, float(P - 1), None, ALU.add))
            link(V.tensor_scalar(shift[:], whole[:], P.bit_length() - 1, None, ALU.logical_shift_right))
            link(V.tensor_copy(small[0][:], shift[:]))
            link(V.tensor_copy(small[1][:], small[0][:]))
            now, step = 1, 1
            while step < EXPERTS:
                src, dst = small[now], small[now + 1]
                V.tensor_copy(dst[:, 0:step], src[:, 0:step])
                link(V.tensor_tensor(dst[:, step:], src[:, step:], src[:, 0:EXPERTS - step], ALU.add))
                now, step = now + 1, 2 * step
            ends, starts = small[now], small[now + 1]
            link(V.tensor_tensor(starts[:], ends[:], small[0][:], ALU.subtract))
            link(V.scalar_tensor_tensor(out=slot_f[:], in0=over(starts), scalar=float(P), in1=running[:],
                                        op0=ALU.mult, op1=ALU.add))
            link(V.tensor_tensor(picked[:], slot_f[:], total[:], ALU.subtract))
            link(V.tensor_tensor(flat(slot_f), flat(picked), pr[:], ALU.add))
            for n in range(2):
                link(V.tensor_tensor(picked[:], slot_f[:], chosen[n][:], ALU.mult))
                link(V.tensor_reduce(slot_sum[:, n], picked[:], AX.X, ALU.add))
            link(V.tensor_copy(slot_i[:], slot_sum[:]))
            link(V.tensor_scalar(slot_t[:], slot_i[:], P.bit_length() - 1, None, ALU.logical_shift_right))
            link(V.tensor_copy(slot_tile[:], slot_t[:]))
            link(V.scalar_tensor_tensor(out=slot_place[:], in0=slot_tile[:], scalar=-float(P), in1=slot_sum[:],
                                        op0=ALU.mult, op1=ALU.add))
            link(V.tensor_tensor(past[:], tile_no[:].unsqueeze(2).broadcast_to([P, TILES, EXPERTS]),
                                 ends[:].unsqueeze(1).broadcast_to([P, TILES, EXPERTS]), ALU.is_ge))
            V.tensor_reduce(past_sum[:], past[:], AX.X, ALU.add).then_inc(slots_s, 1)
            dve.wait_ge(slots_s, 1)
            flat_digits = digits[:].rearrange("p g n -> p (g n)")[:, LAG:LAG + TILES]
            link(V.tensor_scalar(flat_digits, past_sum[:], float(EXPERTS - 1), None, ALU.min))
            value = digits[:, 1:1 + PACKED, (PACK + LAG - 1) % PACK]
            for n, d in enumerate(reversed(range(PACK + LAG - 1))):
                to = packing[n % 2][:]
                link(V.scalar_tensor_tensor(out=to, in0=value, scalar=float(EXPERTS),
                                            in1=digits[:, d // PACK:d // PACK + PACKED, d % PACK],
                                            op0=ALU.mult, op1=ALU.add))
                value = to
            link(V.tensor_copy(packed_experts[:], value))

            def body(q, first):
                for k in range(R):
                    t = (R // 2) * q + k // 2
                    if not first:
                        dve.wait_ge(added_s, R * (q - 1) + k + 1)
                    if k in BY_DVE:
                        nc.vector.tensor_scalar(in_place[:, k], place_no[:], column(slot_place[:, k % 2], t), None,
                                                ALU.is_equal).then_inc(dve_place_s, 1)
                    nc.vector.tensor_scalar(in_tile[:, k], tile_no[:], column(slot_tile[:, k % 2], t),
                                            column(token_1, t), ALU.is_equal, ALU.mult).then_inc(in_tile_s, 1)

            groups(dve, body)
            dve.wait_ge(added_s, PAIRS)
            nc.vector.tensor_copy(table[:], p_table).then_inc(table_s, 1)
            dve.wait_ge(table_s, 1)
            nc.vector.tensor_scalar(empty[:], table[:], 0.0, spare_1[:], ALU.is_equal, ALU.mult).then_inc(table_s, 1)
            dve.wait_ge(table_s, 2)
            nc.vector.scalar_tensor_tensor(out=past_sum[:], in0=table[:], scalar=-1.0, in1=empty[:],
                                           op0=ALU.add, op1=ALU.add).then_inc(table_s, 1)
            dve.wait_ge(table_s, 3)
            nc.vector.tensor_copy(tokens[:], past_sum[:])


def experts(nc, b2, idt, b1_t, b1_loaded, w1_hi, w1_lo, w2_hi, w2_lo, tokens, packed_experts, rows, out):
    DIGIT = EXPERTS.bit_length() - 1
    R, AHEAD = 8, 5
    ROUNDS = TILES // R
    assert TILES % R == 0
    with ExitStack() as ctx:
        a = Names(nc, ctx, "exp")
        U32 = mybir.dt.uint32
        b2_t = a.sbuf("b2", [P, EXPERTS, C])
        source = a.sbuf("source", [P, R, 1], U32)
        target = a.sbuf("target", [P, R, 1], U32)
        x_in = a.sbuf("x_in", [P, R, ROW])
        x_hi = a.sbuf("x_hi", [P, 2, CC, P], F32R)
        x_lo = a.sbuf("x_lo", [P, 2, CC, P], F32R)
        pre = a.sbuf("pre", [P, 2, HID])
        act_t = a.sbuf("gelu", [P, 2, HID])
        h_hi = a.sbuf("h_hi", [P, 2, HK, P], F32R)
        h_lo = a.sbuf("h_lo", [P, 2, HK, P], F32R)
        y_sum = a.sbuf("y_sum", [P, 2, C])
        y = a.sbuf("y", [P, 2, C])
        px = a.psum("x_turned", [P, HALF])[:, 0:CC * P].rearrange("p (k n) -> p k n", k=CC)
        ph = a.psum("hidden", [P, 2, HID])
        pt = a.psum("hidden_turned", [P, 2, HK, P])
        py = a.psum("y_acc", [P, 2, HALF])
        b2_loaded = a.sem("b2_loaded")
        x_loaded = [a.sem(f"x_gathered{i}") for i in range(R)]
        source_s, target_s, passed = a.sem("source_ready"), a.sem("target_ready"), a.sem("waits_passed")
        x_turned, x_hi_s, x_lo_s = a.sem("x_turned"), a.sem("x_hi_ready"), a.sem("x_lo_ready")
        hidden, pre_s, gelu_s = a.sem("hidden"), a.sem("pre_ready"), a.sem("gelu_ready")
        h_turned, h_hi_s, h_lo_s = a.sem("h_turned"), a.sem("h_hi_ready"), a.sem("h_lo_ready")
        y_acc, y_sum_s, y_s, added = a.sem("y_acc"), a.sem("y_sum_ready"), a.sem("y_ready"), a.sem("y_added")

        def over_tiles(engine, body):
            for i in range(R):
                body(i, i, 0)
            with engine.Fori(1, ROUNDS - 1) as r:
                for k in range(R):
                    body(R * r + k, k, r)
            for i in range(TILES - R, TILES + 2):
                body(i, i % R, i // R)

        def exists(i):
            return not isinstance(i, int) or 0 <= i < TILES

        def column(ap, i):
            return ap[:, i:i + 1] if isinstance(i, int) else ap[:, bass.ds(i, 1)]

        def load_experts(engine, i, k, r, known):
            if k % PACK == 0:
                group = (R // PACK) * r + k // PACK
                known["packed"] = engine.value_load(column(packed_experts[0:1], group), min_val=0,
                                                    max_val=EXPERTS ** (PACK + LAG) - 1)

        def expert(known, k, back=0):
            digit = k % PACK + LAG - back
            return (known["packed"] >> (digit * DIGIT)) & (EXPERTS - 1)

        block = ctx.enter_context(nc.Block())

        @block.sync
        def _(sp):
            sp.dma_start(b2_t[:], b2.partition_broadcast(P)).then_inc(b2_loaded, 16)

        @block.gpsimd
        def _(pool):
            def gather(i, k):
                after(pool, y_s, i - R + 1)
                pool.sem_inc(passed, 1)
                nc.gpsimd.tensor_copy(source[:, k], column(tokens, i)).then_inc(source_s, 1)
                pool.wait_ge(source_s, i + 1)
                pool.sem_inc(passed, 1)
                nc.gpsimd.indirect_dma_start(x_in[:, k], None, rows, bass.IndirectOffsetOnAxis(source[:, k], 0))\
                    .then_inc(x_loaded[k], 16)

            for i in range(AHEAD):
                gather(i, i)

            def body(i, k, r):
                if exists(i + AHEAD):
                    gather(i + AHEAD, (k + AHEAD) % R)
                if exists(i - 2):
                    o = (k - 2) % R
                    after(pool, added, 16 * (i - 2))
                    pool.sem_inc(passed, 1)
                    nc.gpsimd.tensor_copy(target[:, o], column(tokens, i - 2)).then_inc(target_s, 1)
                    pool.wait_ge(target_s, i - 1)
                    pool.wait_ge(y_s, i - 1)
                    pool.sem_inc(passed, 1)
                    nc.gpsimd.indirect_dma_start(out, bass.IndirectOffsetOnAxis(target[:, o], 0), y[:, k % 2], None,
                                                 compute_op=ALU.add).then_inc(added, 16)

            over_tiles(pool, body)
            pool.wait_ge(added, 16 * TILES)

        @block.tensor
        def _(pe):
            def turn_x(i, k, r):
                pe.wait_ge(x_loaded[k], 16 * r + 16)
                after(pe, x_lo_s, i)
                for c in range(CC):
                    last = nc.tensor.transpose(px[:, c], x_in[:, k, c * P:(c + 1) * P], idt[:])
                last.then_inc(x_turned, 1)

            def three(out, xs, ws, e, chunks, s):
                n, steps = 0, 3 * chunks
                for k in range(chunks):
                    for w, xx in ((ws[0], xs[0]), (ws[0], xs[1]), (ws[1], xs[0])):
                        last = nc.tensor.matmul(out, xx[:, s, k], w[:, bass.ds(e, 1), k].rearrange("p o n -> p (o n)"),
                                                start=n == 0, stop=n == steps - 1)
                        n += 1
                return last

            turn_x(0, 0, 0)

            known = {}

            def body(i, k, r):
                s = k % 2
                load_experts(pe, i, k, r, known)
                if exists(i):
                    e = expert(known, k)
                    pe.wait_ge(x_lo_s, i + 1)
                    after(pe, pre_s, i - 1)
                    three(ph[:, s], (x_hi, x_lo), (w1_hi, w1_lo), e, CC, s).then_inc(hidden, 1)
                if exists(i + 1):
                    turn_x(i + 1, (k + 1) % R, r + (k + 1) // R)
                if exists(i - 1):
                    pe.wait_ge(gelu_s, i)
                    after(pe, h_lo_s, i - 2)
                    for c in range(HK):
                        last = nc.tensor.transpose(pt[:, 1 - s, c], act_t[:, 1 - s, c * P:(c + 1) * P], idt[:])
                    last.then_inc(h_turned, 1)
                if exists(i - 2):
                    e = expert(known, k, LAG)
                    pe.wait_ge(h_lo_s, i - 1)
                    after(pe, y_sum_s, i - 3)
                    three(py[:, s, 0:C], (h_hi, h_lo), (w2_hi, w2_lo), e, HK, s).then_inc(y_acc, 1)

            over_tiles(pe, body)

        @block.scalar
        def _(act):
            def x_high(i, s):
                act.wait_ge(x_turned, i + 1)
                after(act, hidden, i - 1)
                nc.scalar.activation(x_hi[:, s], px, ACT.Copy).then_inc(x_hi_s, 1)

            x_high(0, 0)
            known = {}

            def body(i, k, r):
                s = k % 2
                load_experts(act, i, k, r, known)
                if exists(i + 1):
                    x_high(i + 1, 1 - s)
                if exists(i - 1):
                    act.wait_ge(h_turned, i)
                    after(act, y_acc, i - 3)
                    nc.scalar.activation(h_hi[:, 1 - s], pt[:, 1 - s], ACT.Copy).then_inc(h_hi_s, 1)
                if exists(i):
                    act.wait_ge(pre_s, i + 1)
                    after(act, h_turned, i - 1)
                    nc.scalar.activation(act_t[:, s], pre[:, s], ACT.Gelu).then_inc(gelu_s, 1)
                if exists(i - 2):
                    e = expert(known, k, LAG)
                    act.wait_ge(y_sum_s, i - 1)
                    after(act, added, 16 * (i - 3))
                    nc.scalar.activation(y[:, s], y_sum[:, s], ACT.Copy,
                                         scale=x_in[:, (k - 2) % R, bass.ds(e + C, 1)]).then_inc(y_s, 1)

            over_tiles(act, body)

        @block.vector
        def _(dve):
            def x_low(i, s):
                dve.wait_ge(x_hi_s, i + 1)
                nc.vector.tensor_tensor(x_lo[:, s], px, x_hi[:, s].bitcast(F32), ALU.subtract).then_inc(x_lo_s, 1)

            x_low(0, 0)
            dve.wait_ge(b1_loaded, 16)

            known = {}

            def body(i, k, r):
                s = k % 2
                load_experts(dve, i, k, r, known)
                if exists(i + 1):
                    x_low(i + 1, 1 - s)
                if exists(i - 1):
                    dve.wait_ge(h_hi_s, i)
                    nc.vector.tensor_tensor(h_lo[:, 1 - s], pt[:, 1 - s], h_hi[:, 1 - s].bitcast(F32), ALU.subtract)\
                        .then_inc(h_lo_s, 1)
                if exists(i):
                    e = expert(known, k)
                    dve.wait_ge(hidden, i + 1)
                    after(dve, gelu_s, i - 1)
                    nc.vector.tensor_tensor(pre[:, s], ph[:, s], b1_t[:, bass.ds(e, 1)].rearrange("p o n -> p (o n)"),
                                            ALU.add).then_inc(pre_s, 1)
                if exists(i - 2):
                    e = expert(known, k, LAG)
                    dve.wait_ge(y_acc, i - 1)
                    if isinstance(i, int) and i == 2:
                        dve.wait_ge(b2_loaded, 16)
                    after(dve, y_s, i - 3)
                    nc.vector.tensor_tensor(y_sum[:, s], py[:, s, 0:C],
                                            b2_t[:, bass.ds(e, 1)].rearrange("p o n -> p (o n)"), ALU.add)\
                        .then_inc(y_sum_s, 1)

            over_tiles(dve, body)


def shape_constants():
    f = np.float32
    half = f(1.0) / (f(10000.0) ** np.linspace(0.0, 1.0, D // 2, dtype=f))
    angle = np.repeat(half, 2)
    index = (np.arange(N1, dtype=f)[:, None] + np.arange(N2, dtype=f)[None, :]).reshape(L)
    phase = (index[:, None] * angle[None, :]).astype(f)
    sign = np.where(np.arange(D) % 2 == 0, f(-1), f(1))
    cos = np.tile(np.cos(phase).astype(f).T, (HG, 1))
    sin = np.tile((np.sin(phase).astype(f) * sign).T, (HG, 1))
    decay = np.log(f(1.0) - f(2.0) ** (f(-2.0) - f(5.0) * np.arange(H, dtype=f) / f(H))).astype(f)
    row, col = np.divmod(np.arange(P), N2)
    rows_apart = np.abs(np.arange(SPAN)[None, :] - (SPAN - N1) - row[:, None])
    cols_apart = np.abs(np.arange(N2)[None, :] - col[:, None])
    apart = (rows_apart[:, None, :, None] + cols_apart[:, None, None, :]).astype(f)
    table = np.exp(apart * decay[None, :, None, None]).astype(f)
    line = np.exp(np.abs(np.arange(N1)[:, None] - np.arange(N1)[None, :]).astype(f) * decay[:, None, None])
    sums = line.astype(np.float64).sum(-1)
    total = (sums[:, :, None] * sums[:, None, :]).reshape(H, L)
    factor = (D ** -0.5 / np.sqrt(total)).astype(f)
    factor = factor.reshape(H, KT, P).transpose(2, 1, 0)
    return {"cos": cos, "sin": sin, "decay": table.reshape(P, H, SPAN * N2),
            "factor": np.ascontiguousarray(factor), "ident": np.eye(P, dtype=f),
            "upper": np.triu(np.ones((P, P), dtype=f), 1)}


def block_program(nc, io):
    scratch = lambda name, shape: nc.dram_tensor(name, shape, F32).ap()
    parts = [scratch(n, (B, C, L)) for n in ("q_hi", "q_lo", "k_hi", "k_lo")]
    v = scratch("v_rows", (T, C))
    rows = scratch("token_rows", (T + P, ROW))
    out = io["out"]
    with ExitStack() as ctx:
        tables = RetainConstants(nc, ctx)
        operands = Operands(nc, ctx, *parts, v)
        project(nc, io, tables, operands, *parts, v)
        retain(nc, io["x"], tables, operands, out[0:T])
    with ExitStack() as ctx:
        a = Names(nc, ctx, "moe")
        w1p = [a.sbuf(f"w1_{n}", [P, EXPERTS, CC, HID], F32R) for n in ("hi", "lo")]
        w2p = [a.sbuf(f"w2_{n}", [P, EXPERTS, HK, C], F32R) for n in ("hi", "lo")]
        idt = a.sbuf("ident", [P, P])
        b1_t = a.sbuf("b1", [P, EXPERTS, HID])
        b1_loaded = a.sem("b1_loaded")
        tokens = a.sbuf("tokens", [P, TILES], mybir.dt.uint32)
        packed_experts = a.sbuf("packed_experts", [P, PACKED], mybir.dt.int32)
        route(nc, out, io["gate_w"], io["gate_b"], io["w1"], io["w2"], io["upper"], io["ident"], io["b1"],
              idt, b1_t, b1_loaded, *w1p, *w2p, tokens, packed_experts, rows)
        experts(nc, io["b2"], idt, b1_t, b1_loaded, *w1p, *w2p, tokens, packed_experts, rows, out)


def kernel(x, L0_conv_Wq, L0_conv_Wk, L0_conv_Wv, L0_conv_Wo, L0_conv_ln_g, L0_conv_ln_b,
           L0_ffn_gate_w, L0_ffn_gate_b, L0_ffn_W1, L0_ffn_b1, L0_ffn_W2, L0_ffn_b2):
    import concourse.bacc as bacc
    from concourse.bass_utils import run_bass_kernel_spmd

    turned = lambda w: np.ascontiguousarray(np.asarray(w).T)
    arrays = {
        "x": np.ascontiguousarray(np.asarray(x)).reshape(T, C),
        "wq": turned(L0_conv_Wq), "wk": turned(L0_conv_Wk), "wv": turned(L0_conv_Wv), "wo": turned(L0_conv_Wo),
        "ln_g": np.asarray(L0_conv_ln_g), "ln_b": np.asarray(L0_conv_ln_b),
        "gate_w": np.asarray(L0_ffn_gate_w), "gate_b": np.asarray(L0_ffn_gate_b),
        "w1": np.asarray(L0_ffn_W1), "b1": np.asarray(L0_ffn_b1),
        "w2": np.asarray(L0_ffn_W2), "b2": np.asarray(L0_ffn_b2),
        **shape_constants(),
    }
    nc = bacc.Bacc("TRN2", target_bir_lowering=False, num_devices=1)
    io = {n: nc.dram_tensor(n, a.shape, mybir.dt.from_np(a.dtype), kind="ExternalInput").ap()
          for n, a in arrays.items()}
    io["out"] = nc.dram_tensor("out", (T + P, C), F32, kind="ExternalOutput").ap()
    block_program(nc, io)
    result = run_bass_kernel_spmd(nc, [arrays], core_ids=[0])
    return result.results[0]["out"][:T].reshape(B, N1, N2, C)
```
